# Optimizing a Trainium2 kernel written in Bass

```python
import numpy as np
import jax
import jax.numpy as jnp

def _softmax(x, axis=-1):
    return jax.nn.softmax(x, axis=axis)

def _gelu(x):
    return jax.nn.gelu(x, approximate=True)

def _silu(x):
    return jax.nn.silu(x)

def _sigmoid(x):
    return jax.nn.sigmoid(x)

def _layernorm(x, axis=-1, eps=1e-05):
    m = jnp.mean(x, axis=axis, keepdims=True)
    v = jnp.var(x, axis=axis, keepdims=True)
    return (x - m) / jnp.sqrt(v + eps)

def _scatter_add(tgt, idx, src, axis=0):
    return tgt.at[idx].add(src)

def _segment_sum(src, seg, n):
    return jax.ops.segment_sum(src, seg, n)
kernel_name = 'mk_prb_d2_jaxref_r4_f0621d'

def setup_inputs(seed: int=0):
    np.random.seed(seed)
    _w = jnp.asarray

    def _L0_attn_setup():
        import jax, jax.numpy as jnp
        import numpy as np
        import math
        N_EMBD = 256
        N_HEAD = 16
        HEAD_DIM = N_EMBD // N_HEAD // 2
        DEPTH = 1
        LAMBDA_INIT = 0.8 - 0.6 * math.exp(-0.3 * (DEPTH - 1))
        EPS = 1e-05
        key = jax.random.key(seed)
        ks = jax.random.split(key, 8)
        B, T, C = (4, 256, N_EMBD)
        x = jax.random.normal(ks[0], (B, T, C), dtype=jnp.float32)
        w_attn = jax.random.normal(ks[1], (C, 3 * C), dtype=jnp.float32) * (1.0 / math.sqrt(C))
        w_proj = jax.random.normal(ks[2], (C, C), dtype=jnp.float32) * (1.0 / math.sqrt(C))
        lambda_q1 = jax.random.normal(ks[3], (HEAD_DIM,), dtype=jnp.float32) * 0.1
        lambda_q2 = jax.random.normal(ks[4], (HEAD_DIM,), dtype=jnp.float32) * 0.1
        lambda_k1 = jax.random.normal(ks[5], (HEAD_DIM,), dtype=jnp.float32) * 0.1
        lambda_k2 = jax.random.normal(ks[6], (HEAD_DIM,), dtype=jnp.float32) * 0.1
        gamma = jnp.ones((2 * HEAD_DIM,), dtype=jnp.float32)
        return {'x': x, 'w_attn': w_attn, 'w_proj': w_proj, 'lambda_q1': lambda_q1, 'lambda_q2': lambda_q2, 'lambda_k1': lambda_k1, 'lambda_k2': lambda_k2, 'gamma': gamma}
    _L0_attn_in = _L0_attn_setup()

    def _L0_ffn_setup():
        import jax, jax.numpy as jnp
        import numpy as np
        E = 8
        H = 256
        M = 512
        K = 2
        SE = 1
        BSZ, SEQ = (2, 256)
        W_SCALE = 0.02
        key = jax.random.key(seed)
        ks = jax.random.split(key, 9)
        return {'x': jax.random.normal(ks[0], (BSZ, SEQ, H), jnp.float32), 'gate_w': jax.random.normal(ks[1], (E, H), jnp.float32) * W_SCALE, 'beta': jnp.zeros((E,), jnp.float32), 'gate_proj_w': jax.random.normal(ks[2], (E, H, M), jnp.float32) * W_SCALE, 'up_proj_w': jax.random.normal(ks[3], (E, H, M), jnp.float32) * W_SCALE, 'down_proj_w': jax.random.normal(ks[4], (E, M, H), jnp.float32) * W_SCALE, 'shared_gate_w': jax.random.normal(ks[5], (SE, H, M), jnp.float32) * W_SCALE, 'shared_up_w': jax.random.normal(ks[6], (SE, H, M), jnp.float32) * W_SCALE, 'shared_down_w': jax.random.normal(ks[7], (SE, M, H), jnp.float32) * W_SCALE}
    _L0_ffn_in = _L0_ffn_setup()

    def _L1_attn_setup():
        import jax, jax.numpy as jnp
        import numpy as np
        D_MODEL = 256
        EXPAND = 2
        D_INNER = D_MODEL * EXPAND
        D_STATE = 16
        D_CONV = 4
        DT_RANK = (D_MODEL + 15) // 16

        def _affine_combine(left, right):
            a_l, u_l = left
            a_r, u_r = right
            return (a_l * a_r, a_r * u_l + u_r)

        def _silu(v):
            return v * jax.nn.sigmoid(v)

        def _forward(x, in_proj_w, conv_w, conv_b, x_proj_w, dt_proj_w, dt_proj_b, A_log, D_skip, out_proj_w):
            B, T, _ = x.shape
            xz = jnp.einsum('btd,ed->bte', x, in_proj_w)
            xc, z = jnp.split(xz, 2, axis=-1)
            xt = jnp.transpose(xc, (0, 2, 1))
            conv = jax.lax.conv_general_dilated(xt, conv_w, window_strides=(1,), padding=[(D_CONV - 1, 0)], dimension_numbers=('NCH', 'OIH', 'NCH'), feature_group_count=D_INNER)
            conv = conv + conv_b[None, :, None]
            xs = jnp.transpose(_silu(conv), (0, 2, 1))
            A = -jnp.exp(A_log)
            x_dbl = jnp.einsum('bti,oi->bto', xs, x_proj_w)
            dt_r = x_dbl[..., :DT_RANK]
            Bv = x_dbl[..., DT_RANK:DT_RANK + D_STATE]
            C = x_dbl[..., DT_RANK + D_STATE:]
            dt = jax.nn.softplus(jnp.einsum('btr,ir->bti', dt_r, dt_proj_w) + dt_proj_b)
            a = jnp.exp(dt[..., None] * A[None, None])
            u = dt[..., None] * Bv[:, :, None, :] * xs[..., None]
            _, h = jax.lax.associative_scan(_affine_combine, (a, u), axis=1)
            y = jnp.einsum('btis,bts->bti', h, C) + xs * D_skip[None, None, :]
            y = y * _silu(z)
            return jnp.einsum('bti,di->btd', y, out_proj_w)
        key = jax.random.key(seed)
        ks = jax.random.split(key, 8)
        B, T = (2, 256)
        x = jax.random.normal(ks[0], (B, T, D_MODEL), dtype=jnp.float32)
        in_proj_w = jax.random.normal(ks[1], (2 * D_INNER, D_MODEL), dtype=jnp.float32) / np.sqrt(D_MODEL)
        conv_w = jax.random.normal(ks[2], (D_INNER, 1, D_CONV), dtype=jnp.float32) / np.sqrt(D_CONV)
        conv_b = jax.random.normal(ks[3], (D_INNER,), dtype=jnp.float32) * 0.01
        x_proj_w = jax.random.normal(ks[4], (DT_RANK + 2 * D_STATE, D_INNER), dtype=jnp.float32) / np.sqrt(D_INNER)
        dt_proj_w = jax.random.normal(ks[5], (D_INNER, DT_RANK), dtype=jnp.float32) / np.sqrt(DT_RANK)
        dt_proj_b = jax.random.normal(ks[6], (D_INNER,), dtype=jnp.float32) * 0.01
        A_log = jnp.log(jnp.tile(jnp.arange(1, D_STATE + 1, dtype=jnp.float32), (D_INNER, 1)))
        D_skip = jnp.ones((D_INNER,), dtype=jnp.float32)
        out_proj_w = jax.random.normal(ks[7], (D_MODEL, D_INNER), dtype=jnp.float32) / np.sqrt(D_INNER)
        return {'x': x, 'in_proj_w': in_proj_w, 'conv_w': conv_w, 'conv_b': conv_b, 'x_proj_w': x_proj_w, 'dt_proj_w': dt_proj_w, 'dt_proj_b': dt_proj_b, 'A_log': A_log, 'D_skip': D_skip, 'out_proj_w': out_proj_w}
    _L1_attn_in = _L1_attn_setup()

    def _L1_ffn_setup():
        import jax, jax.numpy as jnp
        import numpy as np
        import math
        D_IN = 256
        FEATURES = (1024, 1024, 256)
        BATCH, SEQ = (8, 512)

        def _conn_dense(kernel_bool, x):
            w = jnp.where(kernel_bool, jnp.float32(1.0), jnp.float32(-1.0))
            return x @ w
        key = jax.random.key(seed)
        kx, kk0, kk1, kk2 = jax.random.split(key, 4)
        x = jax.random.normal(kx, (BATCH, SEQ, D_IN), dtype=jnp.float32)
        k0 = jax.random.randint(kk0, (2 * D_IN, FEATURES[0]), 0, 2).astype(jnp.bool_)
        k1 = jax.random.randint(kk1, (FEATURES[0], FEATURES[1]), 0, 2).astype(jnp.bool_)
        k2 = jax.random.randint(kk2, (FEATURES[1], FEATURES[2]), 0, 2).astype(jnp.bool_)
        s0 = jnp.asarray(1.0 / math.sqrt(2 * D_IN), dtype=jnp.float32)
        s1 = jnp.asarray(1.0 / math.sqrt(FEATURES[0]), dtype=jnp.float32)
        s2 = jnp.asarray(1.0 / math.sqrt(FEATURES[1]), dtype=jnp.float32)
        return {'x': x, 'k0': k0, 'k1': k1, 'k2': k2, 's0': s0, 's1': s1, 's2': s2}
    _L1_ffn_in = _L1_ffn_setup()
    _d = {'L0_attn_x': _L0_attn_in['x'], 'L0_attn_w_attn': _L0_attn_in['w_attn'], 'L0_attn_w_proj': _L0_attn_in['w_proj'], 'L0_attn_lambda_q1': _L0_attn_in['lambda_q1'], 'L0_attn_lambda_q2': _L0_attn_in['lambda_q2'], 'L0_attn_lambda_k1': _L0_attn_in['lambda_k1'], 'L0_attn_lambda_k2': _L0_attn_in['lambda_k2'], 'L0_attn_gamma': _L0_attn_in['gamma'], 'L0_ffn_gate_w': _L0_ffn_in['gate_w'], 'L0_ffn_beta': _L0_ffn_in['beta'], 'L0_ffn_gate_proj_w': _L0_ffn_in['gate_proj_w'], 'L0_ffn_up_proj_w': _L0_ffn_in['up_proj_w'], 'L0_ffn_down_proj_w': _L0_ffn_in['down_proj_w'], 'L0_ffn_shared_gate_w': _L0_ffn_in['shared_gate_w'], 'L0_ffn_shared_up_w': _L0_ffn_in['shared_up_w'], 'L0_ffn_shared_down_w': _L0_ffn_in['shared_down_w'], 'L1_attn_in_proj_w': _L1_attn_in['in_proj_w'], 'L1_attn_conv_w': _L1_attn_in['conv_w'], 'L1_attn_conv_b': _L1_attn_in['conv_b'], 'L1_attn_x_proj_w': _L1_attn_in['x_proj_w'], 'L1_attn_dt_proj_w': _L1_attn_in['dt_proj_w'], 'L1_attn_dt_proj_b': _L1_attn_in['dt_proj_b'], 'L1_attn_A_log': _L1_attn_in['A_log'], 'L1_attn_D_skip': _L1_attn_in['D_skip'], 'L1_attn_out_proj_w': _L1_attn_in['out_proj_w'], 'L1_ffn_k0': _L1_ffn_in['k0'], 'L1_ffn_k1': _L1_ffn_in['k1'], 'L1_ffn_k2': _L1_ffn_in['k2'], 'L1_ffn_s0': _L1_ffn_in['s0'], 'L1_ffn_s1': _L1_ffn_in['s1'], 'L1_ffn_s2': _L1_ffn_in['s2']}
    _x0 = _d['L0_attn_x']
    _d['L0_attn_x'] = jax.random.normal(jax.random.fold_in(jax.random.key(seed), 1), (2, 2048, 256), dtype=_x0.dtype)
    del _x0
    return _d

def reference(L0_attn_x, L0_attn_w_attn, L0_attn_w_proj, L0_attn_lambda_q1, L0_attn_lambda_q2, L0_attn_lambda_k1, L0_attn_lambda_k2, L0_attn_gamma, L0_ffn_gate_w, L0_ffn_beta, L0_ffn_gate_proj_w, L0_ffn_up_proj_w, L0_ffn_down_proj_w, L0_ffn_shared_gate_w, L0_ffn_shared_up_w, L0_ffn_shared_down_w, L1_attn_in_proj_w, L1_attn_conv_w, L1_attn_conv_b, L1_attn_x_proj_w, L1_attn_dt_proj_w, L1_attn_dt_proj_b, L1_attn_A_log, L1_attn_D_skip, L1_attn_out_proj_w, L1_ffn_k0, L1_ffn_k1, L1_ffn_k2, L1_ffn_s0, L1_ffn_s1, L1_ffn_s2):

    def _L0_attn_ref(x, w_attn, w_proj, lambda_q1, lambda_q2, lambda_k1, lambda_k2, gamma):
        import jax, jax.numpy as jnp
        import numpy as np
        import math
        N_EMBD = 256
        N_HEAD = 16
        HEAD_DIM = N_EMBD // N_HEAD // 2
        DEPTH = 1
        LAMBDA_INIT = 0.8 - 0.6 * math.exp(-0.3 * (DEPTH - 1))
        EPS = 1e-05
        B, T, C = x.shape
        H, hd = (N_HEAD, HEAD_DIM)
        qkv = x @ w_attn
        q, k, v = jnp.split(qkv, 3, axis=-1)
        q = q.reshape(B, T, 2 * H, hd).transpose(0, 2, 1, 3)
        k = k.reshape(B, T, 2 * H, hd).transpose(0, 2, 1, 3)
        v = v.reshape(B, T, H, 2 * hd).transpose(0, 2, 1, 3)
        q = q * hd ** (-0.5)
        att = jnp.einsum('bhtd,bhsd->bhts', q, k) * (1.0 / math.sqrt(hd))
        causal = jnp.tril(jnp.ones((T, T), dtype=bool))
        att = jnp.where(causal, att, -jnp.inf)
        att = jax.nn.softmax(att, axis=-1)
        lam1 = jnp.exp(jnp.sum(lambda_q1 * lambda_k1))
        lam2 = jnp.exp(jnp.sum(lambda_q2 * lambda_k2))
        lambda_full = lam1 - lam2 + LAMBDA_INIT
        att = att.reshape(B, H, 2, T, T)
        att = att[:, :, 0] - lambda_full * att[:, :, 1]
        out = jnp.einsum('bhts,bhsd->bhtd', att, v)
        rms = jax.lax.rsqrt(jnp.mean(out * out, axis=-1, keepdims=True) + EPS)
        out = out * rms * gamma
        out = (1.0 - LAMBDA_INIT) * out
        out = out.transpose(0, 2, 1, 3).reshape(B, T, C)
        return out @ w_proj

    def _L0_ffn_ref(x, gate_w, beta, gate_proj_w, up_proj_w, down_proj_w, shared_gate_w, shared_up_w, shared_down_w):
        import jax, jax.numpy as jnp
        import numpy as np
        E = 8
        H = 256
        M = 512
        K = 2
        SE = 1
        BSZ, SEQ = (2, 256)
        W_SCALE = 0.02
        B0, S0, H0 = x.shape
        xt = x.reshape(-1, H0)
        B = xt.shape[0]
        logits = xt @ gate_w.T
        _, idx = jax.lax.top_k(logits + beta, K)
        probs = jax.nn.sigmoid(jnp.take_along_axis(logits, idx, axis=-1))
        c = jnp.zeros((B, E), xt.dtype).at[jnp.arange(B)[:, None], idx].add(probs)
        g = jnp.einsum('bh,ehm->bem', xt, gate_proj_w)
        u = jnp.einsum('bh,ehm->bem', xt, up_proj_w)
        h = jax.nn.silu(g) * u
        eo = jnp.einsum('bem,emh->beh', h, down_proj_w)
        combined = jnp.einsum('beh,be->bh', eo, c)
        sg = jnp.einsum('bh,ehm->bem', xt, shared_gate_w)
        su = jnp.einsum('bh,ehm->bem', xt, shared_up_w)
        sh = jax.nn.silu(sg) * su
        shared_out = jnp.einsum('bem,emh->beh', sh, shared_down_w).sum(axis=1)
        return (combined + shared_out).reshape(B0, S0, H0)

    def _L1_attn_ref(x, in_proj_w, conv_w, conv_b, x_proj_w, dt_proj_w, dt_proj_b, A_log, D_skip, out_proj_w):
        import jax, jax.numpy as jnp
        import numpy as np
        D_MODEL = 256
        EXPAND = 2
        D_INNER = D_MODEL * EXPAND
        D_STATE = 16
        D_CONV = 4
        DT_RANK = (D_MODEL + 15) // 16

        def _affine_combine(left, right):
            a_l, u_l = left
            a_r, u_r = right
            return (a_l * a_r, a_r * u_l + u_r)

        def _silu(v):
            return v * jax.nn.sigmoid(v)

        def _forward(x, in_proj_w, conv_w, conv_b, x_proj_w, dt_proj_w, dt_proj_b, A_log, D_skip, out_proj_w):
            B, T, _ = x.shape
            xz = jnp.einsum('btd,ed->bte', x, in_proj_w)
            xc, z = jnp.split(xz, 2, axis=-1)
            xt = jnp.transpose(xc, (0, 2, 1))
            conv = jax.lax.conv_general_dilated(xt, conv_w, window_strides=(1,), padding=[(D_CONV - 1, 0)], dimension_numbers=('NCH', 'OIH', 'NCH'), feature_group_count=D_INNER)
            conv = conv + conv_b[None, :, None]
            xs = jnp.transpose(_silu(conv), (0, 2, 1))
            A = -jnp.exp(A_log)
            x_dbl = jnp.einsum('bti,oi->bto', xs, x_proj_w)
            dt_r = x_dbl[..., :DT_RANK]
            Bv = x_dbl[..., DT_RANK:DT_RANK + D_STATE]
            C = x_dbl[..., DT_RANK + D_STATE:]
            dt = jax.nn.softplus(jnp.einsum('btr,ir->bti', dt_r, dt_proj_w) + dt_proj_b)
            a = jnp.exp(dt[..., None] * A[None, None])
            u = dt[..., None] * Bv[:, :, None, :] * xs[..., None]
            _, h = jax.lax.associative_scan(_affine_combine, (a, u), axis=1)
            y = jnp.einsum('btis,bts->bti', h, C) + xs * D_skip[None, None, :]
            y = y * _silu(z)
            return jnp.einsum('bti,di->btd', y, out_proj_w)
        return _forward(x, in_proj_w, conv_w, conv_b, x_proj_w, dt_proj_w, dt_proj_b, A_log, D_skip, out_proj_w)

    def _L1_ffn_ref(x, k0, k1, k2, s0, s1, s2):
        import jax, jax.numpy as jnp
        import numpy as np
        import math
        D_IN = 256
        FEATURES = (1024, 1024, 256)
        BATCH, SEQ = (8, 512)

        def _conn_dense(kernel_bool, x):
            w = jnp.where(kernel_bool, jnp.float32(1.0), jnp.float32(-1.0))
            return x @ w
        h = jnp.concatenate([x, -x], axis=-1)
        h = s0 * _conn_dense(k0, h)
        h = jax.nn.relu(h) * 2
        h = s1 * _conn_dense(k1, h)
        h = jax.nn.relu(h) * 2
        h = s2 * _conn_dense(k2, h)
        return h
    x = L0_attn_x
    xn = _layernorm(x, axis=-1)
    x = x + _L0_attn_ref(xn, L0_attn_w_attn, L0_attn_w_proj, L0_attn_lambda_q1, L0_attn_lambda_q2, L0_attn_lambda_k1, L0_attn_lambda_k2, L0_attn_gamma) + _L0_ffn_ref(xn, L0_ffn_gate_w, L0_ffn_beta, L0_ffn_gate_proj_w, L0_ffn_up_proj_w, L0_ffn_down_proj_w, L0_ffn_shared_gate_w, L0_ffn_shared_up_w, L0_ffn_shared_down_w)
    xn = _layernorm(x, axis=-1)
    x = x + _L1_attn_ref(xn, L1_attn_in_proj_w, L1_attn_conv_w, L1_attn_conv_b, L1_attn_x_proj_w, L1_attn_dt_proj_w, L1_attn_dt_proj_b, L1_attn_A_log, L1_attn_D_skip, L1_attn_out_proj_w) + _L1_ffn_ref(xn, L1_ffn_k0, L1_ffn_k1, L1_ffn_k2, L1_ffn_s0, L1_ffn_s1, L1_ffn_s2)
    return x

_drawn_inputs = setup_inputs


def setup_inputs(seed=0):
    import zlib

    import numpy as np

    out = dict(_drawn_inputs(seed))
    spreads = {'L0_attn_gamma': (1.0, 0.2), 'L0_ffn_beta': (0.0, 0.73), 'L1_attn_D_skip': (1.0, 0.582)}
    factors = {'L0_attn_lambda_q1': 3.578,
     'L0_attn_lambda_q2': 5.715,
     'L0_attn_lambda_k1': 6.746,
     'L0_ffn_gate_w': 3.882,
     'L0_ffn_gate_proj_w': 3.332,
     'L0_ffn_up_proj_w': 3.305,
     'L0_ffn_down_proj_w': 3.289,
     'L0_ffn_shared_gate_w': 2.758,
     'L0_ffn_shared_up_w': 2.711,
     'L0_ffn_shared_down_w': 2.739,
     'L1_attn_conv_b': 8.0,
     'L1_attn_dt_proj_b': 45.843}
    for name, (base, spread) in spreads.items():
        noise = np.random.default_rng([zlib.crc32(name.encode()), seed]).standard_normal(out[name].shape)
        drawn = base * np.exp(spread * noise) if base else spread * noise
        out[name] = jnp.asarray(drawn.astype(out[name].dtype))
    for name, factor in factors.items():
        out[name] = (out[name] * factor).astype(out[name].dtype)
    return out
```

```python
import numpy as np
import concourse.bass as bass
from concourse import mybir
from contextlib import ExitStack

F32 = mybir.dt.float32
BF16 = mybir.dt.bfloat16
F16 = mybir.dt.float16
U32 = mybir.dt.uint32
U8 = mybir.dt.uint8
ACT = mybir.ActivationFunctionType
ALU = mybir.AluOpType
AX = mybir.AxisListType

P = 128
BATCH, T, D = 2, 2048, 256
N = BATCH * T
BLK = 512
NBLK = N // BLK
BPB = T // BLK
TPB = BLK // P
NT = N // P
KD = D // P
HEADS, HD = 16, 8
VD = 2 * HD
E, M = 8, 512
NE = E + 1
EPS = 1e-5
CREDIT = 1
LAMBDA_INIT = 0.2
NEG = -1e30

ST_T = T // P
NH = BATCH * HEADS
KQ = 9 * HD
VW = 32
OC = VD + 1

DI = 512
CT = DI // P
NS = 16
NTAP = 4
RANK = 16
F1 = 1024


def credited(ctx, nc, sems, name):
    sems.append(ctx.enter_context(nc.semaphore(name)))
    return sems[-1]


class Chain:

    def __init__(self, eng, sem, per_turn=0):
        self.eng, self.sem, self.per, self.n, self.base = eng, sem, per_turn, 0, 0

    def turn(self, base):
        self.base, self.n = base, 0

    def mark(self, ins):
        ins.then_inc(self.sem, 1)
        self.n += 1

    def wait(self):
        self.eng.wait_ge(self.sem, self.base + self.n + CREDIT)

    def after(self, ins):
        self.mark(ins)
        self.wait()

    def end(self):
        assert self.n == self.per, (self.n, self.per)


def phase_norm_qkv(nc, io, keep, dram):
    with ExitStack() as ctx:
        sb = lambda name, shape, dt=F32: ctx.enter_context(nc.sbuf_tensor(name, shape, dt))
        ps = lambda name, shape, dt=F32: ctx.enter_context(nc.psum_tensor(name, shape, dt))
        sems = []
        sem = lambda name: credited(ctx, nc, sems, name)

        wqkv = sb("wqkv", [P, KD, 3 * D])
        gate_rows = sb("gate_rows", [E, D])
        gateT = sb("gateT", [P, KD, E])
        beta = sb("beta", [P, E])
        iota_u = sb("iota_u", [P, E], mybir.dt.int32)
        iota_e = sb("iota_e", [P, E])
        x = sb("x", [P, TPB, D])
        stats = sb("stats", [P, TPB, 6])
        mv = sb("mv", [P, TPB, 2])
        std = sb("std", [P, TPB])
        rstd = sb("rstd", [P, TPB])
        xn = sb("xn", [P, TPB, D])
        xnT = sb("xnT", [P, KD, BLK])
        qf = sb("qf", [P, 2, BLK])
        rest = sb("rest", [P, 2, BLK])
        parts = sb("parts", [P, 2, 3, BLK], BF16)
        sel = sb("sel", [P, TPB, E])
        top = sb("top", [P, TPB, E])
        topi = sb("topi", [P, TPB, E], U32)
        topf = sb("topf", [P, TPB, E])
        hot = sb("hot", [P, 2, TPB, E])
        sig = sb("sig", [P, TPB, E])
        carrier = sb("carrier", [P, 4])

        psT = ps("psT", [P, KD, BLK])
        psQ = ps("psQ", [P, 2, BLK])
        psV = ps("psV", [P, TPB, D])
        psL = ps("psL", [P, TPB, E])

        w_in = sem("a_w_in")
        x_in = sem("a_x_in")
        x_free = sem("a_x_free")
        stats_ready = sem("a_stats_ready")
        std_ready = sem("a_std_ready")
        xT_done = sem("a_xT_done")
        xnT_ready = sem("a_xnT_ready")
        xnT_out = sem("a_xnT_out")
        gate_t = sem("a_gate_t")
        gateT_ready = sem("a_gateT_ready")
        qk_done = sem("a_qk_done")
        qf_ready = [sem(f"a_qf_ready{s}") for s in range(2)]
        parts_ready = [sem(f"a_parts_ready{s}") for s in range(2)]
        parts_out = [sem(f"a_parts_out{s}") for s in range(2)]
        v_done = sem("a_v_done")
        v_free = sem("a_v_free")
        l_done = sem("a_l_done")
        sig_ready = sem("a_sig_ready")
        c_ready = sem("a_c_ready")
        dchain = sem("a_dchain")
        pchain = sem("a_pchain")
        iota_ready = sem("a_iota_ready")

        block = ctx.enter_context(nc.Block())
        CH = 41

        @block.sync
        def _(sp):
            for s in sems:
                sp.sem_inc(s, CREDIT)
            sp.dma_start(wqkv[:], io["w_attn"].rearrange("(k p) n -> p k n", p=P)).then_inc(w_in, 16)
            sp.dma_start(gate_rows[:], io["gate_w"]).then_inc(w_in, 16)
            sp.dma_start(beta[:], io["beta"].partition_broadcast(P)).then_inc(w_in, 16)
            x_blk = io["x"].rearrange("(n j p) d -> n p j d", p=P, j=TPB)
            sp.dma_start(x[:], x_blk[0]).then_inc(x_in, 16)

            def stores(b, q):
                blk = b * BPB + q
                for f in range(4):
                    sp.wait_ge(parts_ready[f % 2], 2 * blk + f // 2 + 1 + CREDIT)
                    sp.dma_start(dram["qk"][f // 2, :, b, (f % 2) * P:(f % 2 + 1) * P, bass.ds(q * BLK, BLK)]
                                 .rearrange("s p t -> p s t"), parts[:, f % 2]).then_inc(parts_out[f % 2], 16)

            with sp.Fori(0, BATCH) as b:
                with sp.Fori(0, BPB) as q:
                    blk = b * BPB + q
                    sp.wait_ge(x_free, blk + 1 + CREDIT)
                    sp.dma_start(x[:], io["x"][bass.ds((blk + 1) % NBLK * BLK, BLK), :]
                                 .rearrange("(j p) d -> p j d", p=P)).then_inc(x_in, 16)
                    stores(b, q)
            sp.wait_ge(x_in, 16 * NBLK + 16 + CREDIT)
            for s in range(2):
                sp.wait_ge(parts_out[s], 32 * NBLK + CREDIT)

        @block.gpsimd
        def _(pool):
            c = Chain(pool, pchain)
            c.after(pool.memset(keep["ident"][:], 0.0))
            c.after(pool.affine_select(out=keep["ident"][:], in_=keep["ident"][:], compare_op=ALU.not_equal, fill=1.0,
                                       base=0, pattern=[[-1, P]], channel_multiplier=1))
            c.after(pool.iota(iota_u[:], pattern=[[1, E]], base=0, channel_multiplier=0))
            pool.tensor_copy(iota_e[:], iota_u[:]).then_inc(iota_ready, 1)

        @block.vector
        def _(dve):
            c = Chain(dve, dchain, CH)
            dve.wait_ge(iota_ready, 1 + CREDIT)
            dve.wait_ge(w_in, 48 + CREDIT)
            with dve.Fori(0, NBLK) as blk:
                c.turn(blk * CH)
                dve.wait_ge(x_in, 16 * blk + 16 + CREDIT)
                for j in range(TPB):
                    c.mark(dve.bn_stats(stats[:, j, :], x[:, j, :]))
                c.wait()
                c.mark(dve.memset(carrier[:, 0:1], 0.0))
                for j in range(TPB):
                    c.mark(dve.bn_aggr(mv[:, j, :], stats[:, j, :]))
                c.wait()
                dve.tensor_scalar(rstd[:], mv[:, :, 1], EPS, None, ALU.add).then_inc(stats_ready, 1)
                dve.wait_ge(std_ready, blk + 1 + CREDIT)
                c.after(dve.reciprocal(rstd[:], std[:]))
                dve.wait_ge(xT_done, blk + CREDIT)
                for j in range(TPB):
                    ins = dve.tensor_scalar(xn[:, j, :], x[:, j, :], mv[:, j, 0:1], rstd[:, j:j + 1],
                                            ALU.subtract, ALU.mult)
                ins.then_inc(x_free, 1)
                for f in range(4):
                    s = f % 2
                    dve.wait_ge(qf_ready[s], 2 * blk + f // 2 + 1 + CREDIT)
                    dve.wait_ge(parts_out[s], 16 * (2 * blk + f // 2) + CREDIT)
                    c.after(dve.tensor_copy(parts[:, s, 0], qf[:, s]))
                    c.after(dve.tensor_tensor(rest[:, 0], qf[:, s], parts[:, s, 0], ALU.subtract))
                    c.after(dve.tensor_copy(parts[:, s, 1], rest[:, 0]))
                    c.after(dve.tensor_tensor(rest[:, 1], rest[:, 0], parts[:, s, 1], ALU.subtract))
                    dve.tensor_copy(parts[:, s, 2], rest[:, 1]).then_inc(parts_ready[s], 1)
                dve.wait_ge(l_done, blk + 1 + CREDIT)
                dve.wait_ge(sig_ready, blk + 1 + CREDIT)
                dve.wait_ge(x_free, blk + 1 + CREDIT)
                c.after(dve.tensor_tensor(sel[:], psL[:], beta[:].unsqueeze(1).to_broadcast([P, TPB, E]), ALU.add))
                c.mark(dve.memset(carrier[:, 1:2], 0.0))
                for j in range(TPB):
                    c.mark(dve.max(top[:, j, :], sel[:, j, :]))
                c.wait()
                c.mark(dve.memset(carrier[:, 2:3], 0.0))
                for j in range(TPB):
                    c.mark(dve.max_index(topi[:, j, :], top[:, j, :], sel[:, j, :]))
                c.wait()
                c.after(dve.tensor_copy(topf[:], topi[:]))
                for k in range(2):
                    c.mark(dve.tensor_tensor(hot[:, k], iota_e[:].unsqueeze(1).to_broadcast([P, TPB, E]),
                                             topf[:, :, k:k + 1].to_broadcast([P, TPB, E]), ALU.is_equal))
                c.wait()
                c.after(dve.tensor_tensor(hot[:, 0], hot[:, 0], hot[:, 1], ALU.add))
                dve.tensor_tensor(keep["c"][:, bass.ds(blk * TPB, TPB), :], hot[:, 0], sig[:], ALU.mult)\
                   .then_inc(c_ready, 1)
                dve.wait_ge(c_ready, blk + 1 + CREDIT)
                c.end()

        @block.scalar
        def _(act):
            for e in range(NE):
                g = io["gate_proj"][e] if e < E else io["shared_gate"][0]
                u = io["up_proj"][e] if e < E else io["shared_up"][0]
                d = io["down_proj"][e] if e < E else io["shared_down"][0]
                act.dma_start(keep["wg"][:, e], g.rearrange("(k p) m -> p k m", p=P)).then_inc(keep["moe_w"], 16)
                act.dma_start(keep["wu"][:, e], u.rearrange("(k p) m -> p k m", p=P)).then_inc(keep["moe_w"], 16)
                act.dma_start(keep["wd"][:, e], d.rearrange("(k p) m -> p k m", p=P)).then_inc(keep["moe_w"], 16)
            act.wait_ge(gate_t, 1 + CREDIT)
            act.copy(gateT[:].rearrange("p k e -> p (k e)"), psL[:, 0:KD, :].rearrange("p k e -> p (k e)"))\
               .then_inc(gateT_ready, 1)
            with act.Fori(0, BATCH) as b:
                with act.Fori(0, BPB) as q:
                    blk = b * BPB + q
                    act.wait_ge(stats_ready, blk + 1 + CREDIT)
                    act.activation(std[:], rstd[:], ACT.Sqrt).then_inc(std_ready, 1)
                    act.wait_ge(xT_done, blk + 1 + CREDIT)
                    act.wait_ge(v_done, blk + CREDIT)
                    act.wait_ge(l_done, blk + CREDIT)
                    act.wait_ge(xnT_out, 16 * blk + CREDIT)
                    for k in range(KD):
                        ins = act.copy(xnT[:, k], psT[:, k])
                    ins.then_inc(xnT_ready, 1)
                    act.wait_ge(xnT_ready, blk + 1 + CREDIT)
                    act.dma_start(dram["xnT"][:, :, bass.ds(blk * BLK, BLK)].rearrange("k p t -> p k t"), xnT[:])\
                       .then_inc(xnT_out, 16)
                    for f in range(4):
                        s = f % 2
                        act.wait_ge(qk_done, 4 * blk + f + 1 + CREDIT)
                        act.wait_ge(parts_ready[s], 2 * blk + f // 2 + CREDIT)
                        act.activation(qf[:, s], psQ[:, s], ACT.Copy, scale=(1.0 / HD if f < 2 else 1.0))\
                           .then_inc(qf_ready[s], 1)
                    act.wait_ge(v_done, blk + 1 + CREDIT)
                    act.copy(keep["v"][:, b, :, bass.ds(q * TPB, TPB), :].rearrange("p h j d -> p j h d"),
                             psV[:].rearrange("p j (h d) -> p j h d", h=HEADS)).then_inc(v_free, 1)
                    act.wait_ge(l_done, blk + 1 + CREDIT)
                    act.wait_ge(c_ready, blk + CREDIT)
                    act.activation(sig[:], psL[:], ACT.Sigmoid).then_inc(sig_ready, 1)

            act.wait_ge(xnT_out, 16 * NBLK + CREDIT)

        @block.tensor
        def _(pe):
            pe.wait_ge(w_in, 48 + CREDIT)
            pe.wait_ge(iota_ready, 1 + CREDIT)
            for k in range(KD):
                ins = pe.transpose(psL[:, k, :], gate_rows[:, k * P:(k + 1) * P], keep["ident"][0:E, 0:E])
            ins.then_inc(gate_t, 1)
            pe.wait_ge(gateT_ready, 1 + CREDIT)
            with pe.Fori(0, NBLK) as blk:
                pe.wait_ge(x_free, blk + 1 + CREDIT)
                pe.wait_ge(xnT_ready, blk + CREDIT)
                for j in range(TPB):
                    for k in range(KD):
                        ins = pe.transpose(psT[:, k, j * P:(j + 1) * P], xn[:, j, k * P:(k + 1) * P], keep["ident"][:])
                ins.then_inc(xT_done, 1)
                pe.wait_ge(xnT_ready, blk + 1 + CREDIT)
                for f in range(4):
                    s = f % 2
                    pe.wait_ge(qf_ready[s], 2 * blk + f // 2 + CREDIT)
                    for k in range(KD):
                        ins = pe.matmul(psQ[:, s], wqkv[:, k, f * P:(f + 1) * P], xnT[:, k],
                                        start=(k == 0), stop=(k == KD - 1))
                    ins.then_inc(qk_done, 1)
                pe.wait_ge(v_free, blk + CREDIT)
                for j in range(TPB):
                    for k in range(KD):
                        ins = pe.matmul(psV[:, j], xnT[:, k, j * P:(j + 1) * P], wqkv[:, k, 2 * D:3 * D],
                                        start=(k == 0), stop=(k == KD - 1))
                ins.then_inc(v_done, 1)
                pe.wait_ge(sig_ready, blk + CREDIT)
                pe.wait_ge(c_ready, blk + CREDIT)
                for j in range(TPB):
                    for k in range(KD):
                        ins = pe.matmul(psL[:, j], xnT[:, k, j * P:(j + 1) * P], gateT[:, k],
                                        start=(k == 0), stop=(k == KD - 1))
                ins.then_inc(l_done, 1)


def phase_experts(nc, io, keep, dram):
    with ExitStack() as ctx:
        sb = lambda name, shape, dt=F32: ctx.enter_context(nc.sbuf_tensor(name, shape, dt))
        ps = lambda name, shape, dt=F32: ctx.enter_context(nc.psum_tensor(name, shape, dt))
        sems = []
        sem = lambda name: credited(ctx, nc, sems, name)
        MT = M // P

        xT = [sb(f"xT{u}", [P, KD, P]) for u in range(2)]
        cc = sb("cc", [P, 2, NE])
        sg = sb("sg", [P, 2, M])
        h = sb("h", [P, 2, M])
        hT = sb("hT", [P, 2, MT, P])
        y = sb("y", [P, 2, D])
        psG = ps("psG", [P, 2, M])
        psU = ps("psU", [P, 2, M])
        psH = ps("psH", [P, 2, MT, P])
        psY = ps("psY", [P, 2, 512])

        two = lambda name: [sem(f"m_{name}{s}") for s in range(2)]
        xt_in = two("xt_in")
        gu_done, sg_ready, h_ready = two("gu_done"), two("sg_ready"), two("h_ready")
        t_done, hT_ready, d_done = two("t_done"), two("hT_ready"), two("d_done")
        y_ready, y_out = two("y_ready"), two("y_out")
        cc_ready = sem("m_cc_ready")
        block = ctx.enter_context(nc.Block())
        G = 2 * NE

        @block.sync
        def _(sp):
            for s in sems:
                sp.sem_inc(s, CREDIT)
            def store(j, u):
                sp.wait_ge(y_ready[u], j + 1 + CREDIT)
                rows = slice((2 * j + u) * P, (2 * j + u + 1) * P) if isinstance(j, int) else bass.ds((2 * j + u) * P, P)
                sp.dma_start(dram["ffn"][rows, :], y[:, u]).then_inc(y_out[u], 16)

            for u in range(2):
                sp.dma_start(xT[u][:], dram["xnT"][:, :, u * P:(u + 1) * P].rearrange("k p t -> p k t"))\
                  .then_inc(xt_in[u], 16)
            with sp.Fori(0, NT // 2 - 1) as j:
                for u in range(2):
                    g = (u + 1) * NE - 1
                    sp.wait_ge(gu_done[g % 2], NE * j + g // 2 + 1 + CREDIT)
                    sp.dma_start(xT[u][:], dram["xnT"][:, :, bass.ds((2 * j + u + 2) * P, P)]
                                 .rearrange("k p t -> p k t")).then_inc(xt_in[u], 16)
                    if u == 1:
                        store(j, 0)
                store(j, 1)
            for u in range(2):
                store(NT // 2 - 1, u)
            for u in range(2):
                sp.wait_ge(y_out[u], 16 * (NT // 2) + CREDIT)


        @block.scalar
        def _(act):
            with act.Fori(0, NT // 2) as j:
                for g in range(G + 1):
                    if g < G:
                        s = g % 2
                        act.wait_ge(gu_done[s], NE * j + g // 2 + 1 + CREDIT)
                        act.wait_ge(h_ready[s], NE * j + g // 2 + CREDIT)
                        act.activation(sg[:, s], psG[:, s], ACT.Silu).then_inc(sg_ready[s], 1)
                    if g >= 1:
                        s, n = (g - 1) % 2, (g - 1) // 2
                        act.wait_ge(t_done[s], NE * j + n + 1 + CREDIT)
                        act.wait_ge(d_done[s], NE * j + n + CREDIT)
                        act.copy(hT[:, s].rearrange("p m t -> p (m t)"), psH[:, s].rearrange("p m t -> p (m t)"))\
                           .then_inc(hT_ready[s], 1)

        @block.vector
        def _(dve):
            dve.memset(cc[:], 1.0).then_inc(cc_ready, 1)

            def store(j, u):
                g = (u + 1) * NE - 1
                dve.wait_ge(d_done[g % 2], NE * j + g // 2 + 1 + CREDIT)
                dve.wait_ge(y_out[u], 16 * j + CREDIT)
                dve.tensor_copy(y[:, u], psY[:, u, 0:D]).then_inc(y_ready[u], 1)

            with dve.Fori(0, NT // 2) as j:
                dve.wait_ge(cc_ready, j + 1 + CREDIT)
                for s in range(2):
                    dve.wait_ge(h_ready[s], NE * j + CREDIT)
                dve.tensor_copy(cc[:, :, 0:E], keep["c"][:, bass.ds(2 * j, 2), :]).then_inc(cc_ready, 1)
                dve.wait_ge(cc_ready, j + 2 + CREDIT)
                for g in range(G):
                    s, u, e = g % 2, g // NE, g % NE
                    dve.wait_ge(sg_ready[s], NE * j + g // 2 + 1 + CREDIT)
                    dve.wait_ge(t_done[s], NE * j + g // 2 + CREDIT)
                    dve.scalar_tensor_tensor(out=h[:, s], in0=sg[:, s], scalar=cc[:, u, e:e + 1], in1=psU[:, s],
                                             op0=ALU.mult, op1=ALU.mult).then_inc(h_ready[s], 1)
                    if g == NE + 2:
                        store(j, 0)
                store(j, 1)

        @block.tensor
        def _(pe):
            pe.wait_ge(keep["moe_w"], 16 * 3 * NE)
            with pe.Fori(0, NT // 2) as j:
                for g in range(G + 2):
                    if g < G:
                        s, u, e = g % 2, g // NE, g % NE
                        if e == 0:
                            pe.wait_ge(xt_in[u], 16 * j + 16 + CREDIT)
                        pe.wait_ge(h_ready[s], NE * j + g // 2 + CREDIT)
                        for w, dst in ((keep["wg"], psG), (keep["wu"], psU)):
                            for k in range(KD):
                                ins = pe.matmul(dst[:, s], xT[u][:, k], w[:, e, k], start=(k == 0), stop=(k == KD - 1))
                        ins.then_inc(gu_done[s], 1)
                    if 2 <= g:
                        s, u, e, n = (g - 2) % 2, (g - 2) // NE, (g - 2) % NE, (g - 2) // 2
                        pe.wait_ge(hT_ready[s], NE * j + n + 1 + CREDIT)
                        if e == 0:
                            pe.wait_ge(y_ready[u], j + CREDIT)
                        for m in range(MT):
                            ins = pe.matmul(psY[:, u, 0:D], hT[:, s, m], keep["wd"][:, e, m],
                                            start=(e == 0 and m == 0), stop=(e == NE - 1 and m == MT - 1))
                        ins.then_inc(d_done[s], 1)
                    if 1 <= g <= G:
                        s, n = (g - 1) % 2, (g - 1) // 2
                        pe.wait_ge(h_ready[s], NE * j + n + 1 + CREDIT)
                        pe.wait_ge(hT_ready[s], NE * j + n + CREDIT)
                        for m in range(MT):
                            ins = pe.transpose(psH[:, s, m], h[:, s, m * P:(m + 1) * P], keep["ident"][:])
                        ins.then_inc(t_done[s], 1)


def score_steps():
    out = []
    for c in range(BPB):
        for st in range(TPB * c + TPB):
            r = st - TPB * c
            first = c == 0 and st == 1
            out.append((c, st, 0 if r < 0 or first else P * r, first))
    return out


def max_units():
    return [(a, i, ch, min(BLK, P * (i + 1) - BLK * ch))
            for a in range(2) for i in range(ST_T) for ch in range(i // TPB + 1)]


def phase_attention(nc, io, keep, dram):
    with ExitStack() as ctx:
        sb = lambda name, shape, dt=F32: ctx.enter_context(nc.sbuf_tensor(name, shape, dt))
        ps = lambda name, shape, dt=F32: ctx.enter_context(nc.psum_tensor(name, shape, dt))
        sems = []
        sem = lambda name: credited(ctx, nc, sems, name)

        STEPS, UNITS = score_steps(), max_units()
        NSTEP, NUNIT = len(STEPS), len(UNITS)
        SLOTS = 4
        assert NSTEP % SLOTS == 0
        LAST = [max(k for k, s in enumerate(STEPS) if s[0] == c) for c in range(BPB)]
        FIRST_U, LAST_U = 5, 32
        LAG = 2
        EVAC = LAG + 1
        K_ALL = KQ + 3
        RING_HEAD = NUNIT + 1 + BPB

        kslab = [[sb(f"kslab{u}{a}", [P, T], BF16) for a in range(2)] for u in range(2)]
        qslab = [[sb(f"qslab{u}{a}", [P, T], BF16) for a in range(2)] for u in range(2)]
        vaug = [sb(f"vaug{u}", [P, ST_T, VW]) for u in range(2)]
        prob = [sb(f"prob{s}", [P, 2, BLK]) for s in range(SLOTS)]
        pmax = sb("pmax", [P, 2 * ST_T, BPB])
        nmax = sb("nmax", [P, 2 * ST_T])
        mrest = sb("mrest", [2 * ST_T, 2, P])
        mpart = sb("mpart", [2 * ST_T, 3, P], BF16)
        ident_b = sb("ident_b", [P, P], BF16)
        mask_q = sb("mask_q", [P, P], BF16)
        mask_k = sb("mask_k", [P, 2 * P], BF16)
        fold = sb("fold", [P, 2, OC])
        ov = [sb(f"ov{s}", [P, BLK]) for s in range(2)]
        o = sb("o_head", [P, ST_T, 2, OC])
        rs = sb("rs", [P, ST_T, 2])
        rl = sb("rl", [P, ST_T])
        o1 = sb("o1", [P, ST_T, VD])
        o2 = sb("o2", [P, ST_T, VD])
        lam_in = sb("lam_in", [P, 4, HD])
        lam_w = sb("lam_w", [P, 2, HD])
        lam_s = sb("lam_s", [P, 2])
        lam_e = sb("lam_e", [P, 2])
        lam = sb("lam", [P, 2])

        psS = [ps(f"psS{s}", [P, 2, BLK]) for s in range(2)]
        psR = [ps(f"psR{s}", [P, BLK]) for s in range(2)]
        psV = [ps(f"psVo{s}", [P, BLK]) for s in range(2)]

        lam_load = sem("b_lam_load")
        lam_step = sem("b_lam_step")
        lam_exp = sem("b_lam_exp")
        lam_ready = sem("b_lam_ready")
        masks = sem("b_masks")
        slab_in = [sem(f"b_slab_in{u}") for u in range(2)]
        mrow_in = sem("b_mrow_in")
        scores_done = sem("b_scores_done")
        prob_ready = [sem(f"b_prob_ready{s}") for s in range(SLOTS)]
        pv_done = [sem(f"b_pv_done{s}") for s in range(SLOTS)]
        ov_ready = [sem(f"b_ov_ready{s}") for s in range(2)]
        ring_full = sem("b_ring_full")
        ring_free = sem("b_ring_free")
        nmax_ready = sem("b_nmax_ready")
        mpart_ready = sem("b_mpart_ready")
        dchain = sem("b_dchain")
        rs_ready = sem("b_rs_ready")
        pchain = sem("b_pchain")
        setup = sem("b_setup")
        v_ready = sem("b_v_ready")
        post_done = sem("b_post_done")
        block = ctx.enter_context(nc.Block())

        qk_rows = dram["qk"].rearrange("w s b f t -> w s (b f) t")

        def units_at(k):
            n = LAST_U - FIRST_U + 1
            if not FIRST_U <= k <= LAST_U:
                return []
            return UNITS[(k - FIRST_U) * NUNIT // n:(k - FIRST_U + 1) * NUNIT // n]

        def ring_at(k, more):
            out = [("max", n) for n in units_at(k)] if more else []
            out += [("fold", c) for c in range(BPB) if LAST[c] + EVAC + 1 == k or (k == NSTEP and c == BPB - 1)]
            if more and k == LAST_U + 2:
                out.append(("turn", None))
            return out

        def ring_base(n):
            return NUNIT + 1 + RING_HEAD * n

        def heads(eng, turn):
            with eng.Fori(0, NH // 2 - 1) as j:
                for u in range(2):
                    turn(2 * j + u, u, True)
            turn(NH - 2, 0, True)
            turn(NH - 1, 1, False)

        @block.sync
        def _(sp):
            for s in sems:
                sp.sem_inc(s, CREDIT)
            for w, name in enumerate(("lq1", "lk1", "lq2", "lk2")):
                sp.dma_start(lam_in[:, w, :], io[name].partition_broadcast(P)).then_inc(lam_load, 16)
            sp.wait_ge(setup, 2 + CREDIT)

            def load(n, u):
                for a in range(2):
                    for x in range(3):
                        rows = bass.ds(n * (2 * HD) + a * HD, HD)
                        sp.dma_start(qslab[u][a][x * 3 * HD:(x + 1) * 3 * HD, :], qk_rows[0, :, rows, :])\
                          .then_inc(slab_in[u], 16)
                        sp.dma_start(kslab[u][a][x * 3 * HD:(x + 1) * 3 * HD, :],
                                     qk_rows[1, x, rows, :].partition_broadcast(3)).then_inc(slab_in[u], 16)

            def maxima(n, u):
                sp.wait_ge(mpart_ready, n + 1 + CREDIT)
                for a in range(2):
                    for x in range(3):
                        sp.dma_start(qslab[u][a][KQ + x:KQ + x + 1, :].rearrange("o (i t) -> o i t", t=P),
                                     mpart[a * ST_T:(a + 1) * ST_T, x, :]).then_inc(mrow_in, 16)

            load(0, 0)
            maxima(0, 0)

            def turn(n, u, more):
                if more:
                    sp.wait_ge(scores_done, NSTEP * n + CREDIT)
                    load(n + 1, 1 - u)
                    maxima(n + 1, 1 - u)
            heads(sp, turn)

        @block.gpsimd
        def _(pool):
            c = Chain(pool, masks)
            c.mark(pool.memset(ident_b[:], 0.0))
            c.mark(pool.memset(mask_q[:], 0.0))
            c.mark(pool.memset(mask_k[:, 0:P], NEG))
            c.mark(pool.memset(mask_k[:, P:2 * P], 0.0))
            c.mark(pool.memset(fold[:], 0.0))
            c.wait()
            c.mark(pool.affine_select(out=ident_b[:], in_=ident_b[:], compare_op=ALU.not_equal, fill=1.0, base=0,
                                      pattern=[[-1, P]], channel_multiplier=1))
            c.mark(pool.affine_select(out=mask_q[:], in_=mask_q[:], compare_op=ALU.is_ge, fill=NEG, base=0,
                                      pattern=[[-1, P]], channel_multiplier=1))
            c.mark(pool.affine_select(out=mask_k[:, P:2 * P], in_=mask_k[:, P:2 * P], compare_op=ALU.is_ge, fill=NEG,
                                      base=0, pattern=[[1, P]], channel_multiplier=-1))
            for odd in range(2):
                c.after(pool.affine_select(out=fold[:], in_=fold[:], compare_op=ALU.not_equal, fill=1.0,
                                           base=-VW * odd, pattern=[[-2 * VW, 2], [-1, OC]], channel_multiplier=1))
            pool.wait_ge(setup, 1 + CREDIT)

            def values(n, u):
                pool.tensor_copy(vaug[u][:, :, 0:VD], v_rows[:, bass.ds(n, 1)].rearrange("p o s d -> p (o s) d"))\
                    .then_inc(v_ready, 1)

            v_rows = keep["v"][:].rearrange("p b h s d -> p (b h) s d")
            values(0, 0)
            pool.wait_ge(lam_ready, 1 + CREDIT)

            def turn(n, u, more):
                if more:
                    for s in range(SLOTS):
                        pool.wait_ge(pv_done[s], (NSTEP // SLOTS) * n + CREDIT)
                    values(n + 1, 1 - u)
                pool.wait_ge(rs_ready, n + 1 + CREDIT)
                p = Chain(pool, pchain)
                p.turn(2 * n)
                pool.wait_ge(post_done, n + CREDIT)
                p.mark(pool.tensor_tensor(o1[:], o[:, :, 0, 0:VD], rs[:, :, 0:1].to_broadcast([P, ST_T, VD]), ALU.mult))
                p.after(pool.tensor_tensor(o2[:], o[:, :, 1, 0:VD], rl[:].unsqueeze(2).to_broadcast([P, ST_T, VD]),
                                           ALU.mult))
                pool.tensor_tensor(keep["o"][:, bass.ds(n, 1)].rearrange("p o s d -> p (o s) d"), o1[:], o2[:],
                                   ALU.subtract).then_inc(post_done, 1)
            heads(pool, turn)

        @block.scalar
        def _(act):
            act.wait_ge(lam_step, 2 + CREDIT)
            act.activation(lam_e[:], lam_s[:], ACT.Exp).then_inc(lam_exp, 1)

            def turn(n, u, more):
                for k in range(NSTEP):
                    off, s = STEPS[k][2], k % SLOTS
                    act.wait_ge(scores_done, NSTEP * n + k + 1 + CREDIT)
                    act.wait_ge(pv_done[s], (NSTEP // SLOTS) * n + k // SLOTS + CREDIT)
                    act.activation(prob[s][:, :, off:BLK], psS[k % 2][:, :, off:BLK], ACT.Exp)\
                       .then_inc(prob_ready[s], 1)
                    for c in range(BPB - 1):
                        if LAST[c] + EVAC == k:
                            copy_sum(n, c, more)
                copy_sum(n, BPB - 1, more)

            def copy_sum(n, c, more):
                order = [x for k in range(NSTEP + 1) for x in ring_at(k, more)]
                k = LAST[c]
                for q in (k - 1, k):
                    act.wait_ge(pv_done[q % SLOTS], (NSTEP // SLOTS) * n + q // SLOTS + 1 + CREDIT)
                if c < 2:
                    act.wait_ge(rs_ready, n + CREDIT)
                else:
                    act.wait_ge(ring_free, ring_base(n) + order.index(("fold", c - 2)) + 1 + CREDIT)
                act.copy(ov[c % 2][:], psV[c % 2][:]).then_inc(ov_ready[c % 2], 1)
            heads(act, turn)

        @block.vector
        def _(dve):
            lc = Chain(dve, lam_step)
            dve.wait_ge(lam_load, 64 + CREDIT)
            lv = lam_in[:].rearrange("p (m w) d -> p m w d", w=2)
            lc.after(dve.tensor_tensor(lam_w[:], lv[:, :, 0], lv[:, :, 1], ALU.mult))
            lc.after(dve.tensor_reduce(lam_s[:], lam_w[:], AX.X, ALU.add))
            dve.wait_ge(lam_exp, 1 + CREDIT)
            lc.after(dve.tensor_tensor(lam[:, 0:1], lam_e[:, 0:1], lam_e[:, 1:2], ALU.subtract))
            dve.tensor_scalar(lam[:, 1:2], lam[:, 0:1], LAMBDA_INIT, None, ALU.add).then_inc(lam_ready, 1)
            for u in range(2):
                lc.mark(dve.memset(vaug[u][:, :, VD + 1:VW], 0.0))
                ins = dve.memset(vaug[u][:, :, VD:VD + 1], 1.0)
                if u == 0:
                    lc.mark(ins)
            ins.then_inc(setup, 1)
            for u in range(2):
                for a in range(2):
                    ins = dve.memset(kslab[u][a][64:96, :], 1.0)
                    if (u, a) != (1, 1):
                        lc.mark(ins)
            ins.then_inc(setup, 1)
            lc.after(dve.memset(pmax[:], NEG))
            dve.wait_ge(setup, 2 + CREDIT)
            dve.wait_ge(lam_ready, 1 + CREDIT)
            CH = 4

            class Ring:
                base, n, slot0 = 0, 0, 0

            def ring_bank():
                dve.wait_ge(ring_full, Ring.base + Ring.n + 1 + CREDIT)
                Ring.n += 1
                return psR[(Ring.slot0 + Ring.n - 1) % 2]

            def take_max(unit):
                a, i, ch, w = unit
                dve.tensor_reduce(pmax[:, a * ST_T + i, ch:ch + 1], ring_bank()[:, 0:w], AX.X, ALU.max)\
                   .then_inc(ring_free, 1)

            def whole_max():
                dve.wait_ge(ring_free, Ring.base + Ring.n + CREDIT)
                dve.tensor_reduce(nmax[:], pmax[:], AX.X, ALU.max, negate=True).then_inc(nmax_ready, 1)

            def cut_max(n, c):
                src = ring_bank()[0:2 * ST_T, 0:P]
                dve.wait_ge(mrow_in, 96 * n + CREDIT)
                c.after(dve.tensor_copy(mpart[:, 0], src))
                dve.tensor_tensor(mrest[:, 0], src, mpart[:, 0], ALU.subtract).then_inc(ring_free, 1)
                dve.wait_ge(ring_free, Ring.base + Ring.n + CREDIT)
                c.after(dve.tensor_copy(mpart[:, 1], mrest[:, 0]))
                c.after(dve.tensor_tensor(mrest[:, 1], mrest[:, 0], mpart[:, 1], ALU.subtract))
                dve.tensor_copy(mpart[:, 2], mrest[:, 1]).then_inc(mpart_ready, 1)

            c = Chain(dve, dchain)
            for unit in UNITS:
                take_max(unit)
            whole_max()
            cut_max(0, c)

            def turn(n, u, more):
                c = Chain(dve, dchain)
                c.turn(3 + CH * n)
                Ring.base, Ring.n, Ring.slot0 = ring_base(n), 0, (NUNIT + 1 + RING_HEAD * u) % 2
                for k in range(NSTEP + 1):
                    if k == FIRST_U and more:
                        dve.wait_ge(nmax_ready, n + 1 + CREDIT)
                    for kind, what in ring_at(k, more):
                        if kind == "max":
                            take_max(what)
                        elif kind == "fold":
                            dve.wait_ge(post_done, n + CREDIT)
                            dve.tensor_copy(o[:, TPB * what:TPB * what + TPB].rearrange("p i a d -> p (i a d)"),
                                            ring_bank()[:, 0:TPB * 2 * OC]).then_inc(ring_free, 1)
                        else:
                            cut_max(n + 1, c)
                    if k == LAST_U and more:
                        whole_max()
                dve.wait_ge(ring_free, Ring.base + Ring.n + CREDIT)
                c.after(dve.reciprocal(rs[:], o[:, :, :, VD]))
                dve.tensor_scalar(rl[:], rs[:, :, 1], lam[:, 1:2], None, ALU.mult).then_inc(rs_ready, 1)
            heads(dve, turn)

        @block.tensor
        def _(pe):
            pe.wait_ge(masks, 10 + CREDIT)
            pe.wait_ge(v_ready, 1 + CREDIT)

            class Ring:
                base, n, slot0 = 0, 0, 0

            def take_slot():
                ring = Ring.base + Ring.n
                if not isinstance(ring, int) or ring >= 2:
                    pe.wait_ge(ring_free, ring - 1 + CREDIT)
                s = (Ring.slot0 + Ring.n) % 2
                Ring.n += 1
                return psR[s]

            def max_unit(u, unit):
                a, i, ch, w = unit
                dst = take_slot()
                diag = ch == i // TPB
                ins = pe.matmul(dst[:, 0:w], qslab[u][a][0:KQ, i * P:(i + 1) * P],
                                kslab[u][a][0:KQ, ch * BLK:ch * BLK + w], start=True, stop=True)
                if diag:
                    ins = pe.matmul(dst[:, w - P:w], ident_b[:], mask_q[:], start=False, stop=True,
                                    skip_group_check=True)
                ins.then_inc(ring_full, 1)

            def turn_max(n):
                pe.wait_ge(nmax_ready, n + 1 + CREDIT)
                dst = take_slot()
                pe.transpose(dst[0:2 * ST_T, 0:P], nmax[:], keep["ident"][:]).then_inc(ring_full, 1)

            pe.wait_ge(slab_in[0], 12 * 16 + CREDIT)
            for unit in UNITS:
                max_unit(0, unit)
            turn_max(0)

            def scores(n, u, k):
                c, st, off, first = STEPS[k]
                q = (k - 2) % SLOTS
                pe.wait_ge(prob_ready[q], (NSTEP // SLOTS) * n + ((k - 2) // SLOTS + 1 if k >= 2 else 0) + CREDIT)
                diag = st >= TPB * c
                for a in range(2):
                    ins = pe.matmul(psS[k % 2][:, a, off:BLK], kslab[u][a][0:K_ALL, st * P:(st + 1) * P],
                                    qslab[u][a][0:K_ALL, c * BLK + off:(c + 1) * BLK], start=True, stop=True)
                    if diag:
                        lo = 0 if first else P
                        ins = pe.matmul(psS[k % 2][:, a, off:off + 2 * P - lo], ident_b[:], mask_k[:, lo:2 * P],
                                        start=False, stop=True, skip_group_check=True)
                ins.then_inc(scores_done, 1)

            def value_product(n, u, k):
                c, st, off, _w = STEPS[k]
                pe.wait_ge(prob_ready[k % SLOTS], (NSTEP // SLOTS) * n + k // SLOTS + 1 + CREDIT)
                if st == 0:
                    pe.wait_ge(ov_ready[c % 2], 2 * n + c // 2 + CREDIT)
                for a in range(2):
                    g = 2 * a + st % 2
                    ins = pe.matmul(psV[c % 2][g * VW:(g + 1) * VW, off:BLK], vaug[u][:, st, :],
                                    prob[k % SLOTS][:, a, off:BLK], start=(st < 2), stop=(st >= TPB * c + TPB - 2),
                                    skip_group_check=True)
                ins.then_inc(pv_done[k % SLOTS], 1)

            def fold_sum(n, c):
                pe.wait_ge(ov_ready[c % 2], 2 * n + c // 2 + 1 + CREDIT)
                dst = take_slot()
                for i in range(TPB):
                    ins = pe.matmul(dst[:, i * 2 * OC:(i + 1) * 2 * OC], ov[c % 2][:, i * P:(i + 1) * P],
                                    fold[:].rearrange("p a d -> p (a d)"), start=True, stop=True)
                ins.then_inc(ring_full, 1)

            def turn(n, u, more):
                Ring.base, Ring.n, Ring.slot0 = ring_base(n), 0, (NUNIT + 1 + RING_HEAD * u) % 2
                pe.wait_ge(mrow_in, 96 * (n + 1) + CREDIT)
                pe.wait_ge(v_ready, n + 1 + CREDIT)
                for k in range(NSTEP):
                    scores(n, u, k)
                    if k == FIRST_U and more:
                        pe.wait_ge(slab_in[1 - u], loaded(n, u) + CREDIT)
                    for kind, what in ring_at(k, more):
                        if kind == "max":
                            max_unit(1 - u, what)
                        elif kind == "fold":
                            fold_sum(n, what)
                        else:
                            turn_max(n + 1)
                    if k >= LAG:
                        value_product(n, u, k - LAG)
                for k in range(NSTEP - LAG, NSTEP):
                    value_product(n, u, k)
                for kind, what in ring_at(NSTEP, more):
                    fold_sum(n, what)

            def loaded(n, u):
                return (n + 1 - (1 - u)) * 96 + 192

            heads(pe, turn)


def phase_project(nc, io, keep, dram):
    with ExitStack() as ctx:
        sb = lambda name, shape, dt=F32: ctx.enter_context(nc.sbuf_tensor(name, shape, dt))
        ps = lambda name, shape, dt=F32: ctx.enter_context(nc.psum_tensor(name, shape, dt))
        sems = []
        sem = lambda name: credited(ctx, nc, sems, name)

        wp = sb("wp", [P, KD, D])
        gamma = sb("gamma", [P, 1])
        wps = sb("wps", [P, KD, D])
        sq = sb("sq", [P, HEADS, TPB, VD])
        ss = sb("ss", [P, HEADS, TPB])
        var = sb("var", [P, HEADS, TPB])
        root = sb("root", [P, HEADS, TPB])
        inv = sb("inv", [P, HEADS, TPB])
        y = sb("y_c", [P, TPB, D])
        yT = sb("yT", [P, KD, BLK])
        x = sb("x_c", [P, TPB, D])
        f = sb("f_c", [P, TPB, D])
        xf = sb("xf", [P, TPB, D])
        x1 = sb("x1", [P, TPB, D])
        stats = sb("stats_c", [P, TPB, 6])
        mv = sb("mv_c", [P, TPB, 2])
        vare = sb("vare", [P, TPB])
        std = sb("std_c", [P, TPB])
        rstd = sb("rstd_c", [P, TPB])
        xn = sb("xn_c", [P, TPB, D])
        xnT = sb("xnT_c", [P, KD, BLK])
        carrier = sb("carrier_c", [P, 1])

        psT = ps("psT_c", [P, KD, BLK])
        psO = ps("psO", [P, TPB, D])
        psN = ps("psN", [P, KD, BLK])

        w_in = sem("c_w_in")
        w_ready = sem("c_w_ready")
        in_x = sem("c_in_x")
        xf_ready = sem("c_xf_ready")
        var_ready = sem("c_var_ready")
        root_ready = sem("c_root_ready")
        y_ready = sem("c_y_ready")
        yT_done = sem("c_yT_done")
        yT_ready = sem("c_yT_ready")
        o_done = sem("c_o_done")
        x1_ready = sem("c_x1_ready")
        x1_out = sem("c_x1_out")
        vare_ready = sem("c_vare_ready")
        std_ready = sem("c_std_ready")
        xn_ready = sem("c_xn_ready")
        xT_done = sem("c_xT_done")
        xnT_ready = sem("c_xnT_ready")
        xnT_out = sem("c_xnT_out")
        dchain = sem("c_dchain")
        block = ctx.enter_context(nc.Block())

        @block.sync
        def _(sp):
            for s in sems:
                sp.sem_inc(s, CREDIT)
            sp.dma_start(wp[:], io["w_proj"].rearrange("(k p) n -> p k n", p=P)).then_inc(w_in, 16)
            for g in range(P // VD):
                sp.dma_start(gamma[g * VD:(g + 1) * VD, :], io["gamma"].unsqueeze(1)).then_inc(w_in, 16)
            with sp.Fori(0, NBLK) as blk:
                rows = lambda t: t[bass.ds(blk * BLK, BLK), :].rearrange("(j p) d -> p j d", p=P)
                sp.wait_ge(xf_ready, blk + CREDIT)
                sp.dma_start(x[:], rows(io["x"])).then_inc(in_x, 16)
                sp.dma_start(f[:], rows(dram["ffn"])).then_inc(in_x, 16)
                sp.wait_ge(x1_ready, blk + 1 + CREDIT)
                sp.dma_start(rows(dram["x1"]), x1[:]).then_inc(x1_out, 16)
            sp.wait_ge(x1_out, 16 * NBLK + CREDIT)
            sp.wait_ge(xnT_out, 16 * NBLK + CREDIT)

        @block.gpsimd
        def _(pool):
            with pool.Fori(0, NBLK) as blk:
                pool.wait_ge(in_x, 32 * blk + 32 + CREDIT)
                pool.wait_ge(x1_ready, blk + CREDIT)
                pool.tensor_tensor(xf[:], x[:], f[:], ALU.add).then_inc(xf_ready, 1)

        @block.scalar
        def _(act):
            with act.Fori(0, NBLK) as blk:
                act.wait_ge(var_ready, blk + 1 + CREDIT)
                act.activation(root[:], var[:], ACT.Sqrt).then_inc(root_ready, 1)
                act.wait_ge(yT_done, blk + 1 + CREDIT)
                act.wait_ge(o_done, blk + CREDIT)
                for k in range(KD):
                    ins = act.copy(yT[:, k], psT[:, k])
                ins.then_inc(yT_ready, 1)
                act.wait_ge(vare_ready, blk + 1 + CREDIT)
                act.activation(std[:], vare[:], ACT.Sqrt).then_inc(std_ready, 1)
                act.wait_ge(xT_done, blk + 1 + CREDIT)
                act.wait_ge(xnT_out, 16 * blk + CREDIT)
                for k in range(KD):
                    ins = act.copy(xnT[:, k], psN[:, k])
                ins.then_inc(xnT_ready, 1)
                act.wait_ge(xnT_ready, blk + 1 + CREDIT)
                act.dma_start(dram["xn2T"][:, :, bass.ds(blk * BLK, BLK)].rearrange("k p t -> p k t"), xnT[:])\
                   .then_inc(xnT_out, 16)

        @block.vector
        def _(dve):
            CH = 13
            dve.wait_ge(w_in, 16 * (1 + P // VD) + CREDIT)
            dve.tensor_scalar(wps[:], wp[:], gamma[:, 0:1], 1.0 - LAMBDA_INIT, ALU.mult, ALU.mult).then_inc(w_ready, 1)
            with dve.Fori(0, BATCH) as b:
                with dve.Fori(0, BPB) as q:
                    blk = b * BPB + q
                    c = Chain(dve, dchain, CH)
                    c.turn(blk * CH)
                    ob = keep["o"][:, bass.ds(b * HEADS, HEADS), bass.ds(q * TPB, TPB), :]
                    c.after(dve.tensor_tensor(sq[:], ob, ob, ALU.mult))
                    c.after(dve.tensor_reduce(ss[:], sq[:], AX.X, ALU.add))
                    dve.tensor_scalar(var[:], ss[:], 1.0 / VD, EPS, ALU.mult, ALU.add).then_inc(var_ready, 1)
                    dve.wait_ge(root_ready, blk + 1 + CREDIT)
                    c.after(dve.reciprocal(inv[:], root[:]))
                    dve.wait_ge(yT_done, blk + CREDIT)
                    for j in range(TPB):
                        ins = dve.tensor_tensor(y[:, j].rearrange("p (h d) -> p h d", h=HEADS), ob[:, :, j],
                                                inv[:, :, j:j + 1].to_broadcast([P, HEADS, VD]), ALU.mult)
                    ins.then_inc(y_ready, 1)
                    dve.wait_ge(o_done, blk + 1 + CREDIT)
                    dve.wait_ge(xf_ready, blk + 1 + CREDIT)
                    dve.wait_ge(x1_out, 16 * blk + CREDIT)
                    dve.tensor_tensor(x1[:], psO[:], xf[:], ALU.add).then_inc(x1_ready, 1)
                    dve.wait_ge(x1_ready, blk + 1 + CREDIT)
                    for j in range(TPB):
                        c.mark(dve.bn_stats(stats[:, j, :], x1[:, j, :]))
                    c.wait()
                    c.mark(dve.memset(carrier[:], 0.0))
                    for j in range(TPB):
                        c.mark(dve.bn_aggr(mv[:, j, :], stats[:, j, :]))
                    c.wait()
                    dve.tensor_scalar(vare[:], mv[:, :, 1], EPS, None, ALU.add).then_inc(vare_ready, 1)
                    dve.wait_ge(std_ready, blk + 1 + CREDIT)
                    c.after(dve.reciprocal(rstd[:], std[:]))
                    dve.wait_ge(xT_done, blk + CREDIT)
                    for j in range(TPB):
                        ins = dve.tensor_scalar(xn[:, j, :], x1[:, j, :], mv[:, j, 0:1], rstd[:, j:j + 1],
                                                ALU.subtract, ALU.mult)
                    ins.then_inc(xn_ready, 1)
                    c.end()

        @block.tensor
        def _(pe):
            pe.wait_ge(w_ready, 1 + CREDIT)
            with pe.Fori(0, NBLK) as blk:
                pe.wait_ge(y_ready, blk + 1 + CREDIT)
                pe.wait_ge(yT_ready, blk + CREDIT)
                for j in range(TPB):
                    for k in range(KD):
                        ins = pe.transpose(psT[:, k, j * P:(j + 1) * P], y[:, j, k * P:(k + 1) * P], keep["ident"][:])
                ins.then_inc(yT_done, 1)
                pe.wait_ge(yT_ready, blk + 1 + CREDIT)
                pe.wait_ge(x1_ready, blk + CREDIT)
                for j in range(TPB):
                    for k in range(KD):
                        ins = pe.matmul(psO[:, j], yT[:, k, j * P:(j + 1) * P], wps[:, k], start=(k == 0),
                                        stop=(k == KD - 1))
                ins.then_inc(o_done, 1)
                pe.wait_ge(xn_ready, blk + 1 + CREDIT)
                pe.wait_ge(xnT_ready, blk + CREDIT)
                for j in range(TPB):
                    for k in range(KD):
                        ins = pe.transpose(psN[:, k, j * P:(j + 1) * P], xn[:, j, k * P:(k + 1) * P], keep["ident"][:])
                ins.then_inc(xT_done, 1)


def phase_state_space(nc, io, keep, dram, out):
    with ExitStack() as ctx:
        sb = lambda name, shape, dt=F32: ctx.enter_context(nc.sbuf_tensor(name, shape, dt))
        ps = lambda name, shape, dt=F32: ctx.enter_context(nc.psum_tensor(name, shape, dt))
        sems = []
        sem = lambda name: credited(ctx, nc, sems, name)
        ET = 2 * DI // P
        FT = F1 // P
        XD = RANK + 2 * NS
        UNITS = NS * CT
        LOADS = 24
        HALO = NTAP - 1

        w_x = sb("w_x_raw", [XD, DI])
        w_dt = sb("w_dt_raw", [P, CT, RANK])
        winT = sb("winT", [P, KD, 2 * DI])
        woutT = sb("woutT", [P, CT, D])
        wxT = sb("wxT", [P, CT, XD])
        wdtT = sb("wdtT", [RANK, DI])
        conv_w = sb("conv_w", [P, CT, NTAP])
        vec = sb("vec", [P, 3, CT])
        a_log = sb("a_log", [P, CT, NS])
        a_exp = sb("a_exp", [P, CT, NS])
        a_neg = sb("a_neg", [P, CT, NS])
        scal = sb("scal", [P, 3])
        sgn = sb("sgn", [P, 3])
        mag = sb("mag", [P, 3])
        fac = sb("fac", [P, 4])
        k0 = sb("k0", [P, 2 * KD, F1], U8)
        k2 = sb("k2", [P, FT, D], U8)
        w0 = sb("w0", [P, KD, F1], F16)
        w1 = sb("w1", [P, FT, F1], F16)
        w2 = sb("w2", [P, FT, D], F16)
        pick = sb("pick", [XD, 2 * NS, P])

        xT = sb("xT_s", [P, KD, BLK])
        xh = sb("xh", [P, KD, BLK], F16)
        xl = sb("xl", [P, KD, BLK], F16)
        x1 = sb("x1_s", [P, TPB, D])
        xc = sb("xc", [P, CT, HALO + BLK])
        cv = sb("cv", [P, CT, BLK])
        sz = sb("sz", [P, CT, BLK])
        xs = sb("xs", [P, CT, BLK])
        xd = sb("xd", [XD, BLK])
        ab = sb("ab", [P, CT, BLK])
        ex = cv
        mx = sb("mx", [P, CT, BLK])
        dt_ = sb("dt", [P, CT, BLK])
        dtx = sb("dtx", [P, CT, BLK])
        crep = sb("crep", [P, 2, BLK])
        a = sb("a", [P, 2, BLK])
        u = sb("u", [P, 2, BLK])
        h = sb("h_d", [P, 2, BLK])
        hc = sb("hc", [P, 2, BLK])
        state = sb("state", [P, CT, NS])
        f1h = sb("f1h", [P, FT, BLK], F16)
        f1l = sb("f1l", [P, FT, BLK], F16)
        f2h = sb("f2h", [P, FT, BLK], F16)
        f2l = sb("f2l", [P, FT, BLK], F16)
        r = sb("r", [P, TPB, D])
        yg, ys = ab, mx
        ob = sb("ob", [P, TPB, D])

        w_in = dtx[:].rearrange("p c (h t) -> p (c h) t", h=2)
        w_out = dt_[:, 0:KD]
        kd = f1h[:].rearrange("p (k f) t -> p k (f t)", k=4)[:, 0:KD]

        k1 = f2h[:].rearrange("p k t -> p (k t)").bitcast(U8).rearrange("p (k f) -> p k f", k=FT)

        psY = [ps(f"psYd{c}", [P, BLK]) for c in range(CT)]
        psB = ps("psB", [P, BLK])
        psC = ps("psC", [P, BLK])
        psW = [ps(f"psW{s}", [P, BLK]) for s in range(2)]

        weights = sem("d_weights")
        consts = sem("d_consts")
        wt_full = sem("d_wt_full")
        wt_free = sem("d_wt_free")
        a_ready0 = sem("d_a_exp")
        wchain = sem("d_wchain")
        w_ready = sem("d_w_ready")
        x_in = sem("d_x_in")
        x1_in = sem("d_x1_in")
        xh_ready = sem("d_xh_ready")
        xl_ready = sem("d_xl_ready")
        full = [sem(f"d_full{s}") for s in range(2)]
        free = [sem(f"d_free{s}") for s in range(2)]
        xc_ready = sem("d_xc_ready")
        cchain = sem("d_cchain")
        conv_done = sem("d_conv_done")
        halo_ready = sem("d_halo_ready")
        xs_ready = sem("d_xs_ready")
        xd_ready = sem("d_xd_ready")
        ab_ready = sem("d_ab_ready")
        ex_ready = sem("d_ex_ready")
        ln_ready = sem("d_ln_ready")
        mx_ready = sem("d_mx_ready")
        dt_ready = sem("d_dt_ready")
        dtx_ready = sem("d_dtx_ready")
        b_full = sem("d_b_full")
        c_full = sem("d_c_full")
        crep_ready = sem("d_crep_ready")
        u_ready = sem("d_u_ready")
        a_ready = [sem(f"d_a_ready{s}") for s in range(2)]
        h_ready = [sem(f"d_h_ready{s}") for s in range(2)]
        hc_ready = [sem(f"d_hc_ready{s}") for s in range(2)]
        y_added = [sem(f"d_y_added{s}") for s in range(2)]
        high_ready = sem("d_high_ready")
        low_ready = sem("d_low_ready")
        yg_ready = sem("d_yg_ready")
        ys_ready = sem("d_ys_ready")
        out_sent = sem("d_out_sent")
        block = ctx.enter_context(nc.Block())

        def sign_unit(sidx):
            if sidx < 4:
                return [("l1", 2 * sidx), ("l1", 2 * sidx + 1)]
            if sidx < 12:
                return [("l2", sidx - 4)]
            return [("l3", sidx - 12)]

        ORDER = [("xz", e) for e in range(ET)] + [("xd", 0)] + [("dt", c) for c in range(CT)]
        for sidx in range(NS):
            ORDER += sign_unit(sidx)
        ORDER += [("out", j) for j in range(TPB)]
        PER = [(len(ORDER) + 1) // 2, len(ORDER) // 2]

        def full_at(blk, kind):
            n = ORDER.index(kind)
            return n % 2, PER[n % 2] * blk + n // 2 + 1

        def weight_copies():
            got = []
            for k in range(KD):
                for half in range(2):
                    got.append((winT[:, k, half * BLK:(half + 1) * BLK], psW[len(got) % 2][:]))
            for c in range(CT):
                got.append((woutT[:, c, :], psW[len(got) % 2][:, 0:D]))
            for c in range(CT):
                got.append((wxT[:, c, :], psW[len(got) % 2][:, 0:XD]))
            got.append((wdtT[:], psW[len(got) % 2][0:RANK, :]))
            return got

        @block.sync
        def _(sp):
            for s in sems:
                sp.sem_inc(s, CREDIT)
            loads = [
                (w_in, io["in_proj"].rearrange("(e p) d -> p e d", p=P)),
                (w_out, io["out_proj"].rearrange("(k p) i -> p k i", p=P)),
                (w_x[:], io["x_proj"]),
                (w_dt[:], io["dt_proj"].rearrange("(c p) r -> p c r", p=P)),
                (conv_w[:], io["conv_w"].rearrange("(c p) o t -> p c (o t)", p=P)),
                (a_log[:], io["A_log"].rearrange("(c p) s -> p c s", p=P)),
                (k0[:], io["k0"].rearrange("(k p) f -> p k f", p=P)),
                (k1, io["k1"].rearrange("(k p) f -> p k f", p=P)),
                (k2[:], io["k2"].rearrange("(k p) f -> p k f", p=P)),
            ]
            for n, name in enumerate(("conv_b", "dt_b", "D_skip")):
                for c in range(CT):
                    loads.append((vec[:, n, c:c + 1], io[name][c * P:(c + 1) * P].unsqueeze(1)))
            for n, name in enumerate(("s0", "s1", "s2")):
                loads.append((scal[:, n:n + 1], io[name].partition_broadcast(P)))
            for dst, src in loads:
                sp.dma_start(dst, src).then_inc(weights, 16)
            assert len(loads) == LOADS
            with sp.Fori(0, NBLK) as blk:
                rows = lambda t: t[bass.ds(blk * BLK, BLK), :].rearrange("(j p) d -> p j d", p=P)
                sp.wait_ge(xl_ready, blk + CREDIT)
                sp.wait_ge(dt_ready, CT * blk + CREDIT)
                sp.dma_start(xT[:], dram["xn2T"][:, :, bass.ds(blk * BLK, BLK)].rearrange("k p t -> p k t"))\
                  .then_inc(x_in, 16)
                sp.dma_start(x1[:], rows(dram["x1"])).then_inc(x1_in, 16)
                for j in (TPB - 2, TPB - 1):
                    s, n = full_at(blk, ("out", j))
                    sp.wait_ge(free[s], n + CREDIT)
                sp.dma_start(rows(out), ob[:]).then_inc(out_sent, 16)
            sp.wait_ge(out_sent, 16 * NBLK + CREDIT)

        @block.gpsimd
        def _(pool):
            c = Chain(pool, consts)
            c.after(pool.memset(pick[:], 1.0))
            c.mark(pool.affine_select(out=pick[:], in_=pick[:], compare_op=ALU.is_equal, fill=0.0, base=-RANK,
                                      pattern=[[-1, 2 * NS], [0, P]], channel_multiplier=1))
            with pool.Fori(0, NBLK) as blk:
                for t in range(UNITS):
                    s, i, sidx, c_ = t % 2, t // 2, t // CT, t % CT
                    n = UNITS // 2 * blk + i
                    pool.wait_ge(h_ready[s], n + 1 + CREDIT)
                    if c_ == 0:
                        pool.wait_ge(crep_ready, NS * blk + sidx + 1 + CREDIT)
                    pool.wait_ge(y_added[s], n + CREDIT)
                    pool.tensor_tensor(hc[:, s], h[:, s], crep[:, sidx % 2], ALU.mult)
                    pool.tensor_copy(state[:, c_, sidx:sidx + 1], h[:, s, BLK - 1:BLK]).then_inc(hc_ready[s], 1)

        @block.scalar
        def _(act):
            act.wait_ge(weights, 16 * LOADS + CREDIT)
            act.activation(a_exp[:], a_log[:], ACT.Exp).then_inc(a_ready0, 1)
            def block_of(b, q):
                blk = b * BPB + q
                act.wait_ge(x_in, 16 * blk + 16 + CREDIT)
                act.wait_ge(high_ready, 2 * FT * blk + CREDIT)
                act.copy(xh[:], xT[:]).then_inc(xh_ready, 1)
                for e in range(ET):
                    s, n = full_at(blk, ("xz", e))
                    act.wait_ge(full[s], n + CREDIT)
                    if e < CT:
                        if e == 0:
                            act.wait_ge(halo_ready, blk + b + 1 + CREDIT)
                        act.copy(xc[:, e, HALO:], psW[s][:]).then_inc(free[s], 1)
                    else:
                        if e == CT:
                            act.wait_ge(ys_ready, CT * blk + CREDIT)
                        act.activation(sz[:, e - CT], psW[s][:], ACT.Silu).then_inc(free[s], 1)
                for c in range(CT):
                    act.wait_ge(conv_done, CT * blk + c + 1 + CREDIT)
                    act.wait_ge(yg_ready, CT * blk + CREDIT)
                    act.activation(xs[:, c], cv[:, c], ACT.Silu, bias=vec[:, 0, c:c + 1]).then_inc(xs_ready, 1)
                s, n = full_at(blk, ("xd", 0))
                act.wait_ge(full[s], n + CREDIT)
                act.copy(xd[:], psW[s][0:XD, :]).then_inc(free[s], 1)
                for c in range(CT):
                    s, n = full_at(blk, ("dt", c))
                    act.wait_ge(full[s], n + CREDIT)
                    act.wait_ge(mx_ready, CT * blk + c + 1 + CREDIT)
                    act.activation(ab[:, c], psW[s][:], ACT.Abs, bias=vec[:, 1, c:c + 1]).then_inc(free[s], 1)
                act.wait_ge(free[s], n + CREDIT)
                s, n = full_at(blk, ("dt", CT - 2))
                act.wait_ge(free[s], n + CREDIT)
                act.activation(ex[:], ab[:], ACT.Exp, scale=-1.0).then_inc(ex_ready, 1)
                act.wait_ge(ex_ready, blk + 1 + CREDIT)
                act.activation(ab[:], ex[:], ACT.Ln, bias=1.0).then_inc(ln_ready, 1)
                for sidx in range(NS):
                    act.wait_ge(c_full, NS * blk + sidx + 1 + CREDIT)
                    act.wait_ge(hc_ready[1], UNITS // 2 * blk + max(0, 2 * sidx - 2) + CREDIT)
                    act.copy(crep[:, sidx % 2], psC[:]).then_inc(crep_ready, 1)
                    for c in range(CT):
                        t = sidx * CT + c
                        s, i = t % 2, t // 2
                        if sidx == 0:
                            act.wait_ge(dt_ready, CT * blk + c + 1 + CREDIT)
                        act.wait_ge(h_ready[s], UNITS // 2 * blk + i + CREDIT)
                        act.activation(a[:, s], dt_[:, c], ACT.Exp, scale=a_neg[:, c, sidx:sidx + 1])\
                           .then_inc(a_ready[s], 1)
                    for kind, f in sign_unit(sidx):
                        if kind == "l3":
                            continue
                        s, n = full_at(blk, (kind, f))
                        act.wait_ge(full[s], n + CREDIT)
                        dst = f1h if kind == "l1" else f2h
                        act.activation(dst[:, f], psW[s][:], ACT.Relu).then_inc(high_ready, 1)

            with act.Fori(0, BATCH) as b:
                with act.Fori(0, BPB) as q:
                    block_of(b, q)

        @block.vector
        def _(dve):
            c = Chain(dve, wchain)
            dve.wait_ge(weights, 16 * LOADS + CREDIT)
            c.mark(dve.tensor_scalar(sgn[:], scal[:], 0.0, None, ALU.is_ge))
            dve.wait_ge(a_ready0, 1 + CREDIT)
            c.after(dve.tensor_scalar(a_neg[:], a_exp[:], -1.0, None, ALU.mult))
            c.after(dve.tensor_scalar(sgn[:], sgn[:], 2.0, -1.0, ALU.mult, ALU.add))
            c.after(dve.tensor_tensor(mag[:], sgn[:], scal[:], ALU.mult))
            c.mark(dve.tensor_scalar(fac[:, 0:1], mag[:, 0:1], mag[:, 1:2], 64.0, ALU.mult, ALU.mult))
            c.mark(dve.tensor_scalar(fac[:, 2:3], sgn[:, 1:2], 0.25, None, ALU.mult))
            c.after(dve.tensor_scalar(fac[:, 3:4], sgn[:, 1:2], -0.125, None, ALU.mult))
            c.mark(dve.tensor_tensor(fac[:, 1:2], fac[:, 0:1], scal[:, 2:3], ALU.mult))
            c.after(dve.tensor_tensor(kd, k0[:, 0:KD], k0[:, KD:2 * KD], ALU.subtract))
            c.mark(dve.tensor_scalar(w0[:], kd, sgn[:, 0:1], None, ALU.mult))
            c.mark(dve.tensor_scalar(w1[:], k1, fac[:, 2:3], fac[:, 3:4], ALU.mult, ALU.add))
            dve.tensor_scalar(w2[:], k2[:], 2.0, -1.0, ALU.mult, ALU.add).then_inc(w_ready, 1)

            for n, (dst, src) in enumerate(weight_copies()):
                dve.wait_ge(wt_full, n + 1 + CREDIT)
                dve.tensor_copy(dst, src).then_inc(wt_free, 1)

            CH = CT * (NTAP - 1)
            with dve.Fori(0, BATCH) as b:
                dve.wait_ge(conv_done, CT * BPB * b + CREDIT)
                for s in range(2):
                    dve.wait_ge(hc_ready[s], UNITS // 2 * BPB * b + CREDIT)
                dve.memset(state[:], 0.0)
                dve.memset(xc[:, :, 0:HALO], 0.0).then_inc(halo_ready, 1)
                with dve.Fori(0, BPB) as q:
                    blk = b * BPB + q
                    dve.wait_ge(xh_ready, blk + 1 + CREDIT)
                    dve.tensor_tensor(xl[:], xT[:], xh[:], ALU.subtract).then_inc(xl_ready, 1)
                    k = Chain(dve, cchain, CH)
                    k.turn(CH * blk)
                    for c in range(CT):
                        s, n = full_at(blk, ("xz", c))
                        dve.wait_ge(free[s], n + CREDIT)
                        if c == 0:
                            dve.wait_ge(xs_ready, CT * blk + CREDIT)
                        k.after(dve.tensor_scalar(cv[:, c], xc[:, c, 0:BLK], conv_w[:, c, 0:1], None, ALU.mult))
                        for t in range(1, NTAP):
                            ins = dve.scalar_tensor_tensor(out=cv[:, c], in0=xc[:, c, t:t + BLK],
                                                           scalar=conv_w[:, c, t:t + 1], in1=cv[:, c],
                                                           op0=ALU.mult, op1=ALU.add)
                            if t < NTAP - 1:
                                k.after(ins)
                        ins.then_inc(conv_done, 1)
                    k.end()
                    dve.wait_ge(conv_done, CT * blk + CT + CREDIT)
                    dve.tensor_copy(xc[:, :, 0:HALO], xc[:, :, BLK:]).then_inc(halo_ready, 1)
                    for c in range(CT):
                        s, n = full_at(blk, ("dt", c))
                        dve.wait_ge(full[s], n + CREDIT)
                        dve.tensor_scalar(mx[:, c], psW[s][:], vec[:, 1, c:c + 1], 0.0, ALU.add, ALU.max)\
                           .then_inc(mx_ready, 1)
                    dve.wait_ge(ln_ready, blk + 1 + CREDIT)
                    dve.wait_ge(mx_ready, CT * blk + CT + CREDIT)
                    for c in range(CT):
                        dve.tensor_tensor(dt_[:, c], mx[:, c], ab[:, c], ALU.add).then_inc(dt_ready, 1)
                    for c in range(CT):
                        dve.wait_ge(dt_ready, CT * blk + c + 1 + CREDIT)
                        dve.wait_ge(xs_ready, CT * blk + c + 1 + CREDIT)
                        dve.tensor_tensor(dtx[:, c], dt_[:, c], xs[:, c], ALU.mult).then_inc(dtx_ready, 1)
                    dve.wait_ge(dtx_ready, CT * blk + CT + CREDIT)
                    for sidx in range(NS):
                        for c in range(CT):
                            t = sidx * CT + c
                            s, i = t % 2, t // 2
                            n = UNITS // 2 * blk + i
                            if c == 0:
                                dve.wait_ge(b_full, NS * blk + sidx + 1 + CREDIT)
                            dve.wait_ge(h_ready[s], n + CREDIT)
                            dve.tensor_tensor(u[:, s], dtx[:, c], psB[:], ALU.mult).then_inc(u_ready, 1)
                            dve.wait_ge(a_ready[s], n + 1 + CREDIT)
                            dve.wait_ge(hc_ready[s], n + CREDIT)
                            dve.wait_ge(u_ready, UNITS * blk + t + 1 + CREDIT)
                            dve.tensor_tensor_scan(h[:, s], a[:, s], u[:, s], state[:, c, sidx:sidx + 1],
                                                   ALU.mult, ALU.add).then_inc(h_ready[s], 1)
                        for kind, f in sign_unit(sidx):
                            s, n = full_at(blk, (kind, f))
                            if kind == "l3":
                                if f == 0:
                                    dve.wait_ge(x1_in, 16 * blk + 16 + CREDIT)
                                    for e in range(2):
                                        dve.wait_ge(free[e], PER[e] * blk + CREDIT)
                                dve.wait_ge(full[s], n + CREDIT)
                                dve.scalar_tensor_tensor(out=r[:, f], in0=psW[s][:, 0:D], scalar=fac[:, 1:2],
                                                         in1=x1[:, f], op0=ALU.mult, op1=ALU.add).then_inc(free[s], 1)
                                continue
                            dve.wait_ge(high_ready, 2 * FT * blk + (f if kind == "l1" else FT + f) + 1 + CREDIT)
                            hi, lo = (f1h, f1l) if kind == "l1" else (f2h, f2l)
                            dve.scalar_tensor_tensor(out=lo[:, f], in0=psW[s][:], scalar=0.0, in1=hi[:, f],
                                                     op0=ALU.max, op1=ALU.subtract).then_inc(free[s], 1)
                    s, n = full_at(blk, ("l3", TPB - 1))
                    dve.wait_ge(free[s], n + CREDIT)
                    s, n = full_at(blk, ("l3", TPB - 2))
                    dve.wait_ge(free[s], n + CREDIT)
                    for s in range(2):
                        dve.wait_ge(y_added[s], UNITS // 2 * (blk + 1) + CREDIT)
                    for c in range(CT):
                        dve.scalar_tensor_tensor(out=yg[:, c], in0=xs[:, c], scalar=vec[:, 2, c:c + 1], in1=psY[c][:],
                                                 op0=ALU.mult, op1=ALU.add).then_inc(yg_ready, 1)
                    s, n = full_at(blk, ("xz", ET - 1))
                    dve.wait_ge(free[s], n + CREDIT)
                    for c in range(CT):
                        dve.wait_ge(yg_ready, CT * blk + c + 1 + CREDIT)
                        dve.tensor_tensor(ys[:, c], yg[:, c], sz[:, c], ALU.mult).then_inc(ys_ready, 1)
                    dve.wait_ge(out_sent, 16 * blk + CREDIT)
                    for j in range(TPB):
                        s, n = full_at(blk, ("out", j))
                        dve.wait_ge(full[s], n + CREDIT)
                        dve.tensor_tensor(ob[:, j], psW[s][:, 0:D], r[:, j], ALU.add).then_inc(free[s], 1)

        @block.tensor
        def _(pe):
            pe.wait_ge(weights, 16 * LOADS + CREDIT)
            pe.wait_ge(consts, 2 + CREDIT)
            ident = keep["ident"]
            n = [0]

            def bank():
                if n[0] >= 2:
                    pe.wait_ge(wt_free, n[0] - 1 + CREDIT)
                n[0] += 1
                return psW[(n[0] - 1) % 2]

            for k in range(KD):
                for half in range(2):
                    dst = bank()
                    for e in range(4):
                        ins = pe.transpose(dst[:, e * P:(e + 1) * P], w_in[:, half * 4 + e, k * P:(k + 1) * P], ident[:])
                    ins.then_inc(wt_full, 1)
            for c in range(CT):
                dst = bank()
                for k in range(KD):
                    ins = pe.transpose(dst[:, k * P:(k + 1) * P], w_out[:, k, c * P:(c + 1) * P], ident[:])
                ins.then_inc(wt_full, 1)
            for c in range(CT):
                pe.transpose(bank()[:, 0:XD], w_x[:, c * P:(c + 1) * P], ident[0:XD, 0:XD]).then_inc(wt_full, 1)
            dst = bank()
            for c in range(CT):
                ins = pe.transpose(dst[0:RANK, c * P:(c + 1) * P], w_dt[:, c, :], ident[:])
            ins.then_inc(wt_full, 1)
            pe.wait_ge(wt_free, n[0] + CREDIT)
            pe.wait_ge(w_ready, 1 + CREDIT)

            with pe.Fori(0, NBLK) as blk:
                def work(kind):
                    s, turns = full_at(blk, kind)
                    pe.wait_ge(free[s], turns - 1 + CREDIT)
                    return s, psW[s]

                pe.wait_ge(x_in, 16 * blk + 16 + CREDIT)
                for e in range(ET):
                    s, dst = work(("xz", e))
                    for k in range(KD):
                        ins = pe.matmul(dst[:], winT[:, k, e * P:(e + 1) * P], xT[:, k], start=(k == 0), stop=(k == KD - 1))
                    ins.then_inc(full[s], 1)
                s, dst = work(("xd", 0))
                for c in range(CT):
                    pe.wait_ge(xs_ready, CT * blk + c + 1 + CREDIT)
                    ins = pe.matmul(dst[0:XD, :], wxT[:, c], xs[:, c], start=(c == 0), stop=(c == CT - 1))
                ins.then_inc(full[s], 1)
                sx, nx = full_at(blk, ("xd", 0))
                for c in range(CT):
                    s, dst = work(("dt", c))
                    if c == 0:
                        pe.wait_ge(free[sx], nx + CREDIT)
                    pe.matmul(dst[:], wdtT[:, c * P:(c + 1) * P], xd[0:RANK, :], start=True, stop=True).then_inc(full[s], 1)

                def spread(sidx):
                    pe.wait_ge(u_ready, UNITS * blk + CT * sidx + CREDIT)
                    pe.matmul(psB[:], pick[:, sidx], xd[:], start=True, stop=True).then_inc(b_full, 1)
                    pe.wait_ge(crep_ready, NS * blk + sidx + CREDIT)
                    pe.matmul(psC[:], pick[:, NS + sidx], xd[:], start=True, stop=True).then_inc(c_full, 1)

                def sign_products(kind, f):
                    s, dst = work((kind, f))
                    if kind == "l1":
                        if f == 0:
                            pe.wait_ge(xl_ready, blk + 1 + CREDIT)
                        ops = [(w0[:, k, f * P:(f + 1) * P], x[:, k], BLK) for k in range(KD) for x in (xh, xl)]
                    elif kind == "l2":
                        if f == 0:
                            for g in (FT - 2, FT - 1):
                                sl, nl = full_at(blk, ("l1", g))
                                pe.wait_ge(free[sl], nl + CREDIT)
                        ops = [(w1[:, k, f * P:(f + 1) * P], x[:, k], BLK) for k in range(FT) for x in (f1h, f1l)]
                    else:
                        if f == 0:
                            for g in (FT - 2, FT - 1):
                                sl, nl = full_at(blk, ("l2", g))
                                pe.wait_ge(free[sl], nl + CREDIT)
                        ops = [(x[:, k, f * P:(f + 1) * P], w2[:, k], D) for k in range(FT) for x in (f2h, f2l)]
                    for n, (lhs, rhs, w) in enumerate(ops):
                        ins = pe.matmul(dst[:, 0:w], lhs, rhs, start=(n == 0), stop=(n == len(ops) - 1))
                    ins.then_inc(full[s], 1)

                spread(0)
                for sidx in range(NS):
                    for kind, f in sign_unit(sidx):
                        sign_products(kind, f)
                    for c in range(CT):
                        t = sidx * CT + c
                        s, i = t % 2, t // 2
                        if c == CT - 1 and sidx + 1 < NS:
                            spread(sidx + 1)
                        if sidx == 0:
                            pe.wait_ge(yg_ready, CT * blk + CREDIT)
                        pe.wait_ge(hc_ready[s], UNITS // 2 * blk + i + 1 + CREDIT)
                        pe.matmul(psY[c][:], ident[:], hc[:, s], start=(sidx == 0), stop=(sidx == NS - 1),
                                  skip_group_check=True).then_inc(y_added[s], 1)
                for j in range(TPB):
                    s, dst = work(("out", j))
                    for c in range(CT):
                        if j == 0:
                            pe.wait_ge(ys_ready, CT * blk + c + 1 + CREDIT)
                        ins = pe.matmul(dst[:, 0:D], ys[:, c, j * P:(j + 1) * P], woutT[:, c], start=(c == 0),
                                        stop=(c == CT - 1))
                    ins.then_inc(full[s], 1)


def build(nc, io, out):
    with ExitStack() as ctx:
        scratch = lambda name, shape, dt=F32: nc.dram_tensor(name, shape, dt, kind="Internal").ap()
        dram = {
            "xnT": scratch("xnT_d", [KD, P, N]),
            "qk": scratch("qk_d", [2, 3, BATCH, D, T], BF16),
            "ffn": scratch("ffn_d", [N, D]),
            "x1": scratch("x1_d", [N, D]),
            "xn2T": scratch("xn2T_d", [KD, P, N]),
        }
        sb = lambda c, name, shape, dt=F32: c.enter_context(nc.sbuf_tensor(name, shape, dt))
        keep = {
            "ident": sb(ctx, "ident", [P, P]),
            "moe_w": ctx.enter_context(nc.semaphore("moe_w")),
        }
        with ExitStack() as attn:
            keep["v"] = sb(attn, "v_all", [P, BATCH, HEADS, ST_T, VD])
            with ExitStack() as moe:
                keep["c"] = sb(moe, "c_all", [P, NT, E])
                keep["wg"] = sb(moe, "wg", [P, NE, KD, M])
                keep["wu"] = sb(moe, "wu", [P, NE, KD, M])
                keep["wd"] = sb(moe, "wd", [P, NE, M // P, D])
                phase_norm_qkv(nc, io, keep, dram)
                phase_experts(nc, io, keep, dram)
            keep["o"] = sb(attn, "o_all", [P, NH, ST_T, VD])
            phase_attention(nc, io, keep, dram)
            phase_project(nc, io, keep, dram)
        phase_state_space(nc, io, keep, dram, out)


_SHORT = {
    "L0_attn_x": "x", "L0_attn_w_attn": "w_attn", "L0_attn_w_proj": "w_proj", "L0_attn_lambda_q1": "lq1",
    "L0_attn_lambda_q2": "lq2", "L0_attn_lambda_k1": "lk1", "L0_attn_lambda_k2": "lk2", "L0_attn_gamma": "gamma",
    "L0_ffn_gate_w": "gate_w", "L0_ffn_beta": "beta", "L0_ffn_gate_proj_w": "gate_proj", "L0_ffn_up_proj_w": "up_proj",
    "L0_ffn_down_proj_w": "down_proj", "L0_ffn_shared_gate_w": "shared_gate", "L0_ffn_shared_up_w": "shared_up",
    "L0_ffn_shared_down_w": "shared_down", "L1_attn_in_proj_w": "in_proj", "L1_attn_conv_w": "conv_w",
    "L1_attn_conv_b": "conv_b", "L1_attn_x_proj_w": "x_proj", "L1_attn_dt_proj_w": "dt_proj",
    "L1_attn_dt_proj_b": "dt_b", "L1_attn_A_log": "A_log", "L1_attn_D_skip": "D_skip", "L1_attn_out_proj_w": "out_proj",
    "L1_ffn_k0": "k0", "L1_ffn_k1": "k1", "L1_ffn_k2": "k2", "L1_ffn_s0": "s0", "L1_ffn_s1": "s1", "L1_ffn_s2": "s2",
}


def kernel(**inputs):
    import numpy as _np
    import concourse.bacc as _bacc
    from concourse import mybir as _mybir
    from concourse.bass_utils import run_bass_kernel_spmd as _run

    nc = _bacc.Bacc("TRN2", target_bir_lowering=False, num_devices=1)
    arrays, io = {}, {}
    for name, short in _SHORT.items():
        a = _np.ascontiguousarray(inputs[name])
        if a.ndim == 0:
            a = a.reshape(1)
        arrays[f"in_{name}_dram"] = a
        io[short] = nc.dram_tensor(f"in_{name}_dram", a.shape, _mybir.dt.from_np(a.dtype), kind="ExternalInput").ap()
    io["x"] = io["x"].rearrange("b t d -> (b t) d")
    out = nc.dram_tensor("out_0_dram", (BATCH, T, D), _mybir.dt.float32, kind="ExternalOutput").ap()
    build(nc, io, out.rearrange("b t d -> (b t) d"))
    r = _run(nc, [arrays], core_ids=[0])
    return r.results[0]["out_0_dram"]
```

```python
import numpy as np
import concourse.bass as bass
from concourse import mybir
from contextlib import ExitStack

F32 = mybir.dt.float32
BF16 = mybir.dt.bfloat16
F16 = mybir.dt.float16
U32 = mybir.dt.uint32
U8 = mybir.dt.uint8
ACT = mybir.ActivationFunctionType
ALU = mybir.AluOpType
AX = mybir.AxisListType

P = 128
BATCH, T, D = 2, 2048, 256
N = BATCH * T
BLK = 512
NBLK = N // BLK
BPB = T // BLK
TPB = BLK // P
NT = N // P
KD = D // P
HEADS, HD = 16, 8
VD = 2 * HD
E, M = 8, 512
NE = E + 1
EPS = 1e-5
CREDIT = 1
LAMBDA_INIT = 0.2
NEG = -1e30

ST_T = T // P
NH = BATCH * HEADS
KQ = 9 * HD
VW = 32
OC = VD + 1

DI = 512
CT = DI // P
NS = 16
NTAP = 4
RANK = 16
F1 = 1024


I32 = mybir.dt.int32
REG = N + P
RT = (2 * N + E * (P - 1)) // P + 1
RT -= RT * P > 2 * N + E * (P - 1)
RT += (NT + RT) % 2
TT = NT + RT


def credited(ctx, nc, sems, name):
    sems.append(ctx.enter_context(nc.semaphore(name)))
    return sems[-1]


class Chain:

    def __init__(self, eng, sem, per_turn=0):
        self.eng, self.sem, self.per, self.n, self.base = eng, sem, per_turn, 0, 0

    def turn(self, base):
        self.base, self.n = base, 0

    def mark(self, ins):
        ins.then_inc(self.sem, 1)
        self.n += 1

    def wait(self):
        self.eng.wait_ge(self.sem, self.base + self.n + CREDIT)

    def after(self, ins):
        self.mark(ins)
        self.wait()

    def end(self):
        assert self.n == self.per, (self.n, self.per)


def phase_norm_qkv(nc, io, keep, dram):
    with ExitStack() as ctx:
        sb = lambda name, shape, dt=F32: ctx.enter_context(nc.sbuf_tensor(name, shape, dt))
        ps = lambda name, shape, dt=F32: ctx.enter_context(nc.psum_tensor(name, shape, dt))
        sems = []
        sem = lambda name: credited(ctx, nc, sems, name)

        wqkv = sb("wqkv", [P, KD, 3 * D])
        gate_rows = sb("gate_rows", [E, D])
        gateT = sb("gateT", [P, KD, E])
        beta = sb("beta", [P, E])
        iota_u = sb("iota_u", [P, E + NT + TT], I32)
        iota_f = sb("iota_f", [P, E + NT + TT])
        iota_e = iota_f[:, 0:E]
        iota_m = iota_f[:, E:E + NT]
        iota_t = iota_f[:, E + NT:]
        region = sb("region", [P, E])
        before = sb("before", [P, P])
        ones = sb("ones", [P, P])
        zeros = sb("zeros", [P, D])
        x = sb("x", [P, TPB, D])
        stats = sb("stats", [P, TPB, 6])
        mv = sb("mv", [P, TPB, 2])
        std = sb("std", [P, TPB])
        rstd = sb("rstd", [P, TPB])
        xn = sb("xn", [P, TPB, D])
        xnT = sb("xnT", [P, KD, BLK])
        qf = sb("qf", [P, 2, BLK])
        rest = sb("rest", [P, 2, BLK])
        parts = sb("parts", [P, 2, 3, BLK], BF16)
        sel = sb("sel", [P, TPB, E])
        top = sb("top", [P, TPB, E])
        topi = sb("topi", [P, TPB, E], U32)
        topf = sb("topf", [P, TPB, E])
        hot = sb("hot", [P, 2, TPB, E])
        both = sb("both", [P, TPB, E])
        seen = sb("seen", [P, TPB + 1, E])
        sig = sb("sig", [P, TPB, E])
        place = sb("place", [P, TPB, E])
        pick = sb("picks", [P, 2, 2, TPB, E])
        picked = sb("picked", [P, 2, 2, TPB])
        slot = sb("slot", [P, 2, TPB], I32)
        count = sb("count", [P, E])
        wide = sb("wide", [P, E, RT])
        wide2 = sb("wide2", [P, E, RT])
        tiles = sb("tiles", [P, E])
        ends = sb("ends", [P, E])
        starts = sb("starts", [P, E])
        shift = sb("shift", [P, E])
        tail_f = sb("tail_f", [P, E])
        tail = sb("tail", [P, E], I32)
        table_f = sb("table_f", [P, 2, TT])
        yslot_f = sb("yslot_f", [P, NT * 2])
        yshift = sb("yshift", [P, NT * 2])
        pcarry = sb("pcarry", [P, 2])
        carrier = sb("carrier", [P, 4])

        psT = ps("psT", [P, KD, BLK])
        psQ = ps("psQ", [P, 2, BLK])
        psV = ps("psV", [P, TPB, D])
        psL = ps("psL", [P, TPB, E])
        psK = ps("psK", [P, TPB, E])

        w_in = sem("a_w_in")
        x_in = sem("a_x_in")
        x_free = sem("a_x_free")
        stats_ready = sem("a_stats_ready")
        std_ready = sem("a_std_ready")
        xT_done = sem("a_xT_done")
        xnT_ready = sem("a_xnT_ready")
        xn_out = sem("a_xn_out")
        scattered = ctx.enter_context(nc.semaphore("a_scattered"))
        scatter_free = sem("a_scatter_free")
        both_ready = sem("a_both_ready")
        ranked = sem("a_ranked")
        slot_ready = sem("a_slot_ready")
        consts = sem("a_consts")
        tail_ready = sem("a_tail_ready")
        tail_out = sem("a_tail_out")
        gate_t = sem("a_gate_t")
        gateT_ready = sem("a_gateT_ready")
        qk_done = sem("a_qk_done")
        qf_ready = [sem(f"a_qf_ready{s}") for s in range(2)]
        parts_ready = [sem(f"a_parts_ready{s}") for s in range(2)]
        parts_out = [sem(f"a_parts_out{s}") for s in range(2)]
        v_done = sem("a_v_done")
        v_free = sem("a_v_free")
        l_done = sem("a_l_done")
        sig_ready = sem("a_sig_ready")
        dchain = sem("a_dchain")
        pchain = sem("a_pchain")
        iota_ready = sem("a_iota_ready")

        block = ctx.enter_context(nc.Block())
        CH = 52

        @block.sync
        def _(sp):
            for s in sems:
                sp.sem_inc(s, CREDIT)
            sp.dma_start(wqkv[:], io["w_attn"].rearrange("(k p) n -> p k n", p=P)).then_inc(w_in, 16)
            sp.dma_start(gate_rows[:], io["gate_w"]).then_inc(w_in, 16)
            sp.dma_start(beta[:], io["beta"].partition_broadcast(P)).then_inc(w_in, 16)
            x_blk = io["x"].rearrange("(n j p) d -> n p j d", p=P, j=TPB)
            sp.dma_start(x[:], x_blk[0]).then_inc(x_in, 16)

            def stores(b, q):
                blk = b * BPB + q
                for f in range(4):
                    sp.wait_ge(parts_ready[f % 2], 2 * blk + f // 2 + 1 + CREDIT)
                    maps = slice(f % 2 * HEADS, (f % 2 + 1) * HEADS)
                    if f < 2:
                        for x in range(3):
                            sp.dma_start(dram["q"][b, maps, x, :, bass.ds(q * BLK, BLK)], parts[:, f % 2, x])\
                              .then_inc(parts_out[f % 2], 16)
                    else:
                        sp.dma_start(dram["k"][b, maps, :, :, bass.ds(q * BLK, BLK)]
                                     .rearrange("n d x t -> (n d) x t"), parts[:, f % 2]).then_inc(parts_out[f % 2], 16)

            with sp.Fori(0, BATCH) as b:
                with sp.Fori(0, BPB) as q:
                    blk = b * BPB + q
                    sp.wait_ge(x_free, blk + 1 + CREDIT)
                    sp.dma_start(dram["rows"][bass.ds(blk * BLK + E * REG, BLK), :]
                                 .rearrange("(j p) d -> p j d", p=P), xn[:]).then_inc(xn_out, 16)
                    sp.dma_start(x[:], io["x"][bass.ds((blk + 1) % NBLK * BLK, BLK), :]
                                 .rearrange("(j p) d -> p j d", p=P)).then_inc(x_in, 16)
                    stores(b, q)
            sp.wait_ge(x_in, 16 * NBLK + 16 + CREDIT)
            for s in range(2):
                sp.wait_ge(parts_out[s], 64 * NBLK + CREDIT)
            sp.wait_ge(xn_out, 16 * NBLK + CREDIT)
            sp.wait_ge(tail_ready, 1 + CREDIT)
            for e in range(E):
                row = sp.value_load(tail[0:1, e:e + 1], min_val=e * REG, max_val=e * REG + N)
                sp.dma_start(dram["rows"][bass.ds(row, P), :], zeros[:]).then_inc(tail_out, 16)
            sp.wait_ge(tail_out, 16 * E + CREDIT)

        @block.gpsimd
        def _(pool):
            c = Chain(pool, pchain)
            c.after(pool.memset(keep["ident"][:], 0.0))
            c.after(pool.affine_select(out=keep["ident"][:], in_=keep["ident"][:], compare_op=ALU.not_equal, fill=1.0,
                                       base=0, pattern=[[-1, P]], channel_multiplier=1))
            c.mark(pool.iota(iota_u[:, 0:E], pattern=[[1, E]], base=0, channel_multiplier=0))
            c.mark(pool.iota(iota_u[:, E:E + NT], pattern=[[P, NT]], base=0, channel_multiplier=0))
            c.mark(pool.iota(iota_u[:, E + NT:], pattern=[[1, TT]], base=0, channel_multiplier=0))
            c.wait()
            pool.tensor_copy(iota_f[:], iota_u[:]).then_inc(iota_ready, 1)
            c.mark(pool.memset(zeros[:], 0.0))
            c.mark(pool.memset(pcarry[:], 0.0))
            c.mark(pool.memset(before[:], 1.0))
            c.after(pool.memset(ones[:], 1.0))
            pool.affine_select(out=before[:], in_=before[:], compare_op=ALU.is_gt, fill=0.0, base=0,
                               pattern=[[1, P]], channel_multiplier=-1).then_inc(consts, 1)
            with pool.Fori(0, NBLK) as blk:
                pool.wait_ge(slot_ready, blk + 1 + CREDIT)
                pool.tensor_tensor(pcarry[:, 0:1], pcarry[:, 0:1], pcarry[:, 0:1], ALU.mult)
                for k in range(2):
                    for j in range(TPB):
                        pool.indirect_dma_start(dram["rows"], bass.IndirectOffsetOnAxis(slot[:, k, j:j + 1], 0),
                                                xn[:, j, :], None).then_inc(scattered, 16)
                pool.wait_ge(scattered, 16 * 2 * TPB * (blk + 1))
                pool.tensor_tensor(pcarry[:, 1:2], pcarry[:, 1:2], pcarry[:, 1:2], ALU.mult).then_inc(scatter_free, 1)

        @block.vector
        def _(dve):
            c = Chain(dve, dchain, CH)
            dve.wait_ge(iota_ready, 1 + CREDIT)
            dve.wait_ge(w_in, 48 + CREDIT)
            c.mark(dve.tensor_scalar(region[:], iota_e, float(REG), None, ALU.mult))
            c.after(dve.memset(seen[:], 0.0))
            with dve.Fori(0, NBLK) as blk:
                c.turn(2 + blk * CH)
                dve.wait_ge(x_in, 16 * blk + 16 + CREDIT)
                for j in range(TPB):
                    c.mark(dve.bn_stats(stats[:, j, :], x[:, j, :]))
                c.wait()
                c.mark(dve.memset(carrier[:, 0:1], 0.0))
                for j in range(TPB):
                    c.mark(dve.bn_aggr(mv[:, j, :], stats[:, j, :]))
                c.wait()
                dve.tensor_scalar(rstd[:], mv[:, :, 1], EPS, None, ALU.add).then_inc(stats_ready, 1)
                dve.wait_ge(std_ready, blk + 1 + CREDIT)
                c.after(dve.reciprocal(rstd[:], std[:]))
                dve.wait_ge(xT_done, blk + CREDIT)
                dve.wait_ge(xn_out, 16 * blk + CREDIT)
                dve.wait_ge(scatter_free, blk + CREDIT)
                for j in range(TPB):
                    ins = dve.tensor_scalar(xn[:, j, :], x[:, j, :], mv[:, j, 0:1], rstd[:, j:j + 1],
                                            ALU.subtract, ALU.mult)
                ins.then_inc(x_free, 1)
                dve.wait_ge(l_done, blk + 1 + CREDIT)
                dve.wait_ge(sig_ready, blk + 1 + CREDIT)
                dve.wait_ge(x_free, blk + 1 + CREDIT)
                c.after(dve.tensor_tensor(sel[:], psL[:], beta[:].unsqueeze(1).to_broadcast([P, TPB, E]), ALU.add))
                c.mark(dve.memset(carrier[:, 1:2], 0.0))
                for j in range(TPB):
                    c.mark(dve.max(top[:, j, :], sel[:, j, :]))
                c.wait()
                c.mark(dve.memset(carrier[:, 2:3], 0.0))
                for j in range(TPB):
                    c.mark(dve.max_index(topi[:, j, :], top[:, j, :], sel[:, j, :]))
                c.wait()
                c.after(dve.tensor_copy(topf[:], topi[:]))
                c.mark(dve.tensor_copy(seen[:, 0], seen[:, TPB]))
                for k in range(2):
                    c.mark(dve.tensor_tensor(hot[:, k], iota_e.unsqueeze(1).to_broadcast([P, TPB, E]),
                                             topf[:, :, k:k + 1].to_broadcast([P, TPB, E]), ALU.is_equal))
                c.wait()
                c.mark(dve.tensor_copy(keep["hot"][:, bass.ds(blk, 1)].rearrange("p o k j e -> p (o k j e)"),
                                       hot[:].rearrange("p k j e -> p (k j e)")))
                c.after(dve.tensor_tensor(both[:], hot[:, 0], hot[:, 1], ALU.add))
                for j in range(TPB):
                    ins = dve.tensor_tensor(seen[:, j + 1], seen[:, j], both[:, j], ALU.add)
                    if j < TPB - 1:
                        c.after(ins)
                ins.then_inc(both_ready, 1)

                def cut(f):
                    s = f % 2
                    dve.wait_ge(qf_ready[s], 2 * blk + f // 2 + 1 + CREDIT)
                    dve.wait_ge(parts_out[s], 64 * blk + f // 2 * 48 + CREDIT)
                    c.after(dve.tensor_copy(parts[:, s, 0], qf[:, s]))
                    c.after(dve.tensor_tensor(rest[:, 0], qf[:, s], parts[:, s, 0], ALU.subtract))
                    c.after(dve.tensor_copy(parts[:, s, 1], rest[:, 0]))
                    c.after(dve.tensor_tensor(rest[:, 1], rest[:, 0], parts[:, s, 1], ALU.subtract))
                    dve.tensor_copy(parts[:, s, 2], rest[:, 1]).then_inc(parts_ready[s], 1)

                cut(0)
                dve.wait_ge(ranked, blk + 1 + CREDIT)
                c.after(dve.tensor_tensor(place[:], psK[:], region[:].unsqueeze(1).to_broadcast([P, TPB, E]), ALU.add))
                for w, src in enumerate((place, sig)):
                    c.mark(dve.tensor_tensor(pick[:, w].rearrange("p k j e -> p k (j e)"),
                                             hot[:].rearrange("p k j e -> p k (j e)"),
                                             src[:].rearrange("p j e -> p (j e)").unsqueeze(1)
                                             .to_broadcast([P, 2, TPB * E]), ALU.mult))
                c.wait()
                c.after(dve.tensor_reduce(picked[:].rearrange("p w k j -> p (w k j)"),
                                          pick[:].rearrange("p w k j e -> p (w k j) e"), AX.X, ALU.add))
                c.mark(dve.tensor_copy(keep["slot"][:, bass.ds(blk, 1), :], picked[:, 0].rearrange("p k j -> p (k j)")
                                       .unsqueeze(1)))
                c.mark(dve.tensor_copy(keep["c"][:, bass.ds(blk, 1), :], picked[:, 1].rearrange("p k j -> p (k j)")
                                       .unsqueeze(1)))
                dve.wait_ge(scatter_free, blk + CREDIT)
                dve.tensor_copy(slot[:], picked[:, 0]).then_inc(slot_ready, 1)
                dve.wait_ge(slot_ready, blk + 1 + CREDIT)
                cut(1)
                cut(2)
                cut(3)
                c.end()


            c.turn(2 + NBLK * CH)
            dve.wait_ge(ranked, NBLK + 1 + CREDIT)
            c.after(dve.tensor_copy(count[:], psK[:, 0]))
            c.mark(dve.tensor_tensor(tail_f[:], count[:], region[:], ALU.add))
            c.mark(dve.tensor_tensor(wide[:, :, 0:NT], count[:].unsqueeze(2).to_broadcast([P, E, NT]),
                                     iota_m.unsqueeze(1).to_broadcast([P, E, NT]), ALU.is_gt))
            c.wait()
            dve.tensor_copy(tail[:], tail_f[:]).then_inc(tail_ready, 1)
            c.after(dve.tensor_reduce(tiles[:], wide[:, :, 0:NT], AX.X, ALU.add))
            c.after(dve.tensor_tensor(wide[:, :, 0:E], iota_e.unsqueeze(1).to_broadcast([P, E, E]),
                                      iota_e.unsqueeze(2).to_broadcast([P, E, E]), ALU.is_le))
            c.after(dve.tensor_tensor(wide2[:, :, 0:E], wide[:, :, 0:E], tiles[:].unsqueeze(1).to_broadcast([P, E, E]),
                                      ALU.mult))
            c.after(dve.tensor_reduce(ends[:], wide2[:, :, 0:E], AX.X, ALU.add))
            c.after(dve.tensor_tensor(starts[:], ends[:], tiles[:], ALU.subtract))
            c.after(dve.scalar_tensor_tensor(out=shift[:], in0=starts[:], scalar=-float(P), in1=region[:],
                                             op0=ALU.mult, op1=ALU.add))
            routed = iota_t[:, 0:RT].unsqueeze(1).to_broadcast([P, E, RT])
            c.mark(dve.tensor_tensor(wide[:], routed, starts[:].unsqueeze(2).to_broadcast([P, E, RT]), ALU.is_ge))
            c.mark(dve.tensor_tensor(wide2[:], routed, ends[:].unsqueeze(2).to_broadcast([P, E, RT]), ALU.is_lt))
            c.wait()
            c.after(dve.tensor_tensor(wide[:], wide[:], wide2[:], ALU.mult))
            c.after(dve.tensor_tensor(wide2[:], wide[:], iota_e.unsqueeze(2).to_broadcast([P, E, RT]), ALU.mult))
            c.after(dve.tensor_reduce(table_f[:, 0, NT:TT], wide2[:].rearrange("p e t -> p t e"), AX.X, ALU.add))
            c.after(dve.scalar_tensor_tensor(out=wide2[:], in0=routed, scalar=float(P),
                                             in1=shift[:].unsqueeze(2).to_broadcast([P, E, RT]),
                                             op0=ALU.mult, op1=ALU.add))
            c.after(dve.tensor_tensor(wide2[:], wide[:], wide2[:], ALU.mult))
            c.mark(dve.tensor_reduce(table_f[:, 1, NT:TT], wide2[:].rearrange("p e t -> p t e"), AX.X, ALU.add))
            c.mark(dve.memset(table_f[:, 0, 0:NT], float(E)))
            c.mark(dve.tensor_scalar(table_f[:, 1, 0:NT], iota_m, float(E * REG), None, ALU.add))
            c.wait()
            c.mark(dve.tensor_copy(keep["table"][:], table_f[:]))
            pickall = keep["hot"][:].rearrange("p b k j e -> p (b k j) e")
            c.after(dve.tensor_tensor(keep["hot"][:].rearrange("p b k j e -> p (b k j) e"), pickall,
                                      shift[:].unsqueeze(1).to_broadcast([P, 2 * NT, E]), ALU.mult))
            c.after(dve.tensor_reduce(yshift[:], pickall, AX.X, ALU.add))
            c.after(dve.tensor_tensor(yslot_f[:], keep["slot"][:].rearrange("p b k -> p (b k)"), yshift[:],
                                      ALU.subtract))
            c.after(dve.tensor_scalar(keep["yslot"][:].rearrange("p b k -> p (b k)"), yslot_f[:], float(N), None,
                                      ALU.add))

        @block.scalar
        def _(act):
            for e in range(NE):
                g = io["gate_proj"][e] if e < E else io["shared_gate"][0]
                u = io["up_proj"][e] if e < E else io["shared_up"][0]
                d = io["down_proj"][e] if e < E else io["shared_down"][0]
                act.dma_start(keep["wg"][:, e], g.rearrange("(k p) m -> p k m", p=P)).then_inc(keep["moe_w"], 16)
                act.dma_start(keep["wu"][:, e], u.rearrange("(k p) m -> p k m", p=P)).then_inc(keep["moe_w"], 16)
                act.dma_start(keep["wd"][:, e], d.rearrange("(k p) m -> p k m", p=P)).then_inc(keep["moe_w"], 16)
            act.wait_ge(gate_t, 1 + CREDIT)
            act.copy(gateT[:].rearrange("p k e -> p (k e)"), psL[:, 0:KD, :].rearrange("p k e -> p (k e)"))\
               .then_inc(gateT_ready, 1)
            with act.Fori(0, BATCH) as b:
                with act.Fori(0, BPB) as q:
                    blk = b * BPB + q
                    act.wait_ge(stats_ready, blk + 1 + CREDIT)
                    act.activation(std[:], rstd[:], ACT.Sqrt).then_inc(std_ready, 1)
                    act.wait_ge(xT_done, blk + 1 + CREDIT)
                    act.wait_ge(v_done, blk + CREDIT)
                    act.wait_ge(l_done, blk + CREDIT)
                    for k in range(KD):
                        ins = act.copy(xnT[:, k], psT[:, k])
                    ins.then_inc(xnT_ready, 1)
                    act.wait_ge(l_done, blk + 1 + CREDIT)
                    act.wait_ge(slot_ready, blk + CREDIT)
                    act.activation(sig[:], psL[:], ACT.Sigmoid).then_inc(sig_ready, 1)
                    for f in range(4):
                        s = f % 2
                        act.wait_ge(qk_done, 4 * blk + f + 1 + CREDIT)
                        act.wait_ge(parts_ready[s], 2 * blk + f // 2 + CREDIT)
                        act.activation(qf[:, s], psQ[:, s], ACT.Copy, scale=(1.0 / HD if f < 2 else 1.0))\
                           .then_inc(qf_ready[s], 1)
                    act.wait_ge(v_done, blk + 1 + CREDIT)
                    act.copy(keep["v"][:, b, :, bass.ds(q * TPB, TPB), :].rearrange("p h j d -> p j h d"),
                             psV[:].rearrange("p j (h d) -> p j h d", h=HEADS)).then_inc(v_free, 1)

        @block.tensor
        def _(pe):
            pe.wait_ge(w_in, 48 + CREDIT)
            pe.wait_ge(consts, 1 + CREDIT)
            for k in range(KD):
                ins = pe.transpose(psL[:, k, :], gate_rows[:, k * P:(k + 1) * P], keep["ident"][0:E, 0:E])
            ins.then_inc(gate_t, 1)
            pe.wait_ge(gateT_ready, 1 + CREDIT)
            with pe.Fori(0, NBLK) as blk:
                pe.wait_ge(x_free, blk + 1 + CREDIT)
                pe.wait_ge(xnT_ready, blk + CREDIT)
                for j in range(TPB):
                    for k in range(KD):
                        ins = pe.transpose(psT[:, k, j * P:(j + 1) * P], xn[:, j, k * P:(k + 1) * P], keep["ident"][:])
                ins.then_inc(xT_done, 1)
                pe.wait_ge(xnT_ready, blk + 1 + CREDIT)
                pe.wait_ge(both_ready, blk + CREDIT)
                for j in range(TPB):
                    for k in range(KD):
                        ins = pe.matmul(psL[:, j], xnT[:, k, j * P:(j + 1) * P], gateT[:, k],
                                        start=(k == 0), stop=(k == KD - 1))
                ins.then_inc(l_done, 1)

                def qk(f):
                    s = f % 2
                    pe.wait_ge(qf_ready[s], 2 * blk + f // 2 + CREDIT)
                    for k in range(KD):
                        ins = pe.matmul(psQ[:, s], wqkv[:, k, f * P:(f + 1) * P], xnT[:, k],
                                        start=(k == 0), stop=(k == KD - 1))
                    ins.then_inc(qk_done, 1)

                qk(0)
                qk(1)
                pe.wait_ge(both_ready, blk + 1 + CREDIT)
                pe.wait_ge(slot_ready, blk + CREDIT)
                pe.matmul(psK[:].rearrange("p j e -> p (j e)"), before[:], both[:].rearrange("p j e -> p (j e)"),
                          start=True, stop=False)
                pe.matmul(psK[:].rearrange("p j e -> p (j e)"), ones[:],
                          seen[:, 0:TPB].rearrange("p j e -> p (j e)"), start=False, stop=True).then_inc(ranked, 1)
                qk(2)
                qk(3)
                pe.wait_ge(v_free, blk + CREDIT)
                for j in range(TPB):
                    for k in range(KD):
                        ins = pe.matmul(psV[:, j], xnT[:, k, j * P:(j + 1) * P], wqkv[:, k, 2 * D:3 * D],
                                        start=(k == 0), stop=(k == KD - 1))
                ins.then_inc(v_done, 1)
            pe.wait_ge(slot_ready, NBLK + CREDIT)
            pe.matmul(psK[:, 0], ones[:], seen[:, TPB], start=True, stop=True).then_inc(ranked, 1)


def phase_experts(nc, io, keep, dram):
    with ExitStack() as ctx:
        sb = lambda name, shape, dt=F32: ctx.enter_context(nc.sbuf_tensor(name, shape, dt))
        ps = lambda name, shape, dt=F32: ctx.enter_context(nc.psum_tensor(name, shape, dt))
        sems = []
        sem = lambda name: credited(ctx, nc, sems, name)
        MT = M // P

        x = sb("x_e", [P, 2, D])
        xT = sb("xT_e", [P, 2, KD, P])
        sg = sb("sg", [P, 2, M])
        h = sb("h", [P, 2, M])
        hT = sb("hT", [P, 2, MT, P])
        y = sb("y", [P, 2, D])
        psG = ps("psG", [P, 2, M])
        psU = ps("psU", [P, 2, M])
        psH = ps("psH", [P, 2, MT, P])
        psX = ps("psX", [P, KD, P])
        psY = ps("psY", [P, D])

        x_in = [sem(f"m_x_in{s}") for s in range(2)]
        x_turned = sem("m_x_turned")
        xT_ready = sem("m_xT_ready")
        gu_done, sg_ready, h_ready = sem("m_gu_done"), sem("m_sg_ready"), sem("m_h_ready")
        h_turned, hT_ready = sem("m_h_turned"), sem("m_hT_ready")
        d_done, y_ready = sem("m_d_done"), sem("m_y_ready")
        y_out = [sem(f"m_y_out{s}") for s in range(2)]
        block = ctx.enter_context(nc.Block())

        def steps(eng, step, first, last):
            lo, hi = 4, TT - 2
            for i in range(first, lo):
                step(i, i % 2)
            with eng.Fori(0, (hi - lo) // 2) as j:
                for s in range(2):
                    step(2 * j + lo + s, s)
            for i in range(hi, last + 1):
                step(i, i % 2)

        def known(i, lo, hi=TT):
            return not isinstance(i, int) or lo <= i < hi

        def at(table, i):
            return table[:, i:i + 1] if isinstance(i, int) else table[:, bass.ds(i, 1)]

        def half(i, s):
            return (i - s) // 2

        @block.sync
        def _(sp):
            for s in sems:
                sp.sem_inc(s, CREDIT)
            def load(i, s):
                row = sp.value_load(at(keep["table"][0:1, 1], i), min_val=0, max_val=E * REG + N - P)
                if known(i, 2):
                    sp.wait_ge(x_turned, i - 1 + CREDIT)
                sp.dma_start(x[:, s], dram["rows"][bass.ds(row, P), :]).then_inc(x_in[s], 16)

            def store(i, s):
                sp.wait_ge(y_ready, i + 1 + CREDIT)
                rows = slice(i * P, (i + 1) * P) if isinstance(i, int) else bass.ds(i * P, P)
                sp.dma_start(dram["y"][rows, :], y[:, s]).then_inc(y_out[s], 16)

            def step(i, s):
                if known(i + 1, 0):
                    load(i + 1, 1 - s)
                if known(i - 4, 0):
                    store(i - 4, s)
            steps(sp, step, -1, TT + 3)
            for s in range(2):
                sp.wait_ge(y_out[s], 16 * (TT // 2) + CREDIT)

        @block.scalar
        def _(act):
            def step(i, s):
                if known(i, 0):
                    act.wait_ge(gu_done, i + 1 + CREDIT)
                    if known(i, 2):
                        act.wait_ge(h_ready, i - 1 + CREDIT)
                    act.activation(sg[:, s], psG[:, s], ACT.Silu).then_inc(sg_ready, 1)
                if known(i - 1, 0):
                    act.wait_ge(h_turned, i + CREDIT)
                    if known(i - 1, 2):
                        act.wait_ge(d_done, i - 2 + CREDIT)
                    act.copy(hT[:, 1 - s].rearrange("p m t -> p (m t)"), psH[:, 1 - s].rearrange("p m t -> p (m t)"))\
                       .then_inc(hT_ready, 1)
            steps(act, step, 0, TT)

        @block.vector
        def _(dve):
            def step(i, s):
                if known(i + 1, 0):
                    dve.wait_ge(x_turned, i + 2 + CREDIT)
                    if known(i + 1, 2):
                        dve.wait_ge(gu_done, i + CREDIT)
                    dve.tensor_copy(xT[:, 1 - s], psX[:]).then_inc(xT_ready, 1)
                if known(i, 0):
                    dve.wait_ge(sg_ready, i + 1 + CREDIT)
                    if known(i, 2):
                        dve.wait_ge(h_turned, i - 1 + CREDIT)
                    dve.tensor_tensor(h[:, s], sg[:, s], psU[:, s], ALU.mult).then_inc(h_ready, 1)
                if known(i - 2, 0):
                    dve.wait_ge(d_done, i - 1 + CREDIT)
                    if known(i - 2, 2):
                        dve.wait_ge(y_out[s], 16 * half(i - 2, s) + CREDIT)
                    dve.tensor_copy(y[:, s], psY[:]).then_inc(y_ready, 1)
            steps(dve, step, -1, TT + 1)

        @block.tensor
        def _(pe):
            pe.wait_ge(keep["moe_w"], 16 * 3 * NE)

            def turn_x(i, s):
                pe.wait_ge(x_in[s], 16 * half(i, s) + 16 + CREDIT)
                if known(i, 1):
                    pe.wait_ge(xT_ready, i + CREDIT)
                for k in range(KD):
                    ins = pe.transpose(psX[:, k], x[:, s, k * P:(k + 1) * P], keep["ident"][:])
                ins.then_inc(x_turned, 1)

            def step(i, s):
                if known(i, 0):
                    e = pe.value_load(at(keep["table"][0:1, 0], i), min_val=0, max_val=E)
                    pe.wait_ge(xT_ready, i + 1 + CREDIT)
                    if known(i, 2):
                        pe.wait_ge(h_ready, i - 1 + CREDIT)
                    for w, dst in ((keep["wg"], psG), (keep["wu"], psU)):
                        for k in range(KD):
                            ins = pe.matmul(dst[:, s], xT[:, s, k], w[:, bass.ds(e, 1), k].rearrange("p o m -> p (o m)"),
                                            start=(k == 0), stop=(k == KD - 1))
                    ins.then_inc(gu_done, 1)
                if known(i + 1, 0):
                    turn_x(i + 1, 1 - s)
                if known(i - 2, 0):
                    e = pe.value_load(at(keep["table"][0:1, 0], i - 2), min_val=0, max_val=E)
                    pe.wait_ge(hT_ready, i - 1 + CREDIT)
                    if known(i - 2, 1):
                        pe.wait_ge(y_ready, i - 2 + CREDIT)
                    for m in range(MT):
                        ins = pe.matmul(psY[:], hT[:, s, m], keep["wd"][:, bass.ds(e, 1), m].rearrange("p o d -> p (o d)"),
                                        start=(m == 0), stop=(m == MT - 1))
                    ins.then_inc(d_done, 1)
                if known(i - 1, 0):
                    pe.wait_ge(h_ready, i + CREDIT)
                    if known(i - 1, 2):
                        pe.wait_ge(hT_ready, i - 2 + CREDIT)
                    for m in range(MT):
                        ins = pe.transpose(psH[:, 1 - s, m], h[:, 1 - s, m * P:(m + 1) * P], keep["ident"][:])
                    ins.then_inc(h_turned, 1)
            steps(pe, step, -1, TT + 1)


def score_steps():
    out = []
    for c in range(BPB):
        for st in range(TPB * c + TPB):
            r = st - TPB * c
            first = c == 0 and st == 1
            out.append((c, st, 0 if r < 0 or first else P * r, first))
    return out


def max_units():
    return [(a, i, ch, min(BLK, P * (i + 1) - BLK * ch))
            for a in range(2) for i in range(ST_T) for ch in range(i // TPB + 1)]


def phase_attention(nc, io, keep, dram):
    with ExitStack() as ctx:
        sb = lambda name, shape, dt=F32: ctx.enter_context(nc.sbuf_tensor(name, shape, dt))
        ps = lambda name, shape, dt=F32: ctx.enter_context(nc.psum_tensor(name, shape, dt))
        sems = []
        sem = lambda name: credited(ctx, nc, sems, name)

        STEPS, UNITS = score_steps(), max_units()
        NSTEP, NUNIT = len(STEPS), len(UNITS)
        SLOTS = 4
        assert NSTEP % SLOTS == 0
        LAST = [max(k for k, s in enumerate(STEPS) if s[0] == c) for c in range(BPB)]
        FIRST_U, LAST_U = 1, 36
        RING_CUTS = ((1, 2), (0, 1))
        ISSUE = 400
        LAG = 2
        EVAC = LAG + 1
        K_MAX, MROW = 96, 96
        RING_HEAD = NUNIT + 1 + BPB

        kslabs = sb("kslabs", [P, 2, 2, T], BF16)
        qslabs = sb("qslabs", [P, 2, 2, T], BF16)
        kslab = [[kslabs[:, u, a] for a in range(2)] for u in range(2)]
        qslab = [[qslabs[:, u, a] for a in range(2)] for u in range(2)]
        vaug = [sb(f"vaug{u}", [P, ST_T, VW]) for u in range(2)]
        prob = [sb(f"prob{s}", [P, 2, BLK]) for s in range(SLOTS)]
        pmax = sb("pmax", [P, 2 * ST_T, BPB])
        nmax = sb("nmax", [P, 2 * ST_T])
        mrest = sb("mrest", [2 * ST_T, 2, P])
        mpart = sb("mpart", [2 * ST_T, 3, P], BF16)
        ident_b = sb("ident_b", [P, P], BF16)
        mask_q = sb("mask_q", [P, P], BF16)
        mask_k = sb("mask_k", [P, 2 * P], BF16)
        fold = sb("fold", [P, 2, OC])
        ov = [sb(f"ov{s}", [P, BLK]) for s in range(2)]
        o = sb("o_head", [P, ST_T, 2, OC])
        rs = sb("rs", [P, ST_T, 2])
        rl = sb("rl", [P, ST_T])
        o1 = sb("o1", [P, ST_T, VD])
        o2 = sb("o2", [P, ST_T, VD])
        lam_in = sb("lam_in", [P, 4, HD])
        lam_w = sb("lam_w", [P, 2, HD])
        lam_s = sb("lam_s", [P, 2])
        lam_e = sb("lam_e", [P, 2])
        lam = sb("lam", [P, 2])

        psS = [ps(f"psS{s}", [P, 2, BLK]) for s in range(2)]
        psR = [ps(f"psR{s}", [P, BLK]) for s in range(2)]
        psV = [ps(f"psVo{s}", [P, BLK]) for s in range(2)]

        lam_load = sem("b_lam_load")
        lam_step = sem("b_lam_step")
        lam_exp = sem("b_lam_exp")
        lam_ready = sem("b_lam_ready")
        masks = sem("b_masks")
        slab_in = [[sem(f"b_slab_in{u}{a}") for a in range(2)] for u in range(2)]
        mrow_in = sem("b_mrow_in")
        scores_done = sem("b_scores_done")
        prob_ready = [sem(f"b_prob_ready{s}") for s in range(SLOTS)]
        pv_done = [sem(f"b_pv_done{s}") for s in range(SLOTS)]
        ov_ready = [sem(f"b_ov_ready{s}") for s in range(2)]
        ring_full = sem("b_ring_full")
        ring_free = sem("b_ring_free")
        nmax_ready = sem("b_nmax_ready")
        mpart_ready = sem("b_mpart_ready")
        dchain = sem("b_dchain")
        rs_ready = sem("b_rs_ready")
        pchain = sem("b_pchain")
        setup = sem("b_setup")
        v_ready = sem("b_v_ready")
        post_done = sem("b_post_done")
        block = ctx.enter_context(nc.Block())

        q_rows = dram["q"].rearrange("b n x d t -> (b n) (x d) t")
        k_rows = dram["k"].rearrange("b n d x t -> (b n) (d x) t")

        def spread_units():
            spans = [2 * (BLK - off) + ISSUE if FIRST_U <= k <= LAST_U else 0 for k, (c, st, off, w) in enumerate(STEPS)]
            costs = [w + ISSUE // 2 for a, i, ch, w in UNITS]
            per_step, done, k = [[] for _ in range(NSTEP + 1)], 0, 0
            for unit, cost in zip(UNITS, costs):
                middle = (done + cost / 2) * sum(spans) / sum(costs)
                while sum(spans[:k + 1]) < middle:
                    k += 1
                per_step[k].append(unit)
                done += cost
            return per_step

        UNITS_AT = spread_units()

        def ring_at(k, more):
            out = [("max", n) for n in UNITS_AT[k]] if more else []
            out += [("fold", c) for c in range(BPB) if LAST[c] + EVAC + 1 == k or (k == NSTEP and c == BPB - 1)]
            if more and k == LAST_U + 2:
                out.append(("turn", None))
            return out

        def ring_base(n):
            return NUNIT + 1 + RING_HEAD * n

        def heads(eng, turn):
            with eng.Fori(0, NH // 2 - 1) as j:
                for u in range(2):
                    turn(2 * j + u, u, True)
            turn(NH - 2, 0, True)
            turn(NH - 1, 1, False)

        @block.sync
        def _(sp):
            for s in sems:
                sp.sem_inc(s, CREDIT)
            for w, name in enumerate(("lq1", "lk1", "lq2", "lk2")):
                sp.dma_start(lam_in[:, w, :], io[name].partition_broadcast(P)).then_inc(lam_load, 16)
            sp.wait_ge(setup, 2 + CREDIT)

            def load(n, u):
                for a in range(2):
                    row = slice(2 * n + a, 2 * n + a + 1) if isinstance(n, int) else bass.ds(n * 2 + a, 1)
                    sp.dma_start(qslab[u][a][0:KQ, :], q_rows[row].rearrange("o r t -> (o r) t").unsqueeze(1)
                                 .to_broadcast([3 * HD, 3, T])).then_inc(slab_in[u][a], 16)
                    sp.dma_start(kslab[u][a][0:KQ, :], k_rows[row].rearrange("o r t -> (o r) t")
                                 .partition_broadcast(3)).then_inc(slab_in[u][a], 16)

            def maxima(n, u):
                sp.wait_ge(mpart_ready, n + 1 + CREDIT)
                for a in range(2):
                    for x in range(3):
                        sp.dma_start(qslab[u][a][MROW + x:MROW + x + 1, :].rearrange("o (i t) -> o i t", t=P),
                                     mpart[a * ST_T:(a + 1) * ST_T, x, :]).then_inc(mrow_in, 16)

            load(0, 0)
            maxima(0, 0)

            def turn(n, u, more):
                if more:
                    sp.wait_ge(scores_done, NSTEP * n + CREDIT)
                    load(n + 1, 1 - u)
                    maxima(n + 1, 1 - u)
            heads(sp, turn)

        @block.gpsimd
        def _(pool):
            c = Chain(pool, masks)
            c.after(pool.memset(kslabs[MROW:P], 1.0))
            c.mark(pool.memset(ident_b[:], 0.0))
            c.mark(pool.memset(mask_q[:], 0.0))
            c.mark(pool.memset(mask_k[:, 0:P], NEG))
            c.mark(pool.memset(mask_k[:, P:2 * P], 0.0))
            c.mark(pool.memset(fold[:], 0.0))
            c.wait()
            c.mark(pool.affine_select(out=ident_b[:], in_=ident_b[:], compare_op=ALU.not_equal, fill=1.0, base=0,
                                      pattern=[[-1, P]], channel_multiplier=1))
            c.mark(pool.affine_select(out=mask_q[:], in_=mask_q[:], compare_op=ALU.is_ge, fill=NEG, base=0,
                                      pattern=[[-1, P]], channel_multiplier=1))
            c.mark(pool.affine_select(out=mask_k[:, P:2 * P], in_=mask_k[:, P:2 * P], compare_op=ALU.is_ge, fill=NEG,
                                      base=0, pattern=[[1, P]], channel_multiplier=-1))
            for odd in range(2):
                c.after(pool.affine_select(out=fold[:], in_=fold[:], compare_op=ALU.not_equal, fill=1.0,
                                           base=-VW * odd, pattern=[[-2 * VW, 2], [-1, OC]], channel_multiplier=1))
            pool.wait_ge(setup, 1 + CREDIT)

            def values(n, u):
                pool.tensor_copy(vaug[u][:, :, 0:VD], v_rows[:, bass.ds(n, 1)].rearrange("p o s d -> p (o s) d"))\
                    .then_inc(v_ready, 1)

            v_rows = keep["v"][:].rearrange("p b h s d -> p (b h) s d")
            values(0, 0)
            pool.wait_ge(lam_ready, 1 + CREDIT)

            def turn(n, u, more):
                if more:
                    for s in range(SLOTS):
                        pool.wait_ge(pv_done[s], (NSTEP // SLOTS) * n + CREDIT)
                    values(n + 1, 1 - u)
                pool.wait_ge(rs_ready, n + 1 + CREDIT)
                p = Chain(pool, pchain)
                p.turn(2 * n)
                pool.wait_ge(post_done, n + CREDIT)
                p.mark(pool.tensor_tensor(o1[:], o[:, :, 0, 0:VD], rs[:, :, 0:1].to_broadcast([P, ST_T, VD]), ALU.mult))
                p.after(pool.tensor_tensor(o2[:], o[:, :, 1, 0:VD], rl[:].unsqueeze(2).to_broadcast([P, ST_T, VD]),
                                           ALU.mult))
                pool.tensor_tensor(keep["o"][:, bass.ds(n, 1)].rearrange("p o s d -> p (o s) d"), o1[:], o2[:],
                                   ALU.subtract).then_inc(post_done, 1)
            heads(pool, turn)

        @block.scalar
        def _(act):
            act.wait_ge(lam_step, 2 + CREDIT)
            act.activation(lam_e[:], lam_s[:], ACT.Exp).then_inc(lam_exp, 1)

            def turn(n, u, more):
                for k in range(NSTEP):
                    off, s = STEPS[k][2], k % SLOTS
                    act.wait_ge(scores_done, NSTEP * n + k + 1 + CREDIT)
                    act.wait_ge(pv_done[s], (NSTEP // SLOTS) * n + k // SLOTS + CREDIT)
                    act.activation(prob[s][:, :, off:BLK], psS[k % 2][:, :, off:BLK], ACT.Exp)\
                       .then_inc(prob_ready[s], 1)
                    for c in range(BPB - 1):
                        if LAST[c] + EVAC == k:
                            copy_sum(n, c, more)
                copy_sum(n, BPB - 1, more)

            def copy_sum(n, c, more):
                order = [x for k in range(NSTEP + 1) for x in ring_at(k, more)]
                k = LAST[c]
                for q in (k - 1, k):
                    act.wait_ge(pv_done[q % SLOTS], (NSTEP // SLOTS) * n + q // SLOTS + 1 + CREDIT)
                if c < 2:
                    act.wait_ge(rs_ready, n + CREDIT)
                else:
                    act.wait_ge(ring_free, ring_base(n) + order.index(("fold", c - 2)) + 1 + CREDIT)
                act.copy(ov[c % 2][:], psV[c % 2][:]).then_inc(ov_ready[c % 2], 1)
            heads(act, turn)

        @block.vector
        def _(dve):
            lc = Chain(dve, lam_step)
            dve.wait_ge(lam_load, 64 + CREDIT)
            lv = lam_in[:].rearrange("p (m w) d -> p m w d", w=2)
            lc.after(dve.tensor_tensor(lam_w[:], lv[:, :, 0], lv[:, :, 1], ALU.mult))
            lc.after(dve.tensor_reduce(lam_s[:], lam_w[:], AX.X, ALU.add))
            dve.wait_ge(lam_exp, 1 + CREDIT)
            lc.after(dve.tensor_tensor(lam[:, 0:1], lam_e[:, 0:1], lam_e[:, 1:2], ALU.subtract))
            dve.tensor_scalar(lam[:, 1:2], lam[:, 0:1], LAMBDA_INIT, None, ALU.add).then_inc(lam_ready, 1)
            for u in range(2):
                lc.mark(dve.memset(vaug[u][:, :, VD + 1:VW], 0.0))
                ins = dve.memset(vaug[u][:, :, VD:VD + 1], 1.0)
                if u == 0:
                    lc.mark(ins)
            ins.then_inc(setup, 1)
            lc.mark(dve.memset(kslabs[64:96].rearrange("p u a t -> p (u a t)").bitcast(F32), 0.0))
            dve.memset(qslabs[64:P].rearrange("p u a t -> p (u a t)").bitcast(F32), 0.0).then_inc(setup, 1)
            lc.after(dve.memset(pmax[:], NEG))
            dve.wait_ge(setup, 2 + CREDIT)
            dve.wait_ge(lam_ready, 1 + CREDIT)
            CH = 4

            class Ring:
                base, n, slot0 = 0, 0, 0

            def ring_bank():
                dve.wait_ge(ring_full, Ring.base + Ring.n + 1 + CREDIT)
                Ring.n += 1
                return psR[(Ring.slot0 + Ring.n - 1) % 2]

            def take_max(unit):
                a, i, ch, w = unit
                dve.tensor_reduce(pmax[:, a * ST_T + i, ch:ch + 1], ring_bank()[:, 0:w], AX.X, ALU.max)\
                   .then_inc(ring_free, 1)

            def whole_max():
                dve.wait_ge(ring_free, Ring.base + Ring.n + CREDIT)
                dve.tensor_reduce(nmax[:], pmax[:], AX.X, ALU.max, negate=True).then_inc(nmax_ready, 1)

            def cut_max(n, c):
                src = ring_bank()[0:2 * ST_T, 0:P]
                dve.wait_ge(mrow_in, 96 * n + CREDIT)
                c.after(dve.tensor_copy(mpart[:, 0], src))
                dve.tensor_tensor(mrest[:, 0], src, mpart[:, 0], ALU.subtract).then_inc(ring_free, 1)
                dve.wait_ge(ring_free, Ring.base + Ring.n + CREDIT)
                c.after(dve.tensor_copy(mpart[:, 1], mrest[:, 0]))
                c.after(dve.tensor_tensor(mrest[:, 1], mrest[:, 0], mpart[:, 1], ALU.subtract))
                dve.tensor_copy(mpart[:, 2], mrest[:, 1]).then_inc(mpart_ready, 1)

            c = Chain(dve, dchain)
            for unit in UNITS:
                take_max(unit)
            whole_max()
            cut_max(0, c)

            def turn(n, u, more):
                c = Chain(dve, dchain)
                c.turn(3 + CH * n)
                Ring.base, Ring.n, Ring.slot0 = ring_base(n), 0, (NUNIT + 1 + RING_HEAD * u) % 2
                for k in range(NSTEP + 1):
                    if k == FIRST_U and more:
                        dve.wait_ge(nmax_ready, n + 1 + CREDIT)
                    for kind, what in ring_at(k, more):
                        if kind == "max":
                            take_max(what)
                        elif kind == "fold":
                            dve.wait_ge(post_done, n + CREDIT)
                            dve.tensor_copy(o[:, TPB * what:TPB * what + TPB].rearrange("p i a d -> p (i a d)"),
                                            ring_bank()[:, 0:TPB * 2 * OC]).then_inc(ring_free, 1)
                        else:
                            cut_max(n + 1, c)
                    if k == LAST_U and more:
                        whole_max()
                dve.wait_ge(ring_free, Ring.base + Ring.n + CREDIT)
                c.after(dve.reciprocal(rs[:], o[:, :, :, VD]))
                dve.tensor_scalar(rl[:], rs[:, :, 1], lam[:, 1:2], None, ALU.mult).then_inc(rs_ready, 1)
            heads(dve, turn)

        @block.tensor
        def _(pe):
            pe.wait_ge(masks, 11 + CREDIT)
            pe.wait_ge(v_ready, 1 + CREDIT)

            class Ring:
                base, n, slot0 = 0, 0, 0

            def take_slot():
                ring = Ring.base + Ring.n
                if not isinstance(ring, int) or ring >= 2:
                    pe.wait_ge(ring_free, ring - 1 + CREDIT)
                s = (Ring.slot0 + Ring.n) % 2
                Ring.n += 1
                return psR[s]

            def max_unit(u, unit):
                a, i, ch, w = unit
                dst = take_slot()
                diag = ch == i // TPB
                ins = pe.matmul(dst[:, 0:w], qslab[u][a][0:K_MAX, i * P:(i + 1) * P],
                                kslab[u][a][0:K_MAX, ch * BLK:ch * BLK + w], start=True, stop=True)
                if diag:
                    ins = pe.matmul(dst[:, w - P:w], ident_b[:], mask_q[:], start=False, stop=True,
                                    skip_group_check=True)
                ins.then_inc(ring_full, 1)

            def turn_max(n):
                pe.wait_ge(nmax_ready, n + 1 + CREDIT)
                dst = take_slot()
                pe.transpose(dst[0:2 * ST_T, 0:P], nmax[:], keep["ident"][:]).then_inc(ring_full, 1)

            for n, unit in enumerate(UNITS):
                if n % (NUNIT // 2) == 0:
                    pe.wait_ge(slab_in[0][unit[0]], 32 + CREDIT)
                max_unit(0, unit)
            turn_max(0)

            def scores(n, u, k):
                c, st, off, first = STEPS[k]
                q = (k - 2) % SLOTS
                pe.wait_ge(prob_ready[q], (NSTEP // SLOTS) * n + ((k - 2) // SLOTS + 1 if k >= 2 else 0) + CREDIT)
                diag = st >= TPB * c
                for a in range(2):
                    ins = pe.matmul(psS[k % 2][:, a, off:BLK], kslab[u][a][:, st * P:(st + 1) * P],
                                    qslab[u][a][:, c * BLK + off:(c + 1) * BLK], start=True, stop=True)
                    if diag:
                        lo = 0 if first else P
                        ins = pe.matmul(psS[k % 2][:, a, off:off + 2 * P - lo], ident_b[:], mask_k[:, lo:2 * P],
                                        start=False, stop=True, skip_group_check=True)
                ins.then_inc(scores_done, 1)

            def value_product(n, u, k):
                c, st, off, _w = STEPS[k]
                pe.wait_ge(prob_ready[k % SLOTS], (NSTEP // SLOTS) * n + k // SLOTS + 1 + CREDIT)
                if st == 0:
                    pe.wait_ge(ov_ready[c % 2], 2 * n + c // 2 + CREDIT)
                for a in range(2):
                    g = 2 * a + st % 2
                    ins = pe.matmul(psV[c % 2][g * VW:(g + 1) * VW, off:BLK], vaug[u][:, st, :],
                                    prob[k % SLOTS][:, a, off:BLK], start=(st < 2), stop=(st >= TPB * c + TPB - 2),
                                    skip_group_check=True)
                ins.then_inc(pv_done[k % SLOTS], 1)

            def fold_sum(n, c):
                pe.wait_ge(ov_ready[c % 2], 2 * n + c // 2 + 1 + CREDIT)
                dst = take_slot()
                for i in range(TPB):
                    ins = pe.matmul(dst[:, i * 2 * OC:(i + 1) * 2 * OC], ov[c % 2][:, i * P:(i + 1) * P],
                                    fold[:].rearrange("p a d -> p (a d)"), start=True, stop=True)
                ins.then_inc(ring_full, 1)

            def ring_work(n, u, ring):
                for kind, what in ring:
                    if kind == "max":
                        if UNITS.index(what) % (NUNIT // 2) == 0:
                            pe.wait_ge(slab_in[1 - u][what[0]], loaded(n, u) + CREDIT)
                        max_unit(1 - u, what)
                    elif kind == "fold":
                        fold_sum(n, what)
                    else:
                        turn_max(n + 1)

            def turn(n, u, more):
                Ring.base, Ring.n, Ring.slot0 = ring_base(n), 0, (NUNIT + 1 + RING_HEAD * u) % 2
                pe.wait_ge(mrow_in, 96 * (n + 1) + CREDIT)
                pe.wait_ge(v_ready, n + 1 + CREDIT)
                for k in range(NSTEP):
                    ring = ring_at(k, more)
                    cuts = RING_CUTS[k % 2]
                    ring_work(n, u, ring[:cuts[0]])
                    scores(n, u, k)
                    ring_work(n, u, ring[cuts[0]:cuts[1]])
                    if k % 2 and k > LAG:
                        value_product(n, u, k - LAG - 1)
                        value_product(n, u, k - LAG)
                    ring_work(n, u, ring[cuts[1]:])
                for k in range(NSTEP - LAG, NSTEP):
                    value_product(n, u, k)
                for kind, what in ring_at(NSTEP, more):
                    fold_sum(n, what)

            def loaded(n, u):
                return (n + 1 - (1 - u)) * 16 + 32

            heads(pe, turn)


def phase_project(nc, io, keep, dram):
    with ExitStack() as ctx:
        sb = lambda name, shape, dt=F32: ctx.enter_context(nc.sbuf_tensor(name, shape, dt))
        ps = lambda name, shape, dt=F32: ctx.enter_context(nc.psum_tensor(name, shape, dt))
        sems = []
        sem = lambda name: credited(ctx, nc, sems, name)

        wp = sb("wp", [P, KD, D])
        gamma = sb("gamma", [P, 1])
        wps = sb("wps", [P, KD, D])
        sq = sb("sq", [P, HEADS, TPB, VD])
        ss = sb("ss", [P, HEADS, TPB])
        var = sb("var", [P, HEADS, TPB])
        root = sb("root", [P, HEADS, TPB])
        inv = sb("inv", [P, HEADS, TPB])
        y = sb("y_c", [P, TPB, D])
        yT = sb("yT", [P, KD, BLK])
        x = sb("x_c", [P, TPB, D])
        f = sb("f_c", [P, TPB, D])
        routed = sb("routed", [P, 2, TPB, D])
        index = sb("index", [P, 2, TPB], I32)
        weight = sb("weight", [P, 2, TPB])
        xf = sb("xf", [P, TPB, D])
        x1 = sb("x1", [P, TPB, D])
        stats = sb("stats_c", [P, TPB, 6])
        mv = sb("mv_c", [P, TPB, 2])
        vare = sb("vare", [P, TPB])
        std = sb("std_c", [P, TPB])
        rstd = sb("rstd_c", [P, TPB])
        xn = sb("xn_c", [P, TPB, D])
        xnT = sb("xnT_c", [P, KD, BLK])
        carrier = sb("carrier_c", [P, 1])
        pcarry = sb("pcarry_c", [P, 2])

        psT = ps("psT_c", [P, KD, BLK])
        psO = ps("psO", [P, TPB, D])
        psN = ps("psN", [P, KD, BLK])

        w_in = sem("c_w_in")
        w_ready = sem("c_w_ready")
        in_x = sem("c_in_x")
        xf_ready = sem("c_xf_ready")
        gathered = ctx.enter_context(nc.semaphore("c_gathered"))
        gather_in = sem("c_gather_in")
        index_ready = sem("c_index_ready")
        summed = sem("c_summed")
        pool_set = sem("c_pool_set")
        var_ready = sem("c_var_ready")
        root_ready = sem("c_root_ready")
        y_ready = sem("c_y_ready")
        yT_done = sem("c_yT_done")
        yT_ready = sem("c_yT_ready")
        o_done = sem("c_o_done")
        x1_ready = sem("c_x1_ready")
        x1_out = sem("c_x1_out")
        vare_ready = sem("c_vare_ready")
        std_ready = sem("c_std_ready")
        xn_ready = sem("c_xn_ready")
        xT_done = sem("c_xT_done")
        xnT_ready = sem("c_xnT_ready")
        xnT_out = sem("c_xnT_out")
        dchain = sem("c_dchain")
        block = ctx.enter_context(nc.Block())

        @block.sync
        def _(sp):
            for s in sems:
                sp.sem_inc(s, CREDIT)
            sp.dma_start(wp[:], io["w_proj"].rearrange("(k p) n -> p k n", p=P)).then_inc(w_in, 16)
            for g in range(P // VD):
                sp.dma_start(gamma[g * VD:(g + 1) * VD, :], io["gamma"].unsqueeze(1)).then_inc(w_in, 16)
            with sp.Fori(0, NBLK) as blk:
                rows = lambda t: t[bass.ds(blk * BLK, BLK), :].rearrange("(j p) d -> p j d", p=P)
                sp.wait_ge(xf_ready, blk + CREDIT)
                sp.dma_start(x[:], rows(io["x"])).then_inc(in_x, 16)
                sp.dma_start(f[:], rows(dram["y"])).then_inc(in_x, 16)
                sp.wait_ge(x1_ready, blk + 1 + CREDIT)
                sp.dma_start(rows(dram["x1"]), x1[:]).then_inc(x1_out, 16)
            sp.wait_ge(x1_out, 16 * NBLK + CREDIT)
            sp.wait_ge(xnT_out, 16 * NBLK + CREDIT)

        @block.gpsimd
        def _(pool):
            pool.memset(pcarry[:], 0.0).then_inc(pool_set, 1)
            pool.wait_ge(pool_set, 1 + CREDIT)
            with pool.Fori(0, NBLK) as blk:
                pool.wait_ge(index_ready, blk + 1 + CREDIT)
                pool.tensor_tensor(pcarry[:, 0:1], pcarry[:, 0:1], pcarry[:, 0:1], ALU.mult)
                for k in range(2):
                    for j in range(TPB):
                        pool.indirect_dma_start(routed[:, k, j, :], None, dram["y"],
                                                bass.IndirectOffsetOnAxis(index[:, k, j:j + 1], 0)).then_inc(gathered, 16)
                pool.wait_ge(gathered, 16 * 2 * TPB * (blk + 1))
                pool.tensor_tensor(pcarry[:, 1:2], pcarry[:, 1:2], pcarry[:, 1:2], ALU.mult).then_inc(gather_in, 1)
                pool.wait_ge(in_x, 32 * blk + 32 + CREDIT)
                pool.wait_ge(x1_ready, blk + CREDIT)
                pool.tensor_tensor(xf[:], x[:], f[:], ALU.add).then_inc(xf_ready, 1)

        @block.scalar
        def _(act):
            with act.Fori(0, NBLK) as blk:
                act.wait_ge(var_ready, blk + 1 + CREDIT)
                act.activation(root[:], var[:], ACT.Sqrt).then_inc(root_ready, 1)
                act.wait_ge(yT_done, blk + 1 + CREDIT)
                act.wait_ge(o_done, blk + CREDIT)
                for k in range(KD):
                    ins = act.copy(yT[:, k], psT[:, k])
                ins.then_inc(yT_ready, 1)
                act.wait_ge(vare_ready, blk + 1 + CREDIT)
                act.activation(std[:], vare[:], ACT.Sqrt).then_inc(std_ready, 1)
                act.wait_ge(xT_done, blk + 1 + CREDIT)
                act.wait_ge(xnT_out, 16 * blk + CREDIT)
                for k in range(KD):
                    ins = act.copy(xnT[:, k], psN[:, k])
                ins.then_inc(xnT_ready, 1)
                act.wait_ge(xnT_ready, blk + 1 + CREDIT)
                act.dma_start(dram["xn2T"][:, :, bass.ds(blk * BLK, BLK)].rearrange("k p t -> p k t"), xnT[:])\
                   .then_inc(xnT_out, 16)

        @block.vector
        def _(dve):
            CH = 22
            dve.wait_ge(w_in, 16 * (1 + P // VD) + CREDIT)

            def indices(blk):
                row = slice(0, 1) if isinstance(blk, int) else bass.ds(blk, 1)
                dve.tensor_copy(index[:].rearrange("p k j -> p (k j)"), keep["yslot"][:, row].rearrange("p o k -> p (o k)"))\
                   .then_inc(index_ready, 1)

            indices(0)
            dve.tensor_scalar(wps[:], wp[:], gamma[:, 0:1], 1.0 - LAMBDA_INIT, ALU.mult, ALU.mult).then_inc(w_ready, 1)
            with dve.Fori(0, BATCH) as b:
                with dve.Fori(0, BPB) as q:
                    blk = b * BPB + q
                    c = Chain(dve, dchain, CH)
                    c.turn(blk * CH)
                    ob = keep["o"][:, bass.ds(b * HEADS, HEADS), bass.ds(q * TPB, TPB), :]
                    c.after(dve.tensor_tensor(sq[:], ob, ob, ALU.mult))
                    c.after(dve.tensor_reduce(ss[:], sq[:], AX.X, ALU.add))
                    dve.tensor_scalar(var[:], ss[:], 1.0 / VD, EPS, ALU.mult, ALU.add).then_inc(var_ready, 1)
                    dve.wait_ge(root_ready, blk + 1 + CREDIT)
                    c.after(dve.reciprocal(inv[:], root[:]))
                    dve.wait_ge(yT_done, blk + CREDIT)
                    for j in range(TPB):
                        ins = dve.tensor_tensor(y[:, j].rearrange("p (h d) -> p h d", h=HEADS), ob[:, :, j],
                                                inv[:, :, j:j + 1].to_broadcast([P, HEADS, VD]), ALU.mult)
                    ins.then_inc(y_ready, 1)
                    c.after(dve.tensor_copy(weight[:].rearrange("p k j -> p (k j)"), keep["c"][:, bass.ds(blk, 1)]
                                            .rearrange("p o k -> p (o k)")))
                    dve.wait_ge(gather_in, blk + 1 + CREDIT)
                    dve.wait_ge(xf_ready, blk + 1 + CREDIT)
                    for k in range(2):
                        for j in range(TPB):
                            c.mark(dve.scalar_tensor_tensor(out=xf[:, j], in0=routed[:, k, j],
                                                            scalar=weight[:, k, j:j + 1], in1=xf[:, j],
                                                            op0=ALU.mult, op1=ALU.add))
                        c.wait()
                    indices((blk + 1) % NBLK)
                    dve.wait_ge(o_done, blk + 1 + CREDIT)
                    dve.wait_ge(x1_out, 16 * blk + CREDIT)
                    dve.tensor_tensor(x1[:], psO[:], xf[:], ALU.add).then_inc(x1_ready, 1)
                    dve.wait_ge(x1_ready, blk + 1 + CREDIT)
                    for j in range(TPB):
                        c.mark(dve.bn_stats(stats[:, j, :], x1[:, j, :]))
                    c.wait()
                    c.mark(dve.memset(carrier[:], 0.0))
                    for j in range(TPB):
                        c.mark(dve.bn_aggr(mv[:, j, :], stats[:, j, :]))
                    c.wait()
                    dve.tensor_scalar(vare[:], mv[:, :, 1], EPS, None, ALU.add).then_inc(vare_ready, 1)
                    dve.wait_ge(std_ready, blk + 1 + CREDIT)
                    c.after(dve.reciprocal(rstd[:], std[:]))
                    dve.wait_ge(xT_done, blk + CREDIT)
                    for j in range(TPB):
                        ins = dve.tensor_scalar(xn[:, j, :], x1[:, j, :], mv[:, j, 0:1], rstd[:, j:j + 1],
                                                ALU.subtract, ALU.mult)
                    ins.then_inc(xn_ready, 1)
                    c.end()

        @block.tensor
        def _(pe):
            pe.wait_ge(w_ready, 1 + CREDIT)
            with pe.Fori(0, NBLK) as blk:
                pe.wait_ge(y_ready, blk + 1 + CREDIT)
                pe.wait_ge(yT_ready, blk + CREDIT)
                for j in range(TPB):
                    for k in range(KD):
                        ins = pe.transpose(psT[:, k, j * P:(j + 1) * P], y[:, j, k * P:(k + 1) * P], keep["ident"][:])
                ins.then_inc(yT_done, 1)
                pe.wait_ge(yT_ready, blk + 1 + CREDIT)
                pe.wait_ge(x1_ready, blk + CREDIT)
                for j in range(TPB):
                    for k in range(KD):
                        ins = pe.matmul(psO[:, j], yT[:, k, j * P:(j + 1) * P], wps[:, k], start=(k == 0),
                                        stop=(k == KD - 1))
                ins.then_inc(o_done, 1)
                pe.wait_ge(xn_ready, blk + 1 + CREDIT)
                pe.wait_ge(xnT_ready, blk + CREDIT)
                for j in range(TPB):
                    for k in range(KD):
                        ins = pe.transpose(psN[:, k, j * P:(j + 1) * P], xn[:, j, k * P:(k + 1) * P], keep["ident"][:])
                ins.then_inc(xT_done, 1)


def phase_state_space(nc, io, keep, dram, out):
    with ExitStack() as ctx:
        sb = lambda name, shape, dt=F32: ctx.enter_context(nc.sbuf_tensor(name, shape, dt))
        ps = lambda name, shape, dt=F32: ctx.enter_context(nc.psum_tensor(name, shape, dt))
        sems = []
        sem = lambda name: credited(ctx, nc, sems, name)
        ET = 2 * DI // P
        FT = F1 // P
        XD = RANK + 2 * NS
        UNITS = NS * CT
        LOADS = 24
        HALO = NTAP - 1

        w_x = sb("w_x_raw", [XD, DI])
        w_dt = sb("w_dt_raw", [P, CT, RANK])
        winT = sb("winT", [P, KD, 2 * DI])
        woutT = sb("woutT", [P, CT, D])
        wxT = sb("wxT", [P, CT, XD])
        wdtT = sb("wdtT", [RANK, DI])
        conv_w = sb("conv_w", [P, CT, NTAP])
        vec = sb("vec", [P, 3, CT])
        a_log = sb("a_log", [P, CT, NS])
        a_exp = sb("a_exp", [P, CT, NS])
        a_neg = sb("a_neg", [P, CT, NS])
        scal = sb("scal", [P, 3])
        sgn = sb("sgn", [P, 3])
        mag = sb("mag", [P, 3])
        fac = sb("fac", [P, 4])
        k0 = sb("k0", [P, 2 * KD, F1], U8)
        k2 = sb("k2", [P, FT, D], U8)
        w0 = sb("w0", [P, KD, F1], F16)
        w1 = sb("w1", [P, FT, F1], F16)
        w2 = sb("w2", [P, FT, D], F16)
        pick = sb("pick", [XD, 2 * NS, P])

        xT = sb("xT_s", [P, KD, BLK])
        xh = sb("xh", [P, KD, BLK], F16)
        xl = sb("xl", [P, KD, BLK], F16)
        x1 = sb("x1_s", [P, TPB, D])
        xc = sb("xc", [P, CT, HALO + BLK])
        cv = sb("cv", [P, CT, BLK])
        sz = sb("sz", [P, CT, BLK])
        xs = sb("xs", [P, CT, BLK])
        xd = sb("xd", [XD, BLK])
        ab = sb("ab", [P, CT, BLK])
        ex = cv
        mx = sb("mx", [P, CT, BLK])
        dt_ = sb("dt", [P, CT, BLK])
        dtx = sb("dtx", [P, CT, BLK])
        crep = sb("crep", [P, 2, BLK])
        a = sb("a", [P, 2, BLK])
        u = sb("u", [P, 2, BLK])
        h = sb("h_d", [P, 2, BLK])
        hc = sb("hc", [P, 2, BLK])
        state = sb("state", [P, CT, NS])
        f1h = sb("f1h", [P, FT, BLK], F16)
        f1l = sb("f1l", [P, FT, BLK], F16)
        f2h = sb("f2h", [P, FT, BLK], F16)
        f2l = sb("f2l", [P, FT, BLK], F16)
        r = sb("r", [P, TPB, D])
        yg, ys = ab, mx
        ob = sb("ob", [P, TPB, D])

        w_in = dtx[:].rearrange("p c (h t) -> p (c h) t", h=2)
        w_out = dt_[:, 0:KD]
        kd = f1h[:].rearrange("p (k f) t -> p k (f t)", k=4)[:, 0:KD]

        k1 = f2h[:].rearrange("p k t -> p (k t)").bitcast(U8).rearrange("p (k f) -> p k f", k=FT)

        psY = [ps(f"psYd{c}", [P, BLK]) for c in range(CT)]
        psB = ps("psB", [P, BLK])
        psC = ps("psC", [P, BLK])
        psW = [ps(f"psW{s}", [P, BLK]) for s in range(2)]

        weights = sem("d_weights")
        consts = sem("d_consts")
        wt_full = sem("d_wt_full")
        wt_free = sem("d_wt_free")
        a_ready0 = sem("d_a_exp")
        wchain = sem("d_wchain")
        w_ready = sem("d_w_ready")
        x_in = sem("d_x_in")
        x1_in = sem("d_x1_in")
        xh_ready = sem("d_xh_ready")
        xl_ready = sem("d_xl_ready")
        full = [sem(f"d_full{s}") for s in range(2)]
        free = [sem(f"d_free{s}") for s in range(2)]
        xc_ready = sem("d_xc_ready")
        cchain = sem("d_cchain")
        conv_done = sem("d_conv_done")
        halo_ready = sem("d_halo_ready")
        xs_ready = sem("d_xs_ready")
        xd_ready = sem("d_xd_ready")
        ab_ready = sem("d_ab_ready")
        ex_ready = sem("d_ex_ready")
        ln_ready = sem("d_ln_ready")
        mx_ready = sem("d_mx_ready")
        dt_ready = sem("d_dt_ready")
        dtx_ready = sem("d_dtx_ready")
        b_full = sem("d_b_full")
        c_full = sem("d_c_full")
        crep_ready = sem("d_crep_ready")
        u_ready = sem("d_u_ready")
        a_ready = [sem(f"d_a_ready{s}") for s in range(2)]
        h_ready = [sem(f"d_h_ready{s}") for s in range(2)]
        hc_ready = [sem(f"d_hc_ready{s}") for s in range(2)]
        y_added = [sem(f"d_y_added{s}") for s in range(2)]
        high_ready = sem("d_high_ready")
        low_ready = sem("d_low_ready")
        yg_ready = sem("d_yg_ready")
        ys_ready = sem("d_ys_ready")
        out_sent = sem("d_out_sent")
        block = ctx.enter_context(nc.Block())

        def sign_unit(sidx):
            if sidx < 4:
                return [("l1", 2 * sidx), ("l1", 2 * sidx + 1)]
            if sidx < 12:
                return [("l2", sidx - 4)]
            return [("l3", sidx - 12)]

        ORDER = [("xz", e) for e in range(ET)] + [("xd", 0)] + [("dt", c) for c in range(CT)]
        for sidx in range(NS):
            ORDER += sign_unit(sidx)
        ORDER += [("out", j) for j in range(TPB)]
        PER = [(len(ORDER) + 1) // 2, len(ORDER) // 2]

        def full_at(blk, kind):
            n = ORDER.index(kind)
            return n % 2, PER[n % 2] * blk + n // 2 + 1

        def weight_copies():
            got = []
            for k in range(KD):
                for half in range(2):
                    got.append((winT[:, k, half * BLK:(half + 1) * BLK], psW[len(got) % 2][:]))
            for c in range(CT):
                got.append((woutT[:, c, :], psW[len(got) % 2][:, 0:D]))
            for c in range(CT):
                got.append((wxT[:, c, :], psW[len(got) % 2][:, 0:XD]))
            got.append((wdtT[:], psW[len(got) % 2][0:RANK, :]))
            return got

        @block.sync
        def _(sp):
            for s in sems:
                sp.sem_inc(s, CREDIT)
            loads = [
                (w_in, io["in_proj"].rearrange("(e p) d -> p e d", p=P)),
                (w_out, io["out_proj"].rearrange("(k p) i -> p k i", p=P)),
                (w_x[:], io["x_proj"]),
                (w_dt[:], io["dt_proj"].rearrange("(c p) r -> p c r", p=P)),
                (conv_w[:], io["conv_w"].rearrange("(c p) o t -> p c (o t)", p=P)),
                (a_log[:], io["A_log"].rearrange("(c p) s -> p c s", p=P)),
                (k0[:], io["k0"].rearrange("(k p) f -> p k f", p=P)),
                (k1, io["k1"].rearrange("(k p) f -> p k f", p=P)),
                (k2[:], io["k2"].rearrange("(k p) f -> p k f", p=P)),
            ]
            for n, name in enumerate(("conv_b", "dt_b", "D_skip")):
                for c in range(CT):
                    loads.append((vec[:, n, c:c + 1], io[name][c * P:(c + 1) * P].unsqueeze(1)))
            for n, name in enumerate(("s0", "s1", "s2")):
                loads.append((scal[:, n:n + 1], io[name].partition_broadcast(P)))
            for dst, src in loads:
                sp.dma_start(dst, src).then_inc(weights, 16)
            assert len(loads) == LOADS
            with sp.Fori(0, NBLK) as blk:
                rows = lambda t: t[bass.ds(blk * BLK, BLK), :].rearrange("(j p) d -> p j d", p=P)
                sp.wait_ge(xl_ready, blk + CREDIT)
                sp.wait_ge(dt_ready, CT * blk + CREDIT)
                sp.dma_start(xT[:], dram["xn2T"][:, :, bass.ds(blk * BLK, BLK)].rearrange("k p t -> p k t"))\
                  .then_inc(x_in, 16)
                sp.dma_start(x1[:], rows(dram["x1"])).then_inc(x1_in, 16)
                for j in (TPB - 2, TPB - 1):
                    s, n = full_at(blk, ("out", j))
                    sp.wait_ge(free[s], n + CREDIT)
                sp.dma_start(rows(out), ob[:]).then_inc(out_sent, 16)
            sp.wait_ge(out_sent, 16 * NBLK + CREDIT)

        @block.gpsimd
        def _(pool):
            c = Chain(pool, consts)
            c.after(pool.memset(pick[:], 1.0))
            c.mark(pool.affine_select(out=pick[:], in_=pick[:], compare_op=ALU.is_equal, fill=0.0, base=-RANK,
                                      pattern=[[-1, 2 * NS], [0, P]], channel_multiplier=1))
            with pool.Fori(0, NBLK) as blk:
                for t in range(UNITS):
                    s, i, sidx, c_ = t % 2, t // 2, t // CT, t % CT
                    n = UNITS // 2 * blk + i
                    pool.wait_ge(h_ready[s], n + 1 + CREDIT)
                    if c_ == 0:
                        pool.wait_ge(crep_ready, NS * blk + sidx + 1 + CREDIT)
                    pool.wait_ge(y_added[s], n + CREDIT)
                    pool.tensor_tensor(hc[:, s], h[:, s], crep[:, sidx % 2], ALU.mult)
                    pool.tensor_copy(state[:, c_, sidx:sidx + 1], h[:, s, BLK - 1:BLK]).then_inc(hc_ready[s], 1)

        @block.scalar
        def _(act):
            act.wait_ge(weights, 16 * LOADS + CREDIT)
            act.activation(a_exp[:], a_log[:], ACT.Exp).then_inc(a_ready0, 1)
            def block_of(b, q):
                blk = b * BPB + q
                act.wait_ge(x_in, 16 * blk + 16 + CREDIT)
                act.wait_ge(high_ready, 2 * FT * blk + CREDIT)
                act.copy(xh[:], xT[:]).then_inc(xh_ready, 1)
                for e in range(ET):
                    s, n = full_at(blk, ("xz", e))
                    act.wait_ge(full[s], n + CREDIT)
                    if e < CT:
                        if e == 0:
                            act.wait_ge(halo_ready, blk + b + 1 + CREDIT)
                        act.copy(xc[:, e, HALO:], psW[s][:]).then_inc(free[s], 1)
                    else:
                        if e == CT:
                            act.wait_ge(ys_ready, CT * blk + CREDIT)
                        act.activation(sz[:, e - CT], psW[s][:], ACT.Silu).then_inc(free[s], 1)
                for c in range(CT):
                    act.wait_ge(conv_done, CT * blk + c + 1 + CREDIT)
                    act.wait_ge(yg_ready, CT * blk + CREDIT)
                    act.activation(xs[:, c], cv[:, c], ACT.Silu, bias=vec[:, 0, c:c + 1]).then_inc(xs_ready, 1)
                s, n = full_at(blk, ("xd", 0))
                act.wait_ge(full[s], n + CREDIT)
                act.copy(xd[:], psW[s][0:XD, :]).then_inc(free[s], 1)
                for c in range(CT):
                    s, n = full_at(blk, ("dt", c))
                    act.wait_ge(full[s], n + CREDIT)
                    act.wait_ge(mx_ready, CT * blk + c + 1 + CREDIT)
                    act.activation(ab[:, c], psW[s][:], ACT.Abs, bias=vec[:, 1, c:c + 1]).then_inc(free[s], 1)
                act.wait_ge(free[s], n + CREDIT)
                s, n = full_at(blk, ("dt", CT - 2))
                act.wait_ge(free[s], n + CREDIT)
                act.activation(ex[:], ab[:], ACT.Exp, scale=-1.0).then_inc(ex_ready, 1)
                act.wait_ge(ex_ready, blk + 1 + CREDIT)
                act.activation(ab[:], ex[:], ACT.Ln, bias=1.0).then_inc(ln_ready, 1)
                for sidx in range(NS):
                    act.wait_ge(c_full, NS * blk + sidx + 1 + CREDIT)
                    act.wait_ge(hc_ready[1], UNITS // 2 * blk + max(0, 2 * sidx - 2) + CREDIT)
                    act.copy(crep[:, sidx % 2], psC[:]).then_inc(crep_ready, 1)
                    for c in range(CT):
                        t = sidx * CT + c
                        s, i = t % 2, t // 2
                        if sidx == 0:
                            act.wait_ge(dt_ready, CT * blk + c + 1 + CREDIT)
                        act.wait_ge(h_ready[s], UNITS // 2 * blk + i + CREDIT)
                        act.activation(a[:, s], dt_[:, c], ACT.Exp, scale=a_neg[:, c, sidx:sidx + 1])\
                           .then_inc(a_ready[s], 1)
                    for kind, f in sign_unit(sidx):
                        if kind == "l3":
                            continue
                        s, n = full_at(blk, (kind, f))
                        act.wait_ge(full[s], n + CREDIT)
                        dst = f1h if kind == "l1" else f2h
                        act.activation(dst[:, f], psW[s][:], ACT.Relu).then_inc(high_ready, 1)

            with act.Fori(0, BATCH) as b:
                with act.Fori(0, BPB) as q:
                    block_of(b, q)

        @block.vector
        def _(dve):
            c = Chain(dve, wchain)
            dve.wait_ge(weights, 16 * LOADS + CREDIT)
            c.mark(dve.tensor_scalar(sgn[:], scal[:], 0.0, None, ALU.is_ge))
            dve.wait_ge(a_ready0, 1 + CREDIT)
            c.after(dve.tensor_scalar(a_neg[:], a_exp[:], -1.0, None, ALU.mult))
            c.after(dve.tensor_scalar(sgn[:], sgn[:], 2.0, -1.0, ALU.mult, ALU.add))
            c.after(dve.tensor_tensor(mag[:], sgn[:], scal[:], ALU.mult))
            c.mark(dve.tensor_scalar(fac[:, 0:1], mag[:, 0:1], mag[:, 1:2], 64.0, ALU.mult, ALU.mult))
            c.mark(dve.tensor_scalar(fac[:, 2:3], sgn[:, 1:2], 0.25, None, ALU.mult))
            c.after(dve.tensor_scalar(fac[:, 3:4], sgn[:, 1:2], -0.125, None, ALU.mult))
            c.mark(dve.tensor_tensor(fac[:, 1:2], fac[:, 0:1], scal[:, 2:3], ALU.mult))
            c.after(dve.tensor_tensor(kd, k0[:, 0:KD], k0[:, KD:2 * KD], ALU.subtract))
            c.mark(dve.tensor_scalar(w0[:], kd, sgn[:, 0:1], None, ALU.mult))
            c.mark(dve.tensor_scalar(w1[:], k1, fac[:, 2:3], fac[:, 3:4], ALU.mult, ALU.add))
            dve.tensor_scalar(w2[:], k2[:], 2.0, -1.0, ALU.mult, ALU.add).then_inc(w_ready, 1)

            for n, (dst, src) in enumerate(weight_copies()):
                dve.wait_ge(wt_full, n + 1 + CREDIT)
                dve.tensor_copy(dst, src).then_inc(wt_free, 1)

            CH = CT * (NTAP - 1)
            with dve.Fori(0, BATCH) as b:
                dve.wait_ge(conv_done, CT * BPB * b + CREDIT)
                for s in range(2):
                    dve.wait_ge(hc_ready[s], UNITS // 2 * BPB * b + CREDIT)
                dve.memset(state[:], 0.0)
                dve.memset(xc[:, :, 0:HALO], 0.0).then_inc(halo_ready, 1)
                with dve.Fori(0, BPB) as q:
                    blk = b * BPB + q
                    dve.wait_ge(xh_ready, blk + 1 + CREDIT)
                    dve.tensor_tensor(xl[:], xT[:], xh[:], ALU.subtract).then_inc(xl_ready, 1)
                    k = Chain(dve, cchain, CH)
                    k.turn(CH * blk)
                    for c in range(CT):
                        s, n = full_at(blk, ("xz", c))
                        dve.wait_ge(free[s], n + CREDIT)
                        if c == 0:
                            dve.wait_ge(xs_ready, CT * blk + CREDIT)
                        k.after(dve.tensor_scalar(cv[:, c], xc[:, c, 0:BLK], conv_w[:, c, 0:1], None, ALU.mult))
                        for t in range(1, NTAP):
                            ins = dve.scalar_tensor_tensor(out=cv[:, c], in0=xc[:, c, t:t + BLK],
                                                           scalar=conv_w[:, c, t:t + 1], in1=cv[:, c],
                                                           op0=ALU.mult, op1=ALU.add)
                            if t < NTAP - 1:
                                k.after(ins)
                        ins.then_inc(conv_done, 1)
                    k.end()
                    dve.wait_ge(conv_done, CT * blk + CT + CREDIT)
                    dve.tensor_copy(xc[:, :, 0:HALO], xc[:, :, BLK:]).then_inc(halo_ready, 1)
                    for c in range(CT):
                        s, n = full_at(blk, ("dt", c))
                        dve.wait_ge(full[s], n + CREDIT)
                        dve.tensor_scalar(mx[:, c], psW[s][:], vec[:, 1, c:c + 1], 0.0, ALU.add, ALU.max)\
                           .then_inc(mx_ready, 1)
                    dve.wait_ge(ln_ready, blk + 1 + CREDIT)
                    dve.wait_ge(mx_ready, CT * blk + CT + CREDIT)
                    for c in range(CT):
                        dve.tensor_tensor(dt_[:, c], mx[:, c], ab[:, c], ALU.add).then_inc(dt_ready, 1)
                    for c in range(CT):
                        dve.wait_ge(dt_ready, CT * blk + c + 1 + CREDIT)
                        dve.wait_ge(xs_ready, CT * blk + c + 1 + CREDIT)
                        dve.tensor_tensor(dtx[:, c], dt_[:, c], xs[:, c], ALU.mult).then_inc(dtx_ready, 1)
                    dve.wait_ge(dtx_ready, CT * blk + CT + CREDIT)
                    for sidx in range(NS):
                        for c in range(CT):
                            t = sidx * CT + c
                            s, i = t % 2, t // 2
                            n = UNITS // 2 * blk + i
                            if c == 0:
                                dve.wait_ge(b_full, NS * blk + sidx + 1 + CREDIT)
                            dve.wait_ge(h_ready[s], n + CREDIT)
                            dve.tensor_tensor(u[:, s], dtx[:, c], psB[:], ALU.mult).then_inc(u_ready, 1)
                            dve.wait_ge(a_ready[s], n + 1 + CREDIT)
                            dve.wait_ge(hc_ready[s], n + CREDIT)
                            dve.wait_ge(u_ready, UNITS * blk + t + 1 + CREDIT)
                            dve.tensor_tensor_scan(h[:, s], a[:, s], u[:, s], state[:, c, sidx:sidx + 1],
                                                   ALU.mult, ALU.add).then_inc(h_ready[s], 1)
                        for kind, f in sign_unit(sidx):
                            s, n = full_at(blk, (kind, f))
                            if kind == "l3":
                                if f == 0:
                                    dve.wait_ge(x1_in, 16 * blk + 16 + CREDIT)
                                    for e in range(2):
                                        dve.wait_ge(free[e], PER[e] * blk + CREDIT)
                                dve.wait_ge(full[s], n + CREDIT)
                                dve.scalar_tensor_tensor(out=r[:, f], in0=psW[s][:, 0:D], scalar=fac[:, 1:2],
                                                         in1=x1[:, f], op0=ALU.mult, op1=ALU.add).then_inc(free[s], 1)
                                continue
                            dve.wait_ge(high_ready, 2 * FT * blk + (f if kind == "l1" else FT + f) + 1 + CREDIT)
                            hi, lo = (f1h, f1l) if kind == "l1" else (f2h, f2l)
                            dve.scalar_tensor_tensor(out=lo[:, f], in0=psW[s][:], scalar=0.0, in1=hi[:, f],
                                                     op0=ALU.max, op1=ALU.subtract).then_inc(free[s], 1)
                    s, n = full_at(blk, ("l3", TPB - 1))
                    dve.wait_ge(free[s], n + CREDIT)
                    s, n = full_at(blk, ("l3", TPB - 2))
                    dve.wait_ge(free[s], n + CREDIT)
                    for s in range(2):
                        dve.wait_ge(y_added[s], UNITS // 2 * (blk + 1) + CREDIT)
                    for c in range(CT):
                        dve.scalar_tensor_tensor(out=yg[:, c], in0=xs[:, c], scalar=vec[:, 2, c:c + 1], in1=psY[c][:],
                                                 op0=ALU.mult, op1=ALU.add).then_inc(yg_ready, 1)
                    s, n = full_at(blk, ("xz", ET - 1))
                    dve.wait_ge(free[s], n + CREDIT)
                    for c in range(CT):
                        dve.wait_ge(yg_ready, CT * blk + c + 1 + CREDIT)
                        dve.tensor_tensor(ys[:, c], yg[:, c], sz[:, c], ALU.mult).then_inc(ys_ready, 1)
                    dve.wait_ge(out_sent, 16 * blk + CREDIT)
                    for j in range(TPB):
                        s, n = full_at(blk, ("out", j))
                        dve.wait_ge(full[s], n + CREDIT)
                        dve.tensor_tensor(ob[:, j], psW[s][:, 0:D], r[:, j], ALU.add).then_inc(free[s], 1)

        @block.tensor
        def _(pe):
            pe.wait_ge(weights, 16 * LOADS + CREDIT)
            pe.wait_ge(consts, 2 + CREDIT)
            ident = keep["ident"]
            n = [0]

            def bank():
                if n[0] >= 2:
                    pe.wait_ge(wt_free, n[0] - 1 + CREDIT)
                n[0] += 1
                return psW[(n[0] - 1) % 2]

            for k in range(KD):
                for half in range(2):
                    dst = bank()
                    for e in range(4):
                        ins = pe.transpose(dst[:, e * P:(e + 1) * P], w_in[:, half * 4 + e, k * P:(k + 1) * P], ident[:])
                    ins.then_inc(wt_full, 1)
            for c in range(CT):
                dst = bank()
                for k in range(KD):
                    ins = pe.transpose(dst[:, k * P:(k + 1) * P], w_out[:, k, c * P:(c + 1) * P], ident[:])
                ins.then_inc(wt_full, 1)
            for c in range(CT):
                pe.transpose(bank()[:, 0:XD], w_x[:, c * P:(c + 1) * P], ident[0:XD, 0:XD]).then_inc(wt_full, 1)
            dst = bank()
            for c in range(CT):
                ins = pe.transpose(dst[0:RANK, c * P:(c + 1) * P], w_dt[:, c, :], ident[:])
            ins.then_inc(wt_full, 1)
            pe.wait_ge(wt_free, n[0] + CREDIT)
            pe.wait_ge(w_ready, 1 + CREDIT)

            with pe.Fori(0, NBLK) as blk:
                def work(kind):
                    s, turns = full_at(blk, kind)
                    pe.wait_ge(free[s], turns - 1 + CREDIT)
                    return s, psW[s]

                pe.wait_ge(x_in, 16 * blk + 16 + CREDIT)
                for e in range(ET):
                    s, dst = work(("xz", e))
                    for k in range(KD):
                        ins = pe.matmul(dst[:], winT[:, k, e * P:(e + 1) * P], xT[:, k], start=(k == 0), stop=(k == KD - 1))
                    ins.then_inc(full[s], 1)
                s, dst = work(("xd", 0))
                for c in range(CT):
                    pe.wait_ge(xs_ready, CT * blk + c + 1 + CREDIT)
                    ins = pe.matmul(dst[0:XD, :], wxT[:, c], xs[:, c], start=(c == 0), stop=(c == CT - 1))
                ins.then_inc(full[s], 1)
                sx, nx = full_at(blk, ("xd", 0))
                for c in range(CT):
                    s, dst = work(("dt", c))
                    if c == 0:
                        pe.wait_ge(free[sx], nx + CREDIT)
                    pe.matmul(dst[:], wdtT[:, c * P:(c + 1) * P], xd[0:RANK, :], start=True, stop=True).then_inc(full[s], 1)

                def spread(sidx):
                    pe.wait_ge(u_ready, UNITS * blk + CT * sidx + CREDIT)
                    pe.matmul(psB[:], pick[:, sidx], xd[:], start=True, stop=True).then_inc(b_full, 1)
                    pe.wait_ge(crep_ready, NS * blk + sidx + CREDIT)
                    pe.matmul(psC[:], pick[:, NS + sidx], xd[:], start=True, stop=True).then_inc(c_full, 1)

                def sign_products(kind, f):
                    s, dst = work((kind, f))
                    if kind == "l1":
                        if f == 0:
                            pe.wait_ge(xl_ready, blk + 1 + CREDIT)
                        ops = [(w0[:, k, f * P:(f + 1) * P], x[:, k], BLK) for k in range(KD) for x in (xh, xl)]
                    elif kind == "l2":
                        if f == 0:
                            for g in (FT - 2, FT - 1):
                                sl, nl = full_at(blk, ("l1", g))
                                pe.wait_ge(free[sl], nl + CREDIT)
                        ops = [(w1[:, k, f * P:(f + 1) * P], x[:, k], BLK) for k in range(FT) for x in (f1h, f1l)]
                    else:
                        if f == 0:
                            for g in (FT - 2, FT - 1):
                                sl, nl = full_at(blk, ("l2", g))
                                pe.wait_ge(free[sl], nl + CREDIT)
                        ops = [(x[:, k, f * P:(f + 1) * P], w2[:, k], D) for k in range(FT) for x in (f2h, f2l)]
                    for n, (lhs, rhs, w) in enumerate(ops):
                        ins = pe.matmul(dst[:, 0:w], lhs, rhs, start=(n == 0), stop=(n == len(ops) - 1))
                    ins.then_inc(full[s], 1)

                spread(0)
                for sidx in range(NS):
                    for kind, f in sign_unit(sidx):
                        sign_products(kind, f)
                    for c in range(CT):
                        t = sidx * CT + c
                        s, i = t % 2, t // 2
                        if c == CT - 1 and sidx + 1 < NS:
                            spread(sidx + 1)
                        if sidx == 0:
                            pe.wait_ge(yg_ready, CT * blk + CREDIT)
                        pe.wait_ge(hc_ready[s], UNITS // 2 * blk + i + 1 + CREDIT)
                        pe.matmul(psY[c][:], ident[:], hc[:, s], start=(sidx == 0), stop=(sidx == NS - 1),
                                  skip_group_check=True).then_inc(y_added[s], 1)
                for j in range(TPB):
                    s, dst = work(("out", j))
                    for c in range(CT):
                        if j == 0:
                            pe.wait_ge(ys_ready, CT * blk + c + 1 + CREDIT)
                        ins = pe.matmul(dst[:, 0:D], ys[:, c, j * P:(j + 1) * P], woutT[:, c], start=(c == 0),
                                        stop=(c == CT - 1))
                    ins.then_inc(full[s], 1)


def build(nc, io, out):
    with ExitStack() as ctx:
        scratch = lambda name, shape, dt=F32: nc.dram_tensor(name, shape, dt, kind="Internal").ap()
        dram = {
            "rows": scratch("rows_d", [E * REG + N, D]),
            "y": scratch("y_d", [TT * P, D]),
            "q": scratch("q_d", [BATCH, 2 * HEADS, 3, HD, T], BF16),
            "k": scratch("k_d", [BATCH, 2 * HEADS, HD, 3, T], BF16),
            "x1": scratch("x1_d", [N, D]),
            "xn2T": scratch("xn2T_d", [KD, P, N]),
        }
        sb = lambda c, name, shape, dt=F32: c.enter_context(nc.sbuf_tensor(name, shape, dt))
        keep = {
            "ident": sb(ctx, "ident", [P, P]),
            "moe_w": ctx.enter_context(nc.semaphore("moe_w")),
        }
        with ExitStack() as attn:
            keep["c"] = sb(attn, "c_all", [P, NBLK, 2 * TPB])
            keep["yslot"] = sb(attn, "yslot_all", [P, NBLK, 2 * TPB], I32)
            keep["v"] = sb(attn, "v_all", [P, BATCH, HEADS, ST_T, VD])
            with ExitStack() as moe:
                keep["hot"] = sb(moe, "hot_all", [P, NBLK, 2, TPB, E])
                keep["slot"] = sb(moe, "slot_all", [P, NBLK, 2 * TPB])
                keep["table"] = sb(moe, "table", [P, 2, TT], I32)
                keep["wg"] = sb(moe, "wg", [P, NE, KD, M])
                keep["wu"] = sb(moe, "wu", [P, NE, KD, M])
                keep["wd"] = sb(moe, "wd", [P, NE, M // P, D])
                phase_norm_qkv(nc, io, keep, dram)
                phase_experts(nc, io, keep, dram)
            keep["o"] = sb(attn, "o_all", [P, NH, ST_T, VD])
            phase_attention(nc, io, keep, dram)
            phase_project(nc, io, keep, dram)
        phase_state_space(nc, io, keep, dram, out)


_SHORT = {
    "L0_attn_x": "x", "L0_attn_w_attn": "w_attn", "L0_attn_w_proj": "w_proj", "L0_attn_lambda_q1": "lq1",
    "L0_attn_lambda_q2": "lq2", "L0_attn_lambda_k1": "lk1", "L0_attn_lambda_k2": "lk2", "L0_attn_gamma": "gamma",
    "L0_ffn_gate_w": "gate_w", "L0_ffn_beta": "beta", "L0_ffn_gate_proj_w": "gate_proj", "L0_ffn_up_proj_w": "up_proj",
    "L0_ffn_down_proj_w": "down_proj", "L0_ffn_shared_gate_w": "shared_gate", "L0_ffn_shared_up_w": "shared_up",
    "L0_ffn_shared_down_w": "shared_down", "L1_attn_in_proj_w": "in_proj", "L1_attn_conv_w": "conv_w",
    "L1_attn_conv_b": "conv_b", "L1_attn_x_proj_w": "x_proj", "L1_attn_dt_proj_w": "dt_proj",
    "L1_attn_dt_proj_b": "dt_b", "L1_attn_A_log": "A_log", "L1_attn_D_skip": "D_skip", "L1_attn_out_proj_w": "out_proj",
    "L1_ffn_k0": "k0", "L1_ffn_k1": "k1", "L1_ffn_k2": "k2", "L1_ffn_s0": "s0", "L1_ffn_s1": "s1", "L1_ffn_s2": "s2",
}


def kernel(**inputs):
    import numpy as _np
    import concourse.bacc as _bacc
    from concourse import mybir as _mybir
    from concourse.bass_utils import run_bass_kernel_spmd as _run

    nc = _bacc.Bacc("TRN2", target_bir_lowering=False, num_devices=1)
    arrays, io = {}, {}
    for name, short in _SHORT.items():
        a = _np.ascontiguousarray(inputs[name])
        if a.ndim == 0:
            a = a.reshape(1)
        arrays[f"in_{name}_dram"] = a
        io[short] = nc.dram_tensor(f"in_{name}_dram", a.shape, _mybir.dt.from_np(a.dtype), kind="ExternalInput").ap()
    io["x"] = io["x"].rearrange("b t d -> (b t) d")
    out = nc.dram_tensor("out_0_dram", (BATCH, T, D), _mybir.dt.float32, kind="ExternalOutput").ap()
    build(nc, io, out.rearrange("b t d -> (b t) d"))
    r = _run(nc, [arrays], core_ids=[0])
    return r.results[0]["out_0_dram"]
```

```python
import numpy as np
import concourse.bass as bass
from concourse import mybir
from contextlib import ExitStack

F32 = mybir.dt.float32
BF16 = mybir.dt.bfloat16
F16 = mybir.dt.float16
U32 = mybir.dt.uint32
U8 = mybir.dt.uint8
ACT = mybir.ActivationFunctionType
ALU = mybir.AluOpType
AX = mybir.AxisListType

P = 128
BATCH, T, D = 2, 2048, 256
N = BATCH * T
BLK = 512
NBLK = N // BLK
BPB = T // BLK
TPB = BLK // P
NT = N // P
KD = D // P
HEADS, HD = 16, 8
VD = 2 * HD
E, M = 8, 512
NE = E + 1
EPS = 1e-5
CREDIT = 1
LAMBDA_INIT = 0.2
NEG = -1e30

ST_T = T // P
NH = BATCH * HEADS
KQ = 9 * HD
VW = 32
OC = VD + 1

DI = 512
CT = DI // P
NS = 16
NTAP = 4
RANK = 16
F1 = 1024


I32 = mybir.dt.int32
REG = N + P
RT = (2 * N + E * (P - 1)) // P + 1
RT -= RT * P > 2 * N + E * (P - 1)
RT += (NT + RT) % 2
TT = NT + RT


def credited(ctx, nc, sems, name):
    sems.append(ctx.enter_context(nc.semaphore(name)))
    return sems[-1]


class Chain:

    def __init__(self, eng, sem, per_turn=0):
        self.eng, self.sem, self.per, self.n, self.base = eng, sem, per_turn, 0, 0

    def turn(self, base):
        self.base, self.n = base, 0

    def mark(self, ins):
        ins.then_inc(self.sem, 1)
        self.n += 1

    def wait(self):
        self.eng.wait_ge(self.sem, self.base + self.n + CREDIT)

    def after(self, ins):
        self.mark(ins)
        self.wait()

    def end(self):
        assert self.n == self.per, (self.n, self.per)


def phase_norm_qkv(nc, io, keep, dram):
    with ExitStack() as ctx:
        sb = lambda name, shape, dt=F32: ctx.enter_context(nc.sbuf_tensor(name, shape, dt))
        ps = lambda name, shape, dt=F32: ctx.enter_context(nc.psum_tensor(name, shape, dt))
        sems = []
        sem = lambda name: credited(ctx, nc, sems, name)

        wqkv = sb("wqkv", [P, KD, 3 * D])
        gate_rows = sb("gate_rows", [E, D])
        gateT = sb("gateT", [P, KD, E])
        beta = sb("beta", [P, E])
        iota_u = sb("iota_u", [P, E + NT + TT], I32)
        iota_f = sb("iota_f", [P, E + NT + TT])
        iota_e = iota_f[:, 0:E]
        iota_m = iota_f[:, E:E + NT]
        iota_t = iota_f[:, E + NT:]
        region = sb("region", [P, E])
        before = sb("before", [P, P])
        ones = sb("ones", [P, P])
        zeros = sb("zeros", [P, D])
        x = sb("x", [P, TPB, D])
        stats = sb("stats", [P, TPB, 6])
        mv = sb("mv", [P, TPB, 2])
        std = sb("std", [P, TPB])
        rstd = sb("rstd", [P, TPB])
        xn = sb("xn", [P, TPB, D])
        xnT = sb("xnT", [P, KD, BLK])
        qf = sb("qf", [P, 2, BLK])
        rest = sb("rest", [P, 2, BLK])
        parts = sb("parts", [P, 2, 3, BLK], BF16)
        sel = sb("sel", [P, TPB, E])
        top = sb("top", [P, TPB, E])
        topi = sb("topi", [P, TPB, E], U32)
        topf = sb("topf", [P, TPB, E])
        hot = sb("hot", [P, 2, TPB, E])
        both = sb("both", [P, TPB, E])
        seen = sb("seen", [P, TPB + 1, E])
        sig = sb("sig", [P, TPB, E])
        place = sb("place", [P, TPB, E])
        pick = sb("picks", [P, 2, 2, TPB, E])
        picked = sb("picked", [P, 2, 2, TPB])
        slot = sb("slot", [P, 2, TPB], I32)
        count = sb("count", [P, E])
        wide = sb("wide", [P, E, RT])
        wide2 = sb("wide2", [P, E, RT])
        tiles = sb("tiles", [P, E])
        ends = sb("ends", [P, E])
        starts = sb("starts", [P, E])
        shift = sb("shift", [P, E])
        tail_f = sb("tail_f", [P, E])
        tail = sb("tail", [P, E], I32)
        table_f = sb("table_f", [P, 2, TT])
        yslot_f = sb("yslot_f", [P, NT * 2])
        yshift = sb("yshift", [P, NT * 2])
        pcarry = sb("pcarry", [P, 2])
        carrier = sb("carrier", [P, 4])

        psT = ps("psT", [P, KD, BLK])
        psQ = ps("psQ", [P, 2, BLK])
        psV = ps("psV", [P, TPB, D])
        psL = ps("psL", [P, TPB, E])
        psK = ps("psK", [P, TPB, E])

        w_in = sem("a_w_in")
        x_in = sem("a_x_in")
        x_free = sem("a_x_free")
        stats_ready = sem("a_stats_ready")
        std_ready = sem("a_std_ready")
        xT_done = sem("a_xT_done")
        xnT_ready = sem("a_xnT_ready")
        xn_out = sem("a_xn_out")
        scattered = ctx.enter_context(nc.semaphore("a_scattered"))
        scatter_free = sem("a_scatter_free")
        both_ready = sem("a_both_ready")
        ranked = sem("a_ranked")
        slot_ready = sem("a_slot_ready")
        consts = sem("a_consts")
        tail_ready = sem("a_tail_ready")
        tail_out = sem("a_tail_out")
        gate_t = sem("a_gate_t")
        gateT_ready = sem("a_gateT_ready")
        qk_done = sem("a_qk_done")
        qf_ready = [sem(f"a_qf_ready{s}") for s in range(2)]
        parts_ready = [sem(f"a_parts_ready{s}") for s in range(2)]
        parts_out = [sem(f"a_parts_out{s}") for s in range(2)]
        v_done = sem("a_v_done")
        v_free = sem("a_v_free")
        l_done = sem("a_l_done")
        sig_ready = sem("a_sig_ready")
        dchain = sem("a_dchain")
        pchain = sem("a_pchain")
        iota_ready = sem("a_iota_ready")

        block = ctx.enter_context(nc.Block())
        CH = 52

        @block.sync
        def _(sp):
            for s in sems:
                sp.sem_inc(s, CREDIT)
            sp.dma_start(wqkv[:], io["w_attn"].rearrange("(k p) n -> p k n", p=P)).then_inc(w_in, 16)
            sp.dma_start(gate_rows[:], io["gate_w"]).then_inc(w_in, 16)
            sp.dma_start(beta[:], io["beta"].partition_broadcast(P)).then_inc(w_in, 16)
            x_blk = io["x"].rearrange("(n j p) d -> n p j d", p=P, j=TPB)
            sp.dma_start(x[:], x_blk[0]).then_inc(x_in, 16)

            def stores(b, q):
                blk = b * BPB + q
                for f in range(4):
                    sp.wait_ge(parts_ready[f % 2], 2 * blk + f // 2 + 1 + CREDIT)
                    maps = slice(f % 2 * HEADS, (f % 2 + 1) * HEADS)
                    if f < 2:
                        for x in range(3):
                            sp.dma_start(dram["q"][b, maps, x, :, bass.ds(q * BLK, BLK)], parts[:, f % 2, x])\
                              .then_inc(parts_out[f % 2], 16)
                    else:
                        sp.dma_start(dram["k"][b, maps, :, :, bass.ds(q * BLK, BLK)]
                                     .rearrange("n d x t -> (n d) x t"), parts[:, f % 2]).then_inc(parts_out[f % 2], 16)

            with sp.Fori(0, BATCH) as b:
                with sp.Fori(0, BPB) as q:
                    blk = b * BPB + q
                    sp.wait_ge(x_free, blk + 1 + CREDIT)
                    sp.dma_start(dram["rows"][bass.ds(blk * BLK + E * REG, BLK), :]
                                 .rearrange("(j p) d -> p j d", p=P), xn[:]).then_inc(xn_out, 16)
                    sp.dma_start(x[:], io["x"][bass.ds((blk + 1) % NBLK * BLK, BLK), :]
                                 .rearrange("(j p) d -> p j d", p=P)).then_inc(x_in, 16)
                    stores(b, q)
            sp.wait_ge(x_in, 16 * NBLK + 16 + CREDIT)
            for s in range(2):
                sp.wait_ge(parts_out[s], 64 * NBLK + CREDIT)
            sp.wait_ge(xn_out, 16 * NBLK + CREDIT)
            sp.wait_ge(tail_ready, 1 + CREDIT)
            for e in range(E):
                row = sp.value_load(tail[0:1, e:e + 1], min_val=e * REG, max_val=e * REG + N)
                sp.dma_start(dram["rows"][bass.ds(row, P), :], zeros[:]).then_inc(tail_out, 16)
            sp.wait_ge(tail_out, 16 * E + CREDIT)

        @block.gpsimd
        def _(pool):
            c = Chain(pool, pchain)
            c.after(pool.memset(keep["ident"][:], 0.0))
            c.after(pool.affine_select(out=keep["ident"][:], in_=keep["ident"][:], compare_op=ALU.not_equal, fill=1.0,
                                       base=0, pattern=[[-1, P]], channel_multiplier=1))
            c.mark(pool.iota(iota_u[:, 0:E], pattern=[[1, E]], base=0, channel_multiplier=0))
            c.mark(pool.iota(iota_u[:, E:E + NT], pattern=[[P, NT]], base=0, channel_multiplier=0))
            c.mark(pool.iota(iota_u[:, E + NT:], pattern=[[1, TT]], base=0, channel_multiplier=0))
            c.wait()
            pool.tensor_copy(iota_f[:], iota_u[:]).then_inc(iota_ready, 1)
            c.mark(pool.memset(zeros[:], 0.0))
            c.mark(pool.memset(pcarry[:], 0.0))
            c.mark(pool.memset(before[:], 1.0))
            c.after(pool.memset(ones[:], 1.0))
            pool.affine_select(out=before[:], in_=before[:], compare_op=ALU.is_gt, fill=0.0, base=0,
                               pattern=[[1, P]], channel_multiplier=-1).then_inc(consts, 1)
            with pool.Fori(0, NBLK) as blk:
                pool.wait_ge(slot_ready, blk + 1 + CREDIT)
                pool.tensor_tensor(pcarry[:, 0:1], pcarry[:, 0:1], pcarry[:, 0:1], ALU.mult)
                for k in range(2):
                    for j in range(TPB):
                        pool.indirect_dma_start(dram["rows"], bass.IndirectOffsetOnAxis(slot[:, k, j:j + 1], 0),
                                                xn[:, j, :], None).then_inc(scattered, 16)
                pool.wait_ge(scattered, 16 * 2 * TPB * (blk + 1))
                pool.tensor_tensor(pcarry[:, 1:2], pcarry[:, 1:2], pcarry[:, 1:2], ALU.mult).then_inc(scatter_free, 1)

        @block.vector
        def _(dve):
            c = Chain(dve, dchain, CH)
            dve.wait_ge(iota_ready, 1 + CREDIT)
            dve.wait_ge(w_in, 48 + CREDIT)
            c.mark(dve.tensor_scalar(region[:], iota_e, float(REG), None, ALU.mult))
            c.after(dve.memset(seen[:], 0.0))
            with dve.Fori(0, NBLK) as blk:
                c.turn(2 + blk * CH)
                dve.wait_ge(x_in, 16 * blk + 16 + CREDIT)
                for j in range(TPB):
                    c.mark(dve.bn_stats(stats[:, j, :], x[:, j, :]))
                c.wait()
                c.mark(dve.memset(carrier[:, 0:1], 0.0))
                for j in range(TPB):
                    c.mark(dve.bn_aggr(mv[:, j, :], stats[:, j, :]))
                c.wait()
                dve.tensor_scalar(rstd[:], mv[:, :, 1], EPS, None, ALU.add).then_inc(stats_ready, 1)
                dve.wait_ge(std_ready, blk + 1 + CREDIT)
                c.after(dve.reciprocal(rstd[:], std[:]))
                dve.wait_ge(xT_done, blk + CREDIT)
                dve.wait_ge(xn_out, 16 * blk + CREDIT)
                dve.wait_ge(scatter_free, blk + CREDIT)
                for j in range(TPB):
                    ins = dve.tensor_scalar(xn[:, j, :], x[:, j, :], mv[:, j, 0:1], rstd[:, j:j + 1],
                                            ALU.subtract, ALU.mult)
                ins.then_inc(x_free, 1)
                dve.wait_ge(l_done, blk + 1 + CREDIT)
                dve.wait_ge(sig_ready, blk + 1 + CREDIT)
                dve.wait_ge(x_free, blk + 1 + CREDIT)
                c.after(dve.tensor_tensor(sel[:], psL[:], beta[:].unsqueeze(1).to_broadcast([P, TPB, E]), ALU.add))
                c.mark(dve.memset(carrier[:, 1:2], 0.0))
                for j in range(TPB):
                    c.mark(dve.max(top[:, j, :], sel[:, j, :]))
                c.wait()
                c.mark(dve.memset(carrier[:, 2:3], 0.0))
                for j in range(TPB):
                    c.mark(dve.max_index(topi[:, j, :], top[:, j, :], sel[:, j, :]))
                c.wait()
                c.after(dve.tensor_copy(topf[:], topi[:]))
                c.mark(dve.tensor_copy(seen[:, 0], seen[:, TPB]))
                for k in range(2):
                    c.mark(dve.tensor_tensor(hot[:, k], iota_e.unsqueeze(1).to_broadcast([P, TPB, E]),
                                             topf[:, :, k:k + 1].to_broadcast([P, TPB, E]), ALU.is_equal))
                c.wait()
                c.mark(dve.tensor_copy(keep["hot"][:, bass.ds(blk, 1)].rearrange("p o k j e -> p (o k j e)"),
                                       hot[:].rearrange("p k j e -> p (k j e)")))
                c.after(dve.tensor_tensor(both[:], hot[:, 0], hot[:, 1], ALU.add))
                for j in range(TPB):
                    ins = dve.tensor_tensor(seen[:, j + 1], seen[:, j], both[:, j], ALU.add)
                    if j < TPB - 1:
                        c.after(ins)
                ins.then_inc(both_ready, 1)

                def cut(f):
                    s = f % 2
                    dve.wait_ge(qf_ready[s], 2 * blk + f // 2 + 1 + CREDIT)
                    dve.wait_ge(parts_out[s], 64 * blk + f // 2 * 48 + CREDIT)
                    c.after(dve.tensor_copy(parts[:, s, 0], qf[:, s]))
                    c.after(dve.tensor_tensor(rest[:, 0], qf[:, s], parts[:, s, 0], ALU.subtract))
                    c.after(dve.tensor_copy(parts[:, s, 1], rest[:, 0]))
                    c.after(dve.tensor_tensor(rest[:, 1], rest[:, 0], parts[:, s, 1], ALU.subtract))
                    dve.tensor_copy(parts[:, s, 2], rest[:, 1]).then_inc(parts_ready[s], 1)

                cut(0)
                dve.wait_ge(ranked, blk + 1 + CREDIT)
                c.after(dve.tensor_tensor(place[:], psK[:], region[:].unsqueeze(1).to_broadcast([P, TPB, E]), ALU.add))
                for w, src in enumerate((place, sig)):
                    c.mark(dve.tensor_tensor(pick[:, w].rearrange("p k j e -> p k (j e)"),
                                             hot[:].rearrange("p k j e -> p k (j e)"),
                                             src[:].rearrange("p j e -> p (j e)").unsqueeze(1)
                                             .to_broadcast([P, 2, TPB * E]), ALU.mult))
                c.wait()
                c.after(dve.tensor_reduce(picked[:].rearrange("p w k j -> p (w k j)"),
                                          pick[:].rearrange("p w k j e -> p (w k j) e"), AX.X, ALU.add))
                c.mark(dve.tensor_copy(keep["slot"][:, bass.ds(blk, 1), :], picked[:, 0].rearrange("p k j -> p (k j)")
                                       .unsqueeze(1)))
                c.mark(dve.tensor_copy(keep["c"][:, bass.ds(blk, 1), :], picked[:, 1].rearrange("p k j -> p (k j)")
                                       .unsqueeze(1)))
                dve.wait_ge(scatter_free, blk + CREDIT)
                dve.tensor_copy(slot[:], picked[:, 0]).then_inc(slot_ready, 1)
                dve.wait_ge(slot_ready, blk + 1 + CREDIT)
                cut(1)
                cut(2)
                cut(3)
                c.end()


            c.turn(2 + NBLK * CH)
            dve.wait_ge(ranked, NBLK + 1 + CREDIT)
            c.after(dve.tensor_copy(count[:], psK[:, 0]))
            c.mark(dve.tensor_tensor(tail_f[:], count[:], region[:], ALU.add))
            c.mark(dve.tensor_tensor(wide[:, :, 0:NT], count[:].unsqueeze(2).to_broadcast([P, E, NT]),
                                     iota_m.unsqueeze(1).to_broadcast([P, E, NT]), ALU.is_gt))
            c.wait()
            dve.tensor_copy(tail[:], tail_f[:]).then_inc(tail_ready, 1)
            c.after(dve.tensor_reduce(tiles[:], wide[:, :, 0:NT], AX.X, ALU.add))
            c.after(dve.tensor_tensor(wide[:, :, 0:E], iota_e.unsqueeze(1).to_broadcast([P, E, E]),
                                      iota_e.unsqueeze(2).to_broadcast([P, E, E]), ALU.is_le))
            c.after(dve.tensor_tensor(wide2[:, :, 0:E], wide[:, :, 0:E], tiles[:].unsqueeze(1).to_broadcast([P, E, E]),
                                      ALU.mult))
            c.after(dve.tensor_reduce(ends[:], wide2[:, :, 0:E], AX.X, ALU.add))
            c.after(dve.tensor_tensor(starts[:], ends[:], tiles[:], ALU.subtract))
            c.after(dve.scalar_tensor_tensor(out=shift[:], in0=starts[:], scalar=-float(P), in1=region[:],
                                             op0=ALU.mult, op1=ALU.add))
            routed = iota_t[:, 0:RT].unsqueeze(1).to_broadcast([P, E, RT])
            c.mark(dve.tensor_tensor(wide[:], routed, starts[:].unsqueeze(2).to_broadcast([P, E, RT]), ALU.is_ge))
            c.mark(dve.tensor_tensor(wide2[:], routed, ends[:].unsqueeze(2).to_broadcast([P, E, RT]), ALU.is_lt))
            c.wait()
            c.after(dve.tensor_tensor(wide[:], wide[:], wide2[:], ALU.mult))
            c.after(dve.tensor_tensor(wide2[:], wide[:], iota_e.unsqueeze(2).to_broadcast([P, E, RT]), ALU.mult))
            c.after(dve.tensor_reduce(table_f[:, 0, NT:TT], wide2[:].rearrange("p e t -> p t e"), AX.X, ALU.add))
            c.after(dve.scalar_tensor_tensor(out=wide2[:], in0=routed, scalar=float(P),
                                             in1=shift[:].unsqueeze(2).to_broadcast([P, E, RT]),
                                             op0=ALU.mult, op1=ALU.add))
            c.after(dve.tensor_tensor(wide2[:], wide[:], wide2[:], ALU.mult))
            c.mark(dve.tensor_reduce(table_f[:, 1, NT:TT], wide2[:].rearrange("p e t -> p t e"), AX.X, ALU.add))
            c.mark(dve.memset(table_f[:, 0, 0:NT], float(E)))
            c.mark(dve.tensor_scalar(table_f[:, 1, 0:NT], iota_m, float(E * REG), None, ALU.add))
            c.wait()
            c.mark(dve.tensor_copy(keep["table"][:], table_f[:]))
            pickall = keep["hot"][:].rearrange("p b k j e -> p (b k j) e")
            c.after(dve.tensor_tensor(keep["hot"][:].rearrange("p b k j e -> p (b k j) e"), pickall,
                                      shift[:].unsqueeze(1).to_broadcast([P, 2 * NT, E]), ALU.mult))
            c.after(dve.tensor_reduce(yshift[:], pickall, AX.X, ALU.add))
            c.after(dve.tensor_tensor(yslot_f[:], keep["slot"][:].rearrange("p b k -> p (b k)"), yshift[:],
                                      ALU.subtract))
            c.after(dve.tensor_scalar(keep["yslot"][:].rearrange("p b k -> p (b k)"), yslot_f[:], float(N), None,
                                      ALU.add))

        @block.scalar
        def _(act):
            for e in range(NE):
                g = io["gate_proj"][e] if e < E else io["shared_gate"][0]
                u = io["up_proj"][e] if e < E else io["shared_up"][0]
                d = io["down_proj"][e] if e < E else io["shared_down"][0]
                act.dma_start(keep["wg"][:, e], g.rearrange("(k p) m -> p k m", p=P)).then_inc(keep["moe_w"], 16)
                act.dma_start(keep["wu"][:, e], u.rearrange("(k p) m -> p k m", p=P)).then_inc(keep["moe_w"], 16)
                act.dma_start(keep["wd"][:, e], d.rearrange("(k p) m -> p k m", p=P)).then_inc(keep["moe_w"], 16)
            act.wait_ge(gate_t, 1 + CREDIT)
            act.copy(gateT[:].rearrange("p k e -> p (k e)"), psL[:, 0:KD, :].rearrange("p k e -> p (k e)"))\
               .then_inc(gateT_ready, 1)
            with act.Fori(0, BATCH) as b:
                with act.Fori(0, BPB) as q:
                    blk = b * BPB + q
                    act.wait_ge(stats_ready, blk + 1 + CREDIT)
                    act.activation(std[:], rstd[:], ACT.Sqrt).then_inc(std_ready, 1)
                    act.wait_ge(xT_done, blk + 1 + CREDIT)
                    act.wait_ge(v_done, blk + CREDIT)
                    act.wait_ge(l_done, blk + CREDIT)
                    for k in range(KD):
                        ins = act.copy(xnT[:, k], psT[:, k])
                    ins.then_inc(xnT_ready, 1)
                    act.wait_ge(l_done, blk + 1 + CREDIT)
                    act.wait_ge(slot_ready, blk + CREDIT)
                    act.activation(sig[:], psL[:], ACT.Sigmoid).then_inc(sig_ready, 1)
                    for f in range(4):
                        s = f % 2
                        act.wait_ge(qk_done, 4 * blk + f + 1 + CREDIT)
                        act.wait_ge(parts_ready[s], 2 * blk + f // 2 + CREDIT)
                        act.activation(qf[:, s], psQ[:, s], ACT.Copy, scale=(1.0 / HD if f < 2 else 1.0))\
                           .then_inc(qf_ready[s], 1)
                    act.wait_ge(v_done, blk + 1 + CREDIT)
                    act.copy(keep["v"][:, b, :, bass.ds(q * TPB, TPB), :].rearrange("p h j d -> p j h d"),
                             psV[:].rearrange("p j (h d) -> p j h d", h=HEADS)).then_inc(v_free, 1)

        @block.tensor
        def _(pe):
            pe.wait_ge(w_in, 48 + CREDIT)
            pe.wait_ge(consts, 1 + CREDIT)
            for k in range(KD):
                ins = pe.transpose(psL[:, k, :], gate_rows[:, k * P:(k + 1) * P], keep["ident"][0:E, 0:E])
            ins.then_inc(gate_t, 1)
            pe.wait_ge(gateT_ready, 1 + CREDIT)
            with pe.Fori(0, NBLK) as blk:
                pe.wait_ge(x_free, blk + 1 + CREDIT)
                pe.wait_ge(xnT_ready, blk + CREDIT)
                for j in range(TPB):
                    for k in range(KD):
                        ins = pe.transpose(psT[:, k, j * P:(j + 1) * P], xn[:, j, k * P:(k + 1) * P], keep["ident"][:])
                ins.then_inc(xT_done, 1)
                pe.wait_ge(xnT_ready, blk + 1 + CREDIT)
                pe.wait_ge(both_ready, blk + CREDIT)
                for j in range(TPB):
                    for k in range(KD):
                        ins = pe.matmul(psL[:, j], xnT[:, k, j * P:(j + 1) * P], gateT[:, k],
                                        start=(k == 0), stop=(k == KD - 1))
                ins.then_inc(l_done, 1)

                def qk(f):
                    s = f % 2
                    pe.wait_ge(qf_ready[s], 2 * blk + f // 2 + CREDIT)
                    for k in range(KD):
                        ins = pe.matmul(psQ[:, s], wqkv[:, k, f * P:(f + 1) * P], xnT[:, k],
                                        start=(k == 0), stop=(k == KD - 1))
                    ins.then_inc(qk_done, 1)

                qk(0)
                qk(1)
                pe.wait_ge(both_ready, blk + 1 + CREDIT)
                pe.wait_ge(slot_ready, blk + CREDIT)
                pe.matmul(psK[:].rearrange("p j e -> p (j e)"), before[:], both[:].rearrange("p j e -> p (j e)"),
                          start=True, stop=False)
                pe.matmul(psK[:].rearrange("p j e -> p (j e)"), ones[:],
                          seen[:, 0:TPB].rearrange("p j e -> p (j e)"), start=False, stop=True).then_inc(ranked, 1)
                qk(2)
                qk(3)
                pe.wait_ge(v_free, blk + CREDIT)
                for j in range(TPB):
                    for k in range(KD):
                        ins = pe.matmul(psV[:, j], xnT[:, k, j * P:(j + 1) * P], wqkv[:, k, 2 * D:3 * D],
                                        start=(k == 0), stop=(k == KD - 1))
                ins.then_inc(v_done, 1)
            pe.wait_ge(slot_ready, NBLK + CREDIT)
            pe.matmul(psK[:, 0], ones[:], seen[:, TPB], start=True, stop=True).then_inc(ranked, 1)


def phase_experts(nc, io, keep, dram):
    with ExitStack() as ctx:
        sb = lambda name, shape, dt=F32: ctx.enter_context(nc.sbuf_tensor(name, shape, dt))
        ps = lambda name, shape, dt=F32: ctx.enter_context(nc.psum_tensor(name, shape, dt))
        sems = []
        sem = lambda name: credited(ctx, nc, sems, name)
        MT = M // P

        x = sb("x_e", [P, 2, D])
        xT = sb("xT_e", [P, 2, KD, P])
        sg = sb("sg", [P, 2, M])
        h = sb("h", [P, 2, M])
        hT = sb("hT", [P, 2, MT, P])
        y = sb("y", [P, 2, D])
        psG = ps("psG", [P, 2, M])
        psU = ps("psU", [P, 2, M])
        psH = ps("psH", [P, 2, MT, P])
        psX = ps("psX", [P, KD, P])
        psY = ps("psY", [P, D])

        x_in = [sem(f"m_x_in{s}") for s in range(2)]
        x_turned = sem("m_x_turned")
        xT_ready = sem("m_xT_ready")
        gu_done, sg_ready, h_ready = sem("m_gu_done"), sem("m_sg_ready"), sem("m_h_ready")
        h_turned, hT_ready = sem("m_h_turned"), sem("m_hT_ready")
        d_done, y_ready = sem("m_d_done"), sem("m_y_ready")
        y_out = [sem(f"m_y_out{s}") for s in range(2)]
        block = ctx.enter_context(nc.Block())

        def steps(eng, step, first, last):
            lo, hi = 4, TT - 2
            for i in range(first, lo):
                step(i, i % 2)
            with eng.Fori(0, (hi - lo) // 2) as j:
                for s in range(2):
                    step(2 * j + lo + s, s)
            for i in range(hi, last + 1):
                step(i, i % 2)

        def known(i, lo, hi=TT):
            return not isinstance(i, int) or lo <= i < hi

        def at(table, i):
            return table[:, i:i + 1] if isinstance(i, int) else table[:, bass.ds(i, 1)]

        def half(i, s):
            return (i - s) // 2

        @block.sync
        def _(sp):
            for s in sems:
                sp.sem_inc(s, CREDIT)
            def load(i, s):
                row = sp.value_load(at(keep["table"][0:1, 1], i), min_val=0, max_val=E * REG + N - P)
                if known(i, 2):
                    sp.wait_ge(x_turned, i - 1 + CREDIT)
                sp.dma_start(x[:, s], dram["rows"][bass.ds(row, P), :]).then_inc(x_in[s], 16)

            def store(i, s):
                sp.wait_ge(y_ready, i + 1 + CREDIT)
                rows = slice(i * P, (i + 1) * P) if isinstance(i, int) else bass.ds(i * P, P)
                sp.dma_start(dram["y"][rows, :], y[:, s]).then_inc(y_out[s], 16)

            def step(i, s):
                if known(i + 1, 0):
                    load(i + 1, 1 - s)
                if known(i - 4, 0):
                    store(i - 4, s)
            steps(sp, step, -1, TT + 3)
            for s in range(2):
                sp.wait_ge(y_out[s], 16 * (TT // 2) + CREDIT)

        @block.scalar
        def _(act):
            def step(i, s):
                if known(i, 0):
                    act.wait_ge(gu_done, i + 1 + CREDIT)
                    if known(i, 2):
                        act.wait_ge(h_ready, i - 1 + CREDIT)
                    act.activation(sg[:, s], psG[:, s], ACT.Silu).then_inc(sg_ready, 1)
                if known(i - 1, 0):
                    act.wait_ge(h_turned, i + CREDIT)
                    if known(i - 1, 2):
                        act.wait_ge(d_done, i - 2 + CREDIT)
                    act.copy(hT[:, 1 - s].rearrange("p m t -> p (m t)"), psH[:, 1 - s].rearrange("p m t -> p (m t)"))\
                       .then_inc(hT_ready, 1)
            steps(act, step, 0, TT)

        @block.vector
        def _(dve):
            def step(i, s):
                if known(i + 1, 0):
                    dve.wait_ge(x_turned, i + 2 + CREDIT)
                    if known(i + 1, 2):
                        dve.wait_ge(gu_done, i + CREDIT)
                    dve.tensor_copy(xT[:, 1 - s], psX[:]).then_inc(xT_ready, 1)
                if known(i, 0):
                    dve.wait_ge(sg_ready, i + 1 + CREDIT)
                    if known(i, 2):
                        dve.wait_ge(h_turned, i - 1 + CREDIT)
                    dve.tensor_tensor(h[:, s], sg[:, s], psU[:, s], ALU.mult).then_inc(h_ready, 1)
                if known(i - 2, 0):
                    dve.wait_ge(d_done, i - 1 + CREDIT)
                    if known(i - 2, 2):
                        dve.wait_ge(y_out[s], 16 * half(i - 2, s) + CREDIT)
                    dve.tensor_copy(y[:, s], psY[:]).then_inc(y_ready, 1)
            steps(dve, step, -1, TT + 1)

        @block.tensor
        def _(pe):
            pe.wait_ge(keep["moe_w"], 16 * 3 * NE)

            def turn_x(i, s):
                pe.wait_ge(x_in[s], 16 * half(i, s) + 16 + CREDIT)
                if known(i, 1):
                    pe.wait_ge(xT_ready, i + CREDIT)
                for k in range(KD):
                    ins = pe.transpose(psX[:, k], x[:, s, k * P:(k + 1) * P], keep["ident"][:])
                ins.then_inc(x_turned, 1)

            def step(i, s):
                if known(i, 0):
                    e = pe.value_load(at(keep["table"][0:1, 0], i), min_val=0, max_val=E)
                    pe.wait_ge(xT_ready, i + 1 + CREDIT)
                    if known(i, 2):
                        pe.wait_ge(h_ready, i - 1 + CREDIT)
                    for w, dst in ((keep["wg"], psG), (keep["wu"], psU)):
                        for k in range(KD):
                            ins = pe.matmul(dst[:, s], xT[:, s, k], w[:, bass.ds(e, 1), k].rearrange("p o m -> p (o m)"),
                                            start=(k == 0), stop=(k == KD - 1))
                    ins.then_inc(gu_done, 1)
                if known(i + 1, 0):
                    turn_x(i + 1, 1 - s)
                if known(i - 2, 0):
                    e = pe.value_load(at(keep["table"][0:1, 0], i - 2), min_val=0, max_val=E)
                    pe.wait_ge(hT_ready, i - 1 + CREDIT)
                    if known(i - 2, 1):
                        pe.wait_ge(y_ready, i - 2 + CREDIT)
                    for m in range(MT):
                        ins = pe.matmul(psY[:], hT[:, s, m], keep["wd"][:, bass.ds(e, 1), m].rearrange("p o d -> p (o d)"),
                                        start=(m == 0), stop=(m == MT - 1))
                    ins.then_inc(d_done, 1)
                if known(i - 1, 0):
                    pe.wait_ge(h_ready, i + CREDIT)
                    if known(i - 1, 2):
                        pe.wait_ge(hT_ready, i - 2 + CREDIT)
                    for m in range(MT):
                        ins = pe.transpose(psH[:, 1 - s, m], h[:, 1 - s, m * P:(m + 1) * P], keep["ident"][:])
                    ins.then_inc(h_turned, 1)
            steps(pe, step, -1, TT + 1)


def score_steps():
    out = []
    for c in range(BPB):
        for st in range(TPB * c + TPB):
            r = st - TPB * c
            first = c == 0 and st == 1
            out.append((c, st, 0 if r < 0 or first else P * r, first))
    return out


def max_units():
    return [(a, i, ch, min(BLK, P * (i + 1) - BLK * ch))
            for a in range(2) for i in range(ST_T) for ch in range(i // TPB + 1)]


def phase_attention(nc, io, keep, dram):
    with ExitStack() as ctx:
        sb = lambda name, shape, dt=F32: ctx.enter_context(nc.sbuf_tensor(name, shape, dt))
        ps = lambda name, shape, dt=F32: ctx.enter_context(nc.psum_tensor(name, shape, dt))
        sems = []
        sem = lambda name: credited(ctx, nc, sems, name)

        STEPS, UNITS = score_steps(), max_units()
        NSTEP, NUNIT = len(STEPS), len(UNITS)
        BUFS = 8
        SLOTS = 4
        assert NSTEP % BUFS == 0 and BUFS == 2 * SLOTS
        LAST = [max(k for k, s in enumerate(STEPS) if s[0] == c) for c in range(BPB)]
        FIRST_U, LAST_U = 1, 36
        RING_CUTS = ((1, 2), (0, 1))
        ISSUE = 400
        LAG = 6
        EVAC = LAG + 1
        K_MAX, MROW = 96, 96
        RING_HEAD = NUNIT + 1 + BPB

        kslabs = sb("kslabs", [P, 2, 2, T], BF16)
        qslabs = sb("qslabs", [P, 2, 2, T], BF16)
        kslab = [[kslabs[:, u, a] for a in range(2)] for u in range(2)]
        qslab = [[qslabs[:, u, a] for a in range(2)] for u in range(2)]
        vaug = [sb(f"vaug{u}", [P, ST_T, VW]) for u in range(2)]
        prob = [sb(f"prob{s}", [P, 2, BLK]) for s in range(BUFS)]
        pmax = sb("pmax", [P, 2 * ST_T, BPB])
        nmax = sb("nmax", [P, 2 * ST_T])
        mrest = sb("mrest", [2 * ST_T, 2, P])
        mpart = sb("mpart", [2 * ST_T, 3, P], BF16)
        ident_b = sb("ident_b", [P, P], BF16)
        mask_q = sb("mask_q", [P, P], BF16)
        mask_k = sb("mask_k", [P, 2 * P], BF16)
        fold = sb("fold", [P, 2, OC])
        ov = [sb(f"ov{s}", [P, BLK]) for s in range(2)]
        o = sb("o_head", [P, ST_T, 2, OC])
        rs = sb("rs", [P, ST_T, 2])
        rl = sb("rl", [P, ST_T])
        o1 = sb("o1", [P, ST_T, VD])
        o2 = sb("o2", [P, ST_T, VD])
        lam_in = sb("lam_in", [P, 4, HD])
        lam_w = sb("lam_w", [P, 2, HD])
        lam_s = sb("lam_s", [P, 2])
        lam_e = sb("lam_e", [P, 2])
        lam = sb("lam", [P, 2])

        psS = [ps(f"psS{s}", [P, 2, BLK]) for s in range(2)]
        psR = [ps(f"psR{s}", [P, BLK]) for s in range(2)]
        psV = [ps(f"psVo{s}", [P, BLK]) for s in range(2)]

        lam_load = sem("b_lam_load")
        lam_step = sem("b_lam_step")
        lam_exp = sem("b_lam_exp")
        lam_ready = sem("b_lam_ready")
        masks = sem("b_masks")
        slab_in = [[sem(f"b_slab_in{u}{a}") for a in range(2)] for u in range(2)]
        mrow_in = sem("b_mrow_in")
        scores_done = sem("b_scores_done")
        prob_ready = [sem(f"b_prob_ready{s}") for s in range(SLOTS)]
        pv_done = [sem(f"b_pv_done{s}") for s in range(SLOTS)]
        ov_ready = [sem(f"b_ov_ready{s}") for s in range(2)]
        ring_full = sem("b_ring_full")
        ring_free = sem("b_ring_free")
        nmax_ready = sem("b_nmax_ready")
        mpart_ready = sem("b_mpart_ready")
        dchain = sem("b_dchain")
        rs_ready = sem("b_rs_ready")
        pchain = sem("b_pchain")
        setup = sem("b_setup")
        v_ready = sem("b_v_ready")
        post_done = sem("b_post_done")
        block = ctx.enter_context(nc.Block())

        q_rows = dram["q"].rearrange("b n x d t -> (b n) (x d) t")
        k_rows = dram["k"].rearrange("b n d x t -> (b n) (d x) t")

        def spread_units():
            spans = [2 * (BLK - off) + ISSUE if FIRST_U <= k <= LAST_U else 0 for k, (c, st, off, w) in enumerate(STEPS)]
            costs = [w + ISSUE // 2 for a, i, ch, w in UNITS]
            per_step, done, k = [[] for _ in range(NSTEP + 1)], 0, 0
            for unit, cost in zip(UNITS, costs):
                middle = (done + cost / 2) * sum(spans) / sum(costs)
                while sum(spans[:k + 1]) < middle:
                    k += 1
                per_step[k].append(unit)
                done += cost
            return per_step

        UNITS_AT = spread_units()

        def ring_at(k, more):
            out = [("max", n) for n in UNITS_AT[k]] if more else []
            out += [("fold", c) for c in range(BPB) if LAST[c] + EVAC + 1 == k or (k == NSTEP and c == BPB - 1)]
            if more and k == LAST_U + 2:
                out.append(("turn", None))
            return out

        def ring_base(n):
            return NUNIT + 1 + RING_HEAD * n

        def heads(eng, turn):
            with eng.Fori(0, NH // 2 - 1) as j:
                for u in range(2):
                    turn(2 * j + u, u, True)
            turn(NH - 2, 0, True)
            turn(NH - 1, 1, False)

        @block.sync
        def _(sp):
            for s in sems:
                sp.sem_inc(s, CREDIT)
            for w, name in enumerate(("lq1", "lk1", "lq2", "lk2")):
                sp.dma_start(lam_in[:, w, :], io[name].partition_broadcast(P)).then_inc(lam_load, 16)
            sp.wait_ge(setup, 2 + CREDIT)

            def load(n, u):
                for a in range(2):
                    row = slice(2 * n + a, 2 * n + a + 1) if isinstance(n, int) else bass.ds(n * 2 + a, 1)
                    sp.dma_start(qslab[u][a][0:KQ, :], q_rows[row].rearrange("o r t -> (o r) t").unsqueeze(1)
                                 .to_broadcast([3 * HD, 3, T])).then_inc(slab_in[u][a], 16)
                    sp.dma_start(kslab[u][a][0:KQ, :], k_rows[row].rearrange("o r t -> (o r) t")
                                 .partition_broadcast(3)).then_inc(slab_in[u][a], 16)

            def maxima(n, u):
                sp.wait_ge(mpart_ready, n + 1 + CREDIT)
                for a in range(2):
                    for x in range(3):
                        sp.dma_start(qslab[u][a][MROW + x:MROW + x + 1, :].rearrange("o (i t) -> o i t", t=P),
                                     mpart[a * ST_T:(a + 1) * ST_T, x, :]).then_inc(mrow_in, 16)

            load(0, 0)
            maxima(0, 0)

            def turn(n, u, more):
                if more:
                    sp.wait_ge(scores_done, NSTEP * n + CREDIT)
                    load(n + 1, 1 - u)
                    maxima(n + 1, 1 - u)
            heads(sp, turn)

        @block.gpsimd
        def _(pool):
            c = Chain(pool, masks)
            c.after(pool.memset(kslabs[MROW:P], 1.0))
            c.mark(pool.memset(ident_b[:], 0.0))
            c.mark(pool.memset(mask_q[:], 0.0))
            c.mark(pool.memset(mask_k[:, 0:P], NEG))
            c.mark(pool.memset(mask_k[:, P:2 * P], 0.0))
            c.mark(pool.memset(fold[:], 0.0))
            c.wait()
            c.mark(pool.affine_select(out=ident_b[:], in_=ident_b[:], compare_op=ALU.not_equal, fill=1.0, base=0,
                                      pattern=[[-1, P]], channel_multiplier=1))
            c.mark(pool.affine_select(out=mask_q[:], in_=mask_q[:], compare_op=ALU.is_ge, fill=NEG, base=0,
                                      pattern=[[-1, P]], channel_multiplier=1))
            c.mark(pool.affine_select(out=mask_k[:, P:2 * P], in_=mask_k[:, P:2 * P], compare_op=ALU.is_ge, fill=NEG,
                                      base=0, pattern=[[1, P]], channel_multiplier=-1))
            for odd in range(2):
                c.after(pool.affine_select(out=fold[:], in_=fold[:], compare_op=ALU.not_equal, fill=1.0,
                                           base=-VW * odd, pattern=[[-2 * VW, 2], [-1, OC]], channel_multiplier=1))
            pool.wait_ge(setup, 1 + CREDIT)

            def values(n, u):
                pool.tensor_copy(vaug[u][:, :, 0:VD], v_rows[:, bass.ds(n, 1)].rearrange("p o s d -> p (o s) d"))\
                    .then_inc(v_ready, 1)

            v_rows = keep["v"][:].rearrange("p b h s d -> p (b h) s d")
            values(0, 0)
            pool.wait_ge(lam_ready, 1 + CREDIT)

            def turn(n, u, more):
                if more:
                    for s in range(SLOTS):
                        pool.wait_ge(pv_done[s], (NSTEP // SLOTS) * n + CREDIT)
                    values(n + 1, 1 - u)
                pool.wait_ge(rs_ready, n + 1 + CREDIT)
                p = Chain(pool, pchain)
                p.turn(2 * n)
                pool.wait_ge(post_done, n + CREDIT)
                p.mark(pool.tensor_tensor(o1[:], o[:, :, 0, 0:VD], rs[:, :, 0:1].to_broadcast([P, ST_T, VD]), ALU.mult))
                p.after(pool.tensor_tensor(o2[:], o[:, :, 1, 0:VD], rl[:].unsqueeze(2).to_broadcast([P, ST_T, VD]),
                                           ALU.mult))
                pool.tensor_tensor(keep["o"][:, bass.ds(n, 1)].rearrange("p o s d -> p (o s) d"), o1[:], o2[:],
                                   ALU.subtract).then_inc(post_done, 1)
            heads(pool, turn)

        @block.scalar
        def _(act):
            act.wait_ge(lam_step, 2 + CREDIT)
            act.activation(lam_e[:], lam_s[:], ACT.Exp).then_inc(lam_exp, 1)

            def turn(n, u, more):
                for k in range(NSTEP):
                    off, s = STEPS[k][2], k % SLOTS
                    act.wait_ge(scores_done, NSTEP * n + k + 1 + CREDIT)
                    act.wait_ge(pv_done[s], (NSTEP // SLOTS) * n + max(k // SLOTS - 1, 0) + CREDIT)
                    act.activation(prob[k % BUFS][:, :, off:BLK], psS[k % 2][:, :, off:BLK], ACT.Exp)\
                       .then_inc(prob_ready[s], 1)
                    for c in range(BPB - 1):
                        if LAST[c] + EVAC == k:
                            copy_sum(n, c, more)
                copy_sum(n, BPB - 1, more)

            def copy_sum(n, c, more):
                order = [x for k in range(NSTEP + 1) for x in ring_at(k, more)]
                k = LAST[c]
                for q in (k - 1, k):
                    act.wait_ge(pv_done[q % SLOTS], (NSTEP // SLOTS) * n + q // SLOTS + 1 + CREDIT)
                if c < 2:
                    act.wait_ge(rs_ready, n + CREDIT)
                else:
                    act.wait_ge(ring_free, ring_base(n) + order.index(("fold", c - 2)) + 1 + CREDIT)
                act.copy(ov[c % 2][:], psV[c % 2][:]).then_inc(ov_ready[c % 2], 1)
            heads(act, turn)

        @block.vector
        def _(dve):
            lc = Chain(dve, lam_step)
            dve.wait_ge(lam_load, 64 + CREDIT)
            lv = lam_in[:].rearrange("p (m w) d -> p m w d", w=2)
            lc.after(dve.tensor_tensor(lam_w[:], lv[:, :, 0], lv[:, :, 1], ALU.mult))
            lc.after(dve.tensor_reduce(lam_s[:], lam_w[:], AX.X, ALU.add))
            dve.wait_ge(lam_exp, 1 + CREDIT)
            lc.after(dve.tensor_tensor(lam[:, 0:1], lam_e[:, 0:1], lam_e[:, 1:2], ALU.subtract))
            dve.tensor_scalar(lam[:, 1:2], lam[:, 0:1], LAMBDA_INIT, None, ALU.add).then_inc(lam_ready, 1)
            for u in range(2):
                lc.mark(dve.memset(vaug[u][:, :, VD + 1:VW], 0.0))
                ins = dve.memset(vaug[u][:, :, VD:VD + 1], 1.0)
                if u == 0:
                    lc.mark(ins)
            ins.then_inc(setup, 1)
            lc.mark(dve.memset(kslabs[64:96].rearrange("p u a t -> p (u a t)").bitcast(F32), 0.0))
            dve.memset(qslabs[64:P].rearrange("p u a t -> p (u a t)").bitcast(F32), 0.0).then_inc(setup, 1)
            lc.after(dve.memset(pmax[:], NEG))
            dve.wait_ge(setup, 2 + CREDIT)
            dve.wait_ge(lam_ready, 1 + CREDIT)
            CH = 4

            class Ring:
                base, n, slot0 = 0, 0, 0

            def ring_bank():
                dve.wait_ge(ring_full, Ring.base + Ring.n + 1 + CREDIT)
                Ring.n += 1
                return psR[(Ring.slot0 + Ring.n - 1) % 2]

            def take_max(unit):
                a, i, ch, w = unit
                dve.tensor_reduce(pmax[:, a * ST_T + i, ch:ch + 1], ring_bank()[:, 0:w], AX.X, ALU.max)\
                   .then_inc(ring_free, 1)

            def whole_max():
                dve.wait_ge(ring_free, Ring.base + Ring.n + CREDIT)
                dve.tensor_reduce(nmax[:], pmax[:], AX.X, ALU.max, negate=True).then_inc(nmax_ready, 1)

            def cut_max(n, c):
                src = ring_bank()[0:2 * ST_T, 0:P]
                dve.wait_ge(mrow_in, 96 * n + CREDIT)
                c.after(dve.tensor_copy(mpart[:, 0], src))
                dve.tensor_tensor(mrest[:, 0], src, mpart[:, 0], ALU.subtract).then_inc(ring_free, 1)
                dve.wait_ge(ring_free, Ring.base + Ring.n + CREDIT)
                c.after(dve.tensor_copy(mpart[:, 1], mrest[:, 0]))
                c.after(dve.tensor_tensor(mrest[:, 1], mrest[:, 0], mpart[:, 1], ALU.subtract))
                dve.tensor_copy(mpart[:, 2], mrest[:, 1]).then_inc(mpart_ready, 1)

            c = Chain(dve, dchain)
            for unit in UNITS:
                take_max(unit)
            whole_max()
            cut_max(0, c)

            def turn(n, u, more):
                c = Chain(dve, dchain)
                c.turn(3 + CH * n)
                Ring.base, Ring.n, Ring.slot0 = ring_base(n), 0, (NUNIT + 1 + RING_HEAD * u) % 2
                for k in range(NSTEP + 1):
                    if k == FIRST_U and more:
                        dve.wait_ge(nmax_ready, n + 1 + CREDIT)
                    for kind, what in ring_at(k, more):
                        if kind == "max":
                            take_max(what)
                        elif kind == "fold":
                            dve.wait_ge(post_done, n + CREDIT)
                            dve.tensor_copy(o[:, TPB * what:TPB * what + TPB].rearrange("p i a d -> p (i a d)"),
                                            ring_bank()[:, 0:TPB * 2 * OC]).then_inc(ring_free, 1)
                        else:
                            cut_max(n + 1, c)
                    if k == LAST_U and more:
                        whole_max()
                dve.wait_ge(ring_free, Ring.base + Ring.n + CREDIT)
                c.after(dve.reciprocal(rs[:], o[:, :, :, VD]))
                dve.tensor_scalar(rl[:], rs[:, :, 1], lam[:, 1:2], None, ALU.mult).then_inc(rs_ready, 1)
            heads(dve, turn)

        @block.tensor
        def _(pe):
            pe.wait_ge(masks, 11 + CREDIT)
            pe.wait_ge(v_ready, 1 + CREDIT)

            class Ring:
                base, n, slot0 = 0, 0, 0

            def take_slot():
                ring = Ring.base + Ring.n
                if not isinstance(ring, int) or ring >= 2:
                    pe.wait_ge(ring_free, ring - 1 + CREDIT)
                s = (Ring.slot0 + Ring.n) % 2
                Ring.n += 1
                return psR[s]

            def max_unit(u, unit):
                a, i, ch, w = unit
                dst = take_slot()
                diag = ch == i // TPB
                ins = pe.matmul(dst[:, 0:w], qslab[u][a][0:K_MAX, i * P:(i + 1) * P],
                                kslab[u][a][0:K_MAX, ch * BLK:ch * BLK + w], start=True, stop=True)
                if diag:
                    ins = pe.matmul(dst[:, w - P:w], ident_b[:], mask_q[:], start=False, stop=True,
                                    skip_group_check=True)
                ins.then_inc(ring_full, 1)

            def turn_max(n):
                pe.wait_ge(nmax_ready, n + 1 + CREDIT)
                dst = take_slot()
                pe.transpose(dst[0:2 * ST_T, 0:P], nmax[:], keep["ident"][:]).then_inc(ring_full, 1)

            for n, unit in enumerate(UNITS):
                if n % (NUNIT // 2) == 0:
                    pe.wait_ge(slab_in[0][unit[0]], 32 + CREDIT)
                max_unit(0, unit)
            turn_max(0)

            def scores(n, u, k):
                c, st, off, first = STEPS[k]
                q = (k - 2) % SLOTS
                pe.wait_ge(prob_ready[q], (NSTEP // SLOTS) * n + ((k - 2) // SLOTS + 1 if k >= 2 else 0) + CREDIT)
                diag = st >= TPB * c
                for a in range(2):
                    ins = pe.matmul(psS[k % 2][:, a, off:BLK], kslab[u][a][:, st * P:(st + 1) * P],
                                    qslab[u][a][:, c * BLK + off:(c + 1) * BLK], start=True, stop=True)
                    if diag:
                        lo = 0 if first else P
                        ins = pe.matmul(psS[k % 2][:, a, off:off + 2 * P - lo], ident_b[:], mask_k[:, lo:2 * P],
                                        start=False, stop=True, skip_group_check=True)
                ins.then_inc(scores_done, 1)

            def value_product(n, u, k):
                c, st, off, _w = STEPS[k]
                pe.wait_ge(prob_ready[k % SLOTS], (NSTEP // SLOTS) * n + k // SLOTS + 1 + CREDIT)
                if st == 0:
                    pe.wait_ge(ov_ready[c % 2], 2 * n + c // 2 + CREDIT)
                for a in range(2):
                    g = 2 * a + st % 2
                    ins = pe.matmul(psV[c % 2][g * VW:(g + 1) * VW, off:BLK], vaug[u][:, st, :],
                                    prob[k % BUFS][:, a, off:BLK], start=(st < 2), stop=(st >= TPB * c + TPB - 2),
                                    skip_group_check=True)
                ins.then_inc(pv_done[k % SLOTS], 1)

            def fold_sum(n, c):
                pe.wait_ge(ov_ready[c % 2], 2 * n + c // 2 + 1 + CREDIT)
                dst = take_slot()
                for i in range(TPB):
                    ins = pe.matmul(dst[:, i * 2 * OC:(i + 1) * 2 * OC], ov[c % 2][:, i * P:(i + 1) * P],
                                    fold[:].rearrange("p a d -> p (a d)"), start=True, stop=True)
                ins.then_inc(ring_full, 1)

            def ring_work(n, u, ring):
                for kind, what in ring:
                    if kind == "max":
                        if UNITS.index(what) % (NUNIT // 2) == 0:
                            pe.wait_ge(slab_in[1 - u][what[0]], loaded(n, u) + CREDIT)
                        max_unit(1 - u, what)
                    elif kind == "fold":
                        fold_sum(n, what)
                    else:
                        turn_max(n + 1)

            def turn(n, u, more):
                Ring.base, Ring.n, Ring.slot0 = ring_base(n), 0, (NUNIT + 1 + RING_HEAD * u) % 2
                pe.wait_ge(mrow_in, 96 * (n + 1) + CREDIT)
                pe.wait_ge(v_ready, n + 1 + CREDIT)
                for k in range(NSTEP):
                    ring = ring_at(k, more)
                    cuts = RING_CUTS[k % 2]
                    ring_work(n, u, ring[:cuts[0]])
                    scores(n, u, k)
                    ring_work(n, u, ring[cuts[0]:cuts[1]])
                    if k % 2 and k > LAG:
                        value_product(n, u, k - LAG - 1)
                        value_product(n, u, k - LAG)
                    ring_work(n, u, ring[cuts[1]:])
                for k in range(NSTEP - LAG, NSTEP):
                    value_product(n, u, k)
                for kind, what in ring_at(NSTEP, more):
                    fold_sum(n, what)

            def loaded(n, u):
                return (n + 1 - (1 - u)) * 16 + 32

            heads(pe, turn)


def phase_project(nc, io, keep, dram):
    with ExitStack() as ctx:
        sb = lambda name, shape, dt=F32: ctx.enter_context(nc.sbuf_tensor(name, shape, dt))
        ps = lambda name, shape, dt=F32: ctx.enter_context(nc.psum_tensor(name, shape, dt))
        sems = []
        sem = lambda name: credited(ctx, nc, sems, name)

        wp = sb("wp", [P, KD, D])
        gamma = sb("gamma", [P, 1])
        wps = sb("wps", [P, KD, D])
        sq = sb("sq", [P, HEADS, TPB, VD])
        ss = sb("ss", [P, HEADS, TPB])
        var = sb("var", [P, HEADS, TPB])
        root = sb("root", [P, HEADS, TPB])
        inv = sb("inv", [P, HEADS, TPB])
        y = sb("y_c", [P, TPB, D])
        yT = sb("yT", [P, KD, BLK])
        x = sb("x_c", [P, TPB, D])
        f = sb("f_c", [P, TPB, D])
        routed = sb("routed", [P, 2, TPB, D])
        index = sb("index", [P, 2, TPB], I32)
        weight = sb("weight", [P, 2, TPB])
        xf = sb("xf", [P, TPB, D])
        x1 = sb("x1", [P, TPB, D])
        stats = sb("stats_c", [P, TPB, 6])
        mv = sb("mv_c", [P, TPB, 2])
        vare = sb("vare", [P, TPB])
        std = sb("std_c", [P, TPB])
        rstd = sb("rstd_c", [P, TPB])
        xn = sb("xn_c", [P, TPB, D])
        xnT = sb("xnT_c", [P, KD, BLK])
        carrier = sb("carrier_c", [P, 1])
        pcarry = sb("pcarry_c", [P, 2])

        psT = ps("psT_c", [P, KD, BLK])
        psO = ps("psO", [P, TPB, D])
        psN = ps("psN", [P, KD, BLK])

        w_in = sem("c_w_in")
        w_ready = sem("c_w_ready")
        in_x = sem("c_in_x")
        xf_ready = sem("c_xf_ready")
        gathered = ctx.enter_context(nc.semaphore("c_gathered"))
        gather_in = sem("c_gather_in")
        index_ready = sem("c_index_ready")
        summed = sem("c_summed")
        pool_set = sem("c_pool_set")
        var_ready = sem("c_var_ready")
        root_ready = sem("c_root_ready")
        y_ready = sem("c_y_ready")
        yT_done = sem("c_yT_done")
        yT_ready = sem("c_yT_ready")
        o_done = sem("c_o_done")
        x1_ready = sem("c_x1_ready")
        x1_out = sem("c_x1_out")
        vare_ready = sem("c_vare_ready")
        std_ready = sem("c_std_ready")
        xn_ready = sem("c_xn_ready")
        xT_done = sem("c_xT_done")
        xnT_ready = sem("c_xnT_ready")
        xnT_out = sem("c_xnT_out")
        hchain = sem("c_hchain")
        rchain = sem("c_rchain")
        block = ctx.enter_context(nc.Block())

        @block.sync
        def _(sp):
            for s in sems:
                sp.sem_inc(s, CREDIT)
            sp.dma_start(wp[:], io["w_proj"].rearrange("(k p) n -> p k n", p=P)).then_inc(w_in, 16)
            for g in range(P // VD):
                sp.dma_start(gamma[g * VD:(g + 1) * VD, :], io["gamma"].unsqueeze(1)).then_inc(w_in, 16)
            with sp.Fori(0, NBLK) as blk:
                rows = lambda t: t[bass.ds(blk * BLK, BLK), :].rearrange("(j p) d -> p j d", p=P)
                sp.wait_ge(xf_ready, blk + CREDIT)
                sp.dma_start(x[:], rows(io["x"])).then_inc(in_x, 16)
                sp.dma_start(f[:], rows(dram["y"])).then_inc(in_x, 16)
                sp.wait_ge(x1_ready, blk + 1 + CREDIT)
                sp.dma_start(rows(dram["x1"]), x1[:]).then_inc(x1_out, 16)
            sp.wait_ge(x1_out, 16 * NBLK + CREDIT)
            sp.wait_ge(xnT_out, 16 * NBLK + CREDIT)

        @block.gpsimd
        def _(pool):
            pool.memset(pcarry[:], 0.0).then_inc(pool_set, 1)
            pool.wait_ge(pool_set, 1 + CREDIT)
            with pool.Fori(0, NBLK) as blk:
                pool.wait_ge(index_ready, blk + 1 + CREDIT)
                pool.tensor_tensor(pcarry[:, 0:1], pcarry[:, 0:1], pcarry[:, 0:1], ALU.mult)
                for k in range(2):
                    for j in range(TPB):
                        pool.indirect_dma_start(routed[:, k, j, :], None, dram["y"],
                                                bass.IndirectOffsetOnAxis(index[:, k, j:j + 1], 0)).then_inc(gathered, 16)
                pool.wait_ge(gathered, 16 * 2 * TPB * (blk + 1))
                pool.tensor_tensor(pcarry[:, 1:2], pcarry[:, 1:2], pcarry[:, 1:2], ALU.mult).then_inc(gather_in, 1)
                pool.wait_ge(in_x, 32 * blk + 32 + CREDIT)
                pool.wait_ge(x1_ready, blk + CREDIT)
                pool.tensor_tensor(xf[:], x[:], f[:], ALU.add).then_inc(xf_ready, 1)

        @block.scalar
        def _(act):
            def head_root(n):
                act.wait_ge(var_ready, n + 1 + CREDIT)
                act.activation(root[:], var[:], ACT.Sqrt).then_inc(root_ready, 1)

            def copy_heads(n):
                act.wait_ge(yT_done, n + 1 + CREDIT)
                act.wait_ge(o_done, n + CREDIT)
                for k in range(KD):
                    ins = act.copy(yT[:, k], psT[:, k])
                ins.then_inc(yT_ready, 1)

            head_root(0)
            copy_heads(0)
            with act.Fori(0, NBLK) as blk:
                head_root(blk + 1)
                act.wait_ge(vare_ready, blk + 1 + CREDIT)
                act.activation(std[:], vare[:], ACT.Sqrt).then_inc(std_ready, 1)
                copy_heads(blk + 1)
                act.wait_ge(xT_done, blk + 1 + CREDIT)
                act.wait_ge(xnT_out, 16 * blk + CREDIT)
                for k in range(KD):
                    ins = act.copy(xnT[:, k], psN[:, k])
                ins.then_inc(xnT_ready, 1)
                act.wait_ge(xnT_ready, blk + 1 + CREDIT)
                act.dma_start(dram["xn2T"][:, :, bass.ds(blk * BLK, BLK)].rearrange("k p t -> p k t"), xnT[:])\
                   .then_inc(xnT_out, 16)

        @block.vector
        def _(dve):
            CH = 22
            dve.wait_ge(w_in, 16 * (1 + P // VD) + CREDIT)

            def indices(blk):
                row = slice(0, 1) if isinstance(blk, int) else bass.ds(blk, 1)
                dve.tensor_copy(index[:].rearrange("p k j -> p (k j)"), keep["yslot"][:, row].rearrange("p o k -> p (o k)"))\
                   .then_inc(index_ready, 1)

            indices(0)
            dve.tensor_scalar(wps[:], wp[:], gamma[:, 0:1], 1.0 - LAMBDA_INIT, ALU.mult, ALU.mult).then_inc(w_ready, 1)
            SQ, CH = 3, 19

            def heads_of(n):
                m = n % NBLK
                b, q = m // BPB, m % BPB
                if isinstance(m, int):
                    return keep["o"][:, b * HEADS:(b + 1) * HEADS, q * TPB:(q + 1) * TPB, :]
                return keep["o"][:, bass.ds(b * HEADS, HEADS), bass.ds(q * TPB, TPB), :]

            def head_squares(n):
                c = Chain(dve, hchain)
                c.turn(SQ * n)
                ob = heads_of(n)
                c.after(dve.tensor_tensor(sq[:], ob, ob, ALU.mult))
                c.after(dve.tensor_reduce(ss[:], sq[:], AX.X, ALU.add))
                dve.tensor_scalar(var[:], ss[:], 1.0 / VD, EPS, ALU.mult, ALU.add).then_inc(var_ready, 1)

            def head_norm(n):
                c = Chain(dve, hchain)
                c.turn(SQ * n + 2)
                dve.wait_ge(root_ready, n + 1 + CREDIT)
                c.after(dve.reciprocal(inv[:], root[:]))
                dve.wait_ge(yT_done, n + CREDIT)
                ob = heads_of(n)
                for j in range(TPB):
                    ins = dve.tensor_tensor(y[:, j].rearrange("p (h d) -> p h d", h=HEADS), ob[:, :, j],
                                            inv[:, :, j:j + 1].to_broadcast([P, HEADS, VD]), ALU.mult)
                ins.then_inc(y_ready, 1)

            head_squares(0)
            head_norm(0)
            with dve.Fori(0, NBLK) as blk:
                c = Chain(dve, rchain)
                c.turn(CH * blk)
                head_squares(blk + 1)
                c.after(dve.tensor_copy(weight[:].rearrange("p k j -> p (k j)"), keep["c"][:, bass.ds(blk, 1)]
                                        .rearrange("p o k -> p (o k)")))
                dve.wait_ge(gather_in, blk + 1 + CREDIT)
                dve.wait_ge(xf_ready, blk + 1 + CREDIT)
                for k in range(2):
                    for j in range(TPB):
                        c.mark(dve.scalar_tensor_tensor(out=xf[:, j], in0=routed[:, k, j],
                                                        scalar=weight[:, k, j:j + 1], in1=xf[:, j],
                                                        op0=ALU.mult, op1=ALU.add))
                    c.wait()
                indices((blk + 1) % NBLK)
                dve.wait_ge(o_done, blk + 1 + CREDIT)
                dve.wait_ge(x1_out, 16 * blk + CREDIT)
                dve.tensor_tensor(x1[:], psO[:], xf[:], ALU.add).then_inc(x1_ready, 1)
                dve.wait_ge(x1_ready, blk + 1 + CREDIT)
                for j in range(TPB):
                    c.mark(dve.bn_stats(stats[:, j, :], x1[:, j, :]))
                c.wait()
                c.mark(dve.memset(carrier[:], 0.0))
                for j in range(TPB):
                    c.mark(dve.bn_aggr(mv[:, j, :], stats[:, j, :]))
                c.wait()
                dve.tensor_scalar(vare[:], mv[:, :, 1], EPS, None, ALU.add).then_inc(vare_ready, 1)
                head_norm(blk + 1)
                dve.wait_ge(std_ready, blk + 1 + CREDIT)
                c.after(dve.reciprocal(rstd[:], std[:]))
                dve.wait_ge(xT_done, blk + CREDIT)
                for j in range(TPB):
                    ins = dve.tensor_scalar(xn[:, j, :], x1[:, j, :], mv[:, j, 0:1], rstd[:, j:j + 1],
                                            ALU.subtract, ALU.mult)
                ins.then_inc(xn_ready, 1)
                assert c.n == CH

        @block.tensor
        def _(pe):
            pe.wait_ge(w_ready, 1 + CREDIT)
            def turn_heads(n):
                pe.wait_ge(y_ready, n + 1 + CREDIT)
                pe.wait_ge(yT_ready, n + CREDIT)
                for j in range(TPB):
                    for k in range(KD):
                        ins = pe.transpose(psT[:, k, j * P:(j + 1) * P], y[:, j, k * P:(k + 1) * P], keep["ident"][:])
                ins.then_inc(yT_done, 1)

            turn_heads(0)
            with pe.Fori(0, NBLK) as blk:
                pe.wait_ge(yT_ready, blk + 1 + CREDIT)
                pe.wait_ge(x1_ready, blk + CREDIT)
                for j in range(TPB):
                    for k in range(KD):
                        ins = pe.matmul(psO[:, j], yT[:, k, j * P:(j + 1) * P], wps[:, k], start=(k == 0),
                                        stop=(k == KD - 1))
                ins.then_inc(o_done, 1)
                turn_heads(blk + 1)
                pe.wait_ge(xn_ready, blk + 1 + CREDIT)
                pe.wait_ge(xnT_ready, blk + CREDIT)
                for j in range(TPB):
                    for k in range(KD):
                        ins = pe.transpose(psN[:, k, j * P:(j + 1) * P], xn[:, j, k * P:(k + 1) * P], keep["ident"][:])
                ins.then_inc(xT_done, 1)


def phase_state_space(nc, io, keep, dram, out):
    with ExitStack() as ctx:
        sb = lambda name, shape, dt=F32: ctx.enter_context(nc.sbuf_tensor(name, shape, dt))
        ps = lambda name, shape, dt=F32: ctx.enter_context(nc.psum_tensor(name, shape, dt))
        sems = []
        sem = lambda name: credited(ctx, nc, sems, name)
        ET = 2 * DI // P
        FT = F1 // P
        XD = RANK + 2 * NS
        UNITS = NS * CT
        LOADS = 25
        HALO = NTAP - 1

        winT = sb("winT", [P, KD, 2 * DI])
        woutT = sb("woutT", [P, CT, D])
        wxT = sb("wxT", [P, CT, XD])
        wdtT = sb("wdtT", [RANK, DI])
        conv_w = sb("conv_w", [P, CT, NTAP])
        vec = sb("vec", [P, 3, CT])
        a_log = sb("a_log", [P, CT, NS])
        a_exp = sb("a_exp", [P, CT, NS])
        a_neg = sb("a_neg", [P, CT, NS])
        scal = sb("scal", [P, 3])
        sgn = sb("sgn", [P, 3])
        mag = sb("mag", [P, 3])
        fac = sb("fac", [P, 4])
        w0 = sb("w0", [P, KD, F1], F16)
        w1 = sb("w1", [P, FT, F1], F16)
        w2 = sb("w2", [P, FT, D], F16)
        pick = sb("pick", [3 * 2 * NS, 2 * NS, P], BF16)

        xT = sb("xT_s", [P, KD, BLK])
        xh = sb("xh", [P, KD, BLK], F16)
        xl = sb("xl", [P, KD, BLK], F16)
        x1 = sb("x1_s", [P, TPB, D])
        xc = sb("xc", [P, CT, HALO + BLK])
        cv = sb("cv", [P, CT, BLK])
        sz = sb("sz", [P, 2, CT, BLK])
        xs = sb("xs", [P, 2, CT, BLK])
        xdt = sb("xdt", [RANK, BLK])
        bc = sb("bc", [3 * 2 * NS, 2, BLK], BF16)
        bc_rest = sb("bc_rest", [2 * NS, BLK])
        bc_mid = sb("bc_mid", [2 * NS, BLK], BF16)
        dt_ = sb("dt", [P, 2, CT, BLK])
        dtx = sb("dtx", [P, 2, CT, BLK])
        crep = sb("crep", [P, 2, BLK])
        a = sb("a", [P, 2, BLK])
        u = sb("u", [P, 2, BLK])
        h = sb("h_d", [P, 2, BLK])
        hc = sb("hc", [P, 4, BLK])
        state = sb("state", [P, CT, NS])
        carrier = sb("carrier_d", [P, 1])
        f1h = sb("f1h", [P, FT, BLK], F16)
        f1l = sb("f1l", [P, FT, BLK], F16)
        f2h = sb("f2h", [P, FT, BLK], F16)
        f2l = sb("f2l", [P, FT, BLK], F16)
        r = sb("r", [P, TPB, D])

        w_in = dtx[:, 0].rearrange("p c (h t) -> p (c h) t", h=2)
        w_out = dt_[:, 0, 0:KD]
        w_x = cv[0:XD, 0]
        w_dt = cv[:, 1, 0:CT * RANK].rearrange("p (c r) -> p c r", c=CT)
        k0 = f1l[:].rearrange("p k t -> p (k t)").bitcast(U8)[:, 0:2 * KD * F1].rearrange("p (k f) -> p k f", f=F1)
        k2 = f2l[:].rearrange("p k t -> p (k t)").bitcast(U8)[:, 0:FT * D].rearrange("p (k f) -> p k f", f=D)
        kd = f1h[:].rearrange("p (k f) t -> p k (f t)", k=4)[:, 0:KD]

        k1 = f2h[:].rearrange("p k t -> p (k t)").bitcast(U8).rearrange("p (k f) -> p k f", k=FT)

        psY = [ps(f"psYd{c}", [P, BLK]) for c in range(CT)]
        psB = ps("psB", [P, BLK])
        psC = ps("psC", [P, BLK])
        psW = [ps(f"psW{s}", [P, BLK]) for s in range(2)]

        weights = sem("d_weights")
        consts = sem("d_consts")
        wt_full = sem("d_wt_full")
        wt_free = sem("d_wt_free")
        a_ready0 = sem("d_a_exp")
        wchain = sem("d_wchain")
        w_ready = sem("d_w_ready")
        x_in = sem("d_x_in")
        x1_in = sem("d_x1_in")
        xh_ready = sem("d_xh_ready")
        xl_ready = sem("d_xl_ready")
        full = [sem(f"d_full{s}") for s in range(2)]
        free = [sem(f"d_free{s}") for s in range(2)]
        xc_ready = sem("d_xc_ready")
        cchain = sem("d_cchain")
        conv_done = sem("d_conv_done")
        halo_ready = sem("d_halo_ready")
        state_zero = sem("d_state_zero")
        sz_ready = sem("d_sz_ready")
        bc_cut = sem("d_bc_cut")
        bc_ready = sem("d_bc_ready")
        xchain = sem("d_xchain")
        xs_ready = sem("d_xs_ready")
        ex_ready = sem("d_ex_ready")
        ln_ready = sem("d_ln_ready")
        mx_ready = sem("d_mx_ready")
        dt_ready = sem("d_dt_ready")
        dtx_ready = sem("d_dtx_ready")
        b_full = sem("d_b_full")
        c_full = sem("d_c_full")
        crep_ready = sem("d_crep_ready")
        u_ready = sem("d_u_ready")
        a_ready = [sem(f"d_a_ready{s}") for s in range(2)]
        h_ready = [sem(f"d_h_ready{s}") for s in range(2)]
        hc_ready = [sem(f"d_hc_ready{s}") for s in range(2)]
        y_added = [sem(f"d_y_added{s}") for s in range(2)]
        high_ready = sem("d_high_ready")
        low_ready = sem("d_low_ready")
        yg_ready = sem("d_yg_ready")
        ys_ready = sem("d_ys_ready")
        out_ready = sem("d_out_ready")
        out_sent = sem("d_out_sent")
        block = ctx.enter_context(nc.Block())

        def sign_unit(sidx):
            if sidx < 4:
                return [("l1", 2 * sidx), ("l1", 2 * sidx + 1)]
            if sidx < 12:
                return [("l2", sidx - 4)]
            return [("l3", (sidx - 12) // 2)] if sidx % 2 == 0 else []

        def sign_unit_behind(sidx, c):
            return sign_unit(sidx) if c == CT - 1 else []

        def input_unit(sidx):
            if sidx < ET:
                return [("xz", sidx)]
            return {ET: [("xd", 0)], ET + 2: [("dt", 0), ("dt", 1)], ET + 4: [("dt", 2), ("dt", 3)]}.get(sidx, [])

        FIRST = [unit for sidx in range(NS) for unit in input_unit(sidx)]
        ORDER = [unit for sidx in range(NS) for unit in sign_unit(sidx) + input_unit(sidx)]
        ORDER += [("out", j) for j in range(2)]

        def full_at(turn, kind):
            if turn is None:
                n = FIRST.index(kind)
                return n % 2, n // 2 + 1
            b, q = turn
            n = len(FIRST) + len(ORDER) * q + ORDER.index(kind)
            return n % 2, len(ORDER) * BPB // 2 * b + n // 2 + 1

        def turns(eng, turn):
            with eng.Fori(0, BATCH) as b:
                for q in range(BPB):
                    turn(b, q)

        def weight_copies():
            got = []
            for k in range(KD):
                for half in range(2):
                    got.append((winT[:, k, half * BLK:(half + 1) * BLK], psW[len(got) % 2][:]))
            for c in range(CT):
                got.append((woutT[:, c, :], psW[len(got) % 2][:, 0:D]))
            for c in range(CT):
                got.append((wxT[:, c, :], psW[len(got) % 2][:, 0:XD]))
            got.append((wdtT[:], psW[len(got) % 2][0:RANK, :]))
            return got

        @block.sync
        def _(sp):
            for s in sems:
                sp.sem_inc(s, CREDIT)
            loads = [
                (w_in, io["in_proj"].rearrange("(e p) d -> p e d", p=P)),
                (w_out, io["out_proj"].rearrange("(k p) i -> p k i", p=P)),
                (w_x[0:2 * NS], io["x_proj"][RANK:XD]),
                (w_x[2 * NS:XD], io["x_proj"][0:RANK]),
                (w_dt, io["dt_proj"].rearrange("(c p) r -> p c r", p=P)),
                (conv_w[:], io["conv_w"].rearrange("(c p) o t -> p c (o t)", p=P)),
                (a_log[:], io["A_log"].rearrange("(c p) s -> p c s", p=P)),
                (k0, io["k0"].rearrange("(k p) f -> p k f", p=P)),
                (k1, io["k1"].rearrange("(k p) f -> p k f", p=P)),
                (k2, io["k2"].rearrange("(k p) f -> p k f", p=P)),
            ]
            for n, name in enumerate(("conv_b", "dt_b", "D_skip")):
                for c in range(CT):
                    loads.append((vec[:, n, c:c + 1], io[name][c * P:(c + 1) * P].unsqueeze(1)))
            for n, name in enumerate(("s0", "s1", "s2")):
                loads.append((scal[:, n:n + 1], io[name].partition_broadcast(P)))
            for dst, src in loads:
                sp.dma_start(dst, src).then_inc(weights, 16)
            assert len(loads) == LOADS
            out_blk = out.rearrange("(b q j p) d -> b q p j d", q=BPB, j=TPB, p=P)

            def turn(b, q):
                blk = b * BPB + q
                sp.wait_ge(out_ready, blk + 1 + CREDIT)
                sp.dma_start(out_blk[bass.ds(b, 1), q].rearrange("o p j d -> (o p) j d"), r[:]).then_inc(out_sent, 16)
            turns(sp, turn)
            sp.wait_ge(out_sent, 16 * NBLK + CREDIT)

        @block.gpsimd
        def _(pool):
            c = Chain(pool, consts)
            c.after(pool.memset(pick[:], 1.0))
            for part in range(3):
                rows = slice(part * 2 * NS, (part + 1) * 2 * NS)
                ins = pool.affine_select(out=pick[rows], in_=pick[rows], compare_op=ALU.is_equal, fill=0.0, base=0,
                                         pattern=[[-1, 2 * NS], [0, P]], channel_multiplier=1)
                c.after(ins) if part < 2 else c.mark(ins)
            with pool.Fori(0, NBLK) as blk:
                for t in range(UNITS):
                    s, i, sidx, c_ = t % 2, t // 2, t // CT, t % CT
                    n = UNITS // 2 * blk + i
                    pool.wait_ge(h_ready[s], n + 1 + CREDIT)
                    if c_ == 0:
                        pool.wait_ge(crep_ready, NS * blk + sidx + 1 + CREDIT)
                    pool.wait_ge(y_added[s], (n - 1 if i else n) + CREDIT)
                    pool.tensor_tensor(hc[:, t % 4], h[:, s], crep[:, sidx % 2], ALU.mult)
                    pool.tensor_copy(state[:, c_, sidx:sidx + 1], h[:, s, BLK - 1:BLK]).then_inc(hc_ready[s], 1)

        @block.scalar
        def _(act):
            act.wait_ge(weights, 16 * LOADS + CREDIT)
            act.activation(a_exp[:], a_log[:], ACT.Exp).then_inc(a_ready0, 1)
            def load_x(nb):
                act.dma_start(xT[:], dram["xn2T"][:, :, bass.ds(nb * BLK, BLK)].rearrange("k p t -> p k t"))\
                  .then_inc(x_in, 16)

            def load_x1(nb):
                act.dma_start(x1[:], dram["x1"][bass.ds(nb * BLK, BLK), :].rearrange("(j p) d -> p j d", p=P))\
                  .then_inc(x1_in, 16)

            def load_next_x(nb, at):
                s, n = full_at(at, ("xz", ET - 1))
                act.wait_ge(xl_ready, nb + 1 + CREDIT)
                act.wait_ge(full[s], n + CREDIT)
                load_x((nb + 1) % NBLK)

            def copy_x(nb):
                act.wait_ge(x_in, 16 * nb + 16 + CREDIT)
                act.copy(xh[:], xT[:]).then_inc(xh_ready, 1)

            def copy_xz(nb, v, at, e):
                s, n = full_at(at, ("xz", e))
                act.wait_ge(full[s], n + CREDIT)
                if e < CT:
                    if e == 0:
                        act.wait_ge(halo_ready, nb + 1 + CREDIT)
                    act.copy(xc[:, e, HALO:], psW[s][:]).then_inc(free[s], 1)
                else:
                    act.copy(sz[:, v, e - CT], psW[s][:]).then_inc(free[s], 1)

            def silu_conv(nb, v):
                for c in range(CT):
                    act.wait_ge(conv_done, CT * nb + c + 1 + CREDIT)
                    act.activation(xs[:, v, c], cv[:, c], ACT.Silu, bias=vec[:, 0, c:c + 1]).then_inc(xs_ready, 1)

            def silu_gate(nb, v, at):
                for e in (ET - 2, ET - 1):
                    s, n = full_at(at, ("xz", e))
                    act.wait_ge(free[s], n + CREDIT)
                act.activation(sz[:, v], sz[:, v], ACT.Silu).then_inc(sz_ready, 1)

            def copy_step_rows(nb, at):
                s, n = full_at(at, ("xd", 0))
                act.wait_ge(bc_cut, nb + 1 + CREDIT)
                act.copy(xdt[:], psW[s][2 * NS:XD, :]).then_inc(free[s], 1)

            def absolute(nb, at, cs):
                act.wait_ge(xs_ready, CT * nb + CT + CREDIT)
                for c in cs:
                    s, n = full_at(at, ("dt", c))
                    act.wait_ge(mx_ready, CT * nb + c + 1 + CREDIT)
                    act.activation(cv[:, c], psW[s][:], ACT.Abs, bias=vec[:, 1, c:c + 1]).then_inc(free[s], 1)

            def log_term(nb, at):
                for c in (CT - 2, CT - 1):
                    s, n = full_at(at, ("dt", c))
                    act.wait_ge(free[s], n + CREDIT)
                act.activation(cv[:], cv[:], ACT.Exp, scale=-1.0).then_inc(ex_ready, 1)
                act.wait_ge(ex_ready, nb + 1 + CREDIT)
                act.activation(cv[:], cv[:], ACT.Ln, bias=1.0).then_inc(ln_ready, 1)

            def input_work(nb, v, at, sidx, late):
                if not late:
                    if 1 <= sidx <= ET:
                        copy_xz(nb, v, at, sidx - 1)
                    if sidx == ET + 2:
                        copy_step_rows(nb, at)
                    if sidx == ET + 3:
                        absolute(nb, at, (0, 1))
                    if sidx == ET + 5:
                        absolute(nb, at, (2, 3))
                else:
                    if sidx == 4:
                        copy_x(nb)
                    if sidx == 6:
                        silu_conv(nb, v)
                    if sidx == ET + 1:
                        silu_gate(nb, v, at)
                        load_next_x(nb, at)
                    if sidx == ET + 5:
                        log_term(nb, at)

            load_x(0)
            load_x1(0)
            for sidx in range(NS):
                input_work(0, 0, None, sidx, False)
                input_work(0, 0, None, sidx, True)

            def turn(b, q):
                blk, v, at = b * BPB + q, q % 2, (b, q)
                for sidx in range(NS):
                    act.wait_ge(c_full, NS * blk + sidx + 1 + CREDIT)
                    act.wait_ge(hc_ready[1], UNITS // 2 * blk + max(0, 2 * sidx - 2) + CREDIT)
                    act.copy(crep[:, sidx % 2], psC[:]).then_inc(crep_ready, 1)

                    def decay(c):
                        t = sidx * CT + c
                        s, i = t % 2, t // 2
                        if sidx == 0:
                            act.wait_ge(dt_ready, CT * blk + c + 1 + CREDIT)
                        act.wait_ge(h_ready[s], UNITS // 2 * blk + i + CREDIT)
                        act.activation(a[:, s], dt_[:, v, c], ACT.Exp, scale=a_neg[:, c, sidx:sidx + 1])\
                           .then_inc(a_ready[s], 1)

                    for c in range(CT):
                        decay(c)
                        for kind, f in sign_unit_behind(sidx, c):
                            if kind == "l3":
                                continue
                            s, n = full_at(at, (kind, f))
                            act.wait_ge(full[s], n + CREDIT)
                            dst = f1h if kind == "l1" else f2h
                            act.activation(dst[:, f], psW[s][:], ACT.Relu).then_inc(high_ready, 1)
                        if c == 1:
                            input_work(blk + 1, 1 - v, at, sidx, False)
                    input_work(blk + 1, 1 - v, at, sidx, True)
                for j in range(2):
                    s, n = full_at(at, ("l3", j))
                    act.wait_ge(free[s], n + CREDIT)
                load_x1((blk + 1) % NBLK)
            turns(act, turn)
            act.wait_ge(x_in, 16 * (NBLK + 2) + CREDIT)
            act.wait_ge(x1_in, 16 * (NBLK + 1) + CREDIT)

        @block.vector
        def _(dve):
            c = Chain(dve, wchain)
            dve.wait_ge(weights, 16 * LOADS + CREDIT)
            c.mark(dve.tensor_scalar(sgn[:], scal[:], 0.0, None, ALU.is_ge))
            dve.wait_ge(a_ready0, 1 + CREDIT)
            c.after(dve.tensor_scalar(a_neg[:], a_exp[:], -1.0, None, ALU.mult))
            c.after(dve.tensor_scalar(sgn[:], sgn[:], 2.0, -1.0, ALU.mult, ALU.add))
            c.after(dve.tensor_tensor(mag[:], sgn[:], scal[:], ALU.mult))
            c.mark(dve.tensor_scalar(fac[:, 0:1], mag[:, 0:1], mag[:, 1:2], 64.0, ALU.mult, ALU.mult))
            c.mark(dve.tensor_scalar(fac[:, 2:3], sgn[:, 1:2], 0.25, None, ALU.mult))
            c.after(dve.tensor_scalar(fac[:, 3:4], sgn[:, 1:2], -0.125, None, ALU.mult))
            c.mark(dve.tensor_tensor(fac[:, 1:2], fac[:, 0:1], scal[:, 2:3], ALU.mult))
            c.after(dve.tensor_tensor(kd, k0[:, 0:KD], k0[:, KD:2 * KD], ALU.subtract))
            c.mark(dve.tensor_scalar(w0[:], kd, sgn[:, 0:1], None, ALU.mult))
            c.mark(dve.tensor_scalar(w1[:], k1, fac[:, 2:3], fac[:, 3:4], ALU.mult, ALU.add))
            dve.tensor_scalar(w2[:], k2, 2.0, -1.0, ALU.mult, ALU.add).then_inc(w_ready, 1)

            for n, (dst, src) in enumerate(weight_copies()):
                dve.wait_ge(wt_full, n + 1 + CREDIT)
                dve.tensor_copy(dst, src).then_inc(wt_free, 1)

            def cut_x(nb):
                dve.wait_ge(xh_ready, nb + 1 + CREDIT)
                dve.tensor_tensor(xl[:], xT[:], xh[:], ALU.subtract).then_inc(xl_ready, 1)

            def convolve(nb, at, c):
                k = Chain(dve, cchain)
                k.turn((CT * nb + c) * (NTAP - 1))
                s, n = full_at(at, ("xz", c))
                dve.wait_ge(free[s], n + CREDIT)
                if c == 0:
                    dve.wait_ge(dt_ready, CT * nb + CREDIT)
                k.after(dve.tensor_scalar(cv[:, c], xc[:, c, 0:BLK], conv_w[:, c, 0:1], None, ALU.mult))
                for t in range(1, NTAP):
                    ins = dve.scalar_tensor_tensor(out=cv[:, c], in0=xc[:, c, t:t + BLK],
                                                   scalar=conv_w[:, c, t:t + 1], in1=cv[:, c],
                                                   op0=ALU.mult, op1=ALU.add)
                    if t < NTAP - 1:
                        k.after(ins)
                ins.then_inc(conv_done, 1)

            def carry_halo(nb, starts_batch):
                dve.wait_ge(conv_done, CT * nb + CT + CREDIT)
                if starts_batch:
                    dve.memset(xc[:, :, 0:HALO], 0.0).then_inc(halo_ready, 1)
                else:
                    dve.tensor_copy(xc[:, :, 0:HALO], xc[:, :, BLK:]).then_inc(halo_ready, 1)

            def cut_bc(nb, v, at):
                k = Chain(dve, xchain)
                k.turn(4 * nb)
                R = 2 * NS
                s, n = full_at(at, ("xd", 0))
                dve.wait_ge(full[s], n + CREDIT)
                dve.wait_ge(bc_ready, nb + CREDIT)
                k.after(dve.tensor_copy(bc[0:R, v], psW[s][0:R, :]))
                dve.tensor_tensor(bc_rest[:], psW[s][0:R, :], bc[0:R, v], ALU.subtract).then_inc(bc_cut, 1)
                dve.wait_ge(bc_cut, nb + 1 + CREDIT)
                k.mark(dve.tensor_copy(bc[R:2 * R, v], bc_rest[:]))
                k.after(dve.tensor_copy(bc_mid[:], bc_rest[:]))
                k.after(dve.tensor_tensor(bc_rest[:], bc_rest[:], bc_mid[:], ALU.subtract))
                dve.tensor_copy(bc[2 * R:3 * R, v], bc_rest[:]).then_inc(bc_ready, 1)

            def positive_part(v, at, c):
                s, n = full_at(at, ("dt", c))
                dve.wait_ge(full[s], n + CREDIT)
                dve.tensor_scalar(dt_[:, v, c], psW[s][:], vec[:, 1, c:c + 1], 0.0, ALU.add, ALU.max)\
                   .then_inc(mx_ready, 1)

            def positive_parts(v, at, sidx):
                if sidx in (ET + 3, ET + 5):
                    for c in range(2):
                        positive_part(v, at, sidx - ET - 3 + c)

            def step_sizes(nb, v):
                dve.wait_ge(ln_ready, nb + 1 + CREDIT)
                dve.wait_ge(mx_ready, CT * nb + CT + CREDIT)
                for c in range(CT):
                    dve.tensor_tensor(dt_[:, v, c], dt_[:, v, c], cv[:, c], ALU.add).then_inc(dt_ready, 1)

            def scaled_inputs(nb, v):
                for c in range(CT):
                    dve.wait_ge(dt_ready, CT * nb + c + 1 + CREDIT)
                    dve.wait_ge(xs_ready, CT * nb + c + 1 + CREDIT)
                    dve.tensor_tensor(dtx[:, v, c], dt_[:, v, c], xs[:, v, c], ALU.mult).then_inc(dtx_ready, 1)

            def input_work(nb, v, at, sidx, starts_batch):
                if 1 <= sidx < 1 + CT:
                    convolve(nb, at, sidx - 1)
                if sidx == 1 + CT:
                    carry_halo(nb, starts_batch)
                    cut_x(nb)
                if sidx == ET + 1:
                    cut_bc(nb, v, at)
                if sidx == NS - 1:
                    step_sizes(nb, v)
                    scaled_inputs(nb, v)

            dve.memset(xc[:, :, 0:HALO], 0.0).then_inc(halo_ready, 1)
            dve.wait_ge(wt_free, len(weight_copies()) + CREDIT)
            for sidx in range(NS):
                positive_parts(0, None, sidx)
                input_work(0, 0, None, sidx, False)

            def turn(b, q):
                blk, v, at = b * BPB + q, q % 2, (b, q)
                if q == 0:
                    for s in range(2):
                        dve.wait_ge(hc_ready[s], UNITS // 2 * blk + CREDIT)
                    dve.memset(state[:], 0.0).then_inc(state_zero, 1)
                    dve.wait_ge(state_zero, b + 1 + CREDIT)
                dve.wait_ge(dtx_ready, CT * blk + CT + CREDIT)

                def scan(sidx, c):
                    t = sidx * CT + c
                    s, i = t % 2, t // 2
                    n = UNITS // 2 * blk + i
                    if c == 0:
                        dve.wait_ge(b_full, NS * blk + sidx + 1 + CREDIT)
                    dve.wait_ge(h_ready[s], n + CREDIT)
                    dve.tensor_tensor(u[:, s], dtx[:, v, c], psB[:], ALU.mult).then_inc(u_ready, 1)
                    dve.wait_ge(a_ready[s], n + 1 + CREDIT)
                    dve.wait_ge(hc_ready[s], n + CREDIT)
                    dve.wait_ge(u_ready, UNITS * blk + t + 1 + CREDIT)
                    dve.tensor_tensor_scan(h[:, s], a[:, s], u[:, s], state[:, c, sidx:sidx + 1],
                                           ALU.mult, ALU.add).then_inc(h_ready[s], 1)

                def sign_work(kind, f):
                    s, n = full_at(at, (kind, f))
                    if kind == "l3":
                        if f == 0:
                            dve.wait_ge(x1_in, 16 * blk + 16 + CREDIT)
                            dve.wait_ge(out_sent, 16 * blk + CREDIT)
                        dve.wait_ge(full[s], n + CREDIT)
                        dve.scalar_tensor_tensor(out=r[:, 2 * f:2 * f + 2].rearrange("p j d -> p (j d)"),
                                                 in0=psW[s][:], scalar=fac[:, 1:2],
                                                 in1=x1[:, 2 * f:2 * f + 2].rearrange("p j d -> p (j d)"),
                                                 op0=ALU.mult, op1=ALU.add).then_inc(free[s], 1)
                        return
                    dve.wait_ge(high_ready, 2 * FT * blk + (f if kind == "l1" else FT + f) + 1 + CREDIT)
                    hi, lo = (f1h, f1l) if kind == "l1" else (f2h, f2l)
                    dve.scalar_tensor_tensor(out=lo[:, f], in0=psW[s][:], scalar=0.0, in1=hi[:, f],
                                             op0=ALU.max, op1=ALU.subtract).then_inc(free[s], 1)

                for sidx in range(NS):
                    for c in range(CT):
                        scan(sidx, c)
                        if c == 1:
                            positive_parts(1 - v, at, sidx)
                        for kind, f in sign_unit_behind(sidx, c):
                            sign_work(kind, f)
                    input_work(blk + 1, 1 - v, at, sidx, q + 2 == BPB)
                for s in range(2):
                    dve.wait_ge(y_added[s], UNITS // 2 * (blk + 1) + CREDIT)
                for c in range(CT):
                    dve.scalar_tensor_tensor(out=xs[:, v, c], in0=xs[:, v, c], scalar=vec[:, 2, c:c + 1], in1=psY[c][:],
                                             op0=ALU.mult, op1=ALU.add).then_inc(yg_ready, 1)
                dve.wait_ge(sz_ready, blk + 1 + CREDIT)
                for c in range(CT):
                    dve.wait_ge(yg_ready, CT * blk + c + 1 + CREDIT)
                    dve.tensor_tensor(sz[:, v, c], xs[:, v, c], sz[:, v, c], ALU.mult).then_inc(ys_ready, 1)
                for j in range(2):
                    s, n = full_at(at, ("l3", j))
                    dve.wait_ge(free[s], n + CREDIT)
                for j in range(2):
                    s, n = full_at(at, ("out", j))
                    dve.wait_ge(full[s], n + CREDIT)
                    dve.tensor_tensor(r[:, 2 * j:2 * j + 2].rearrange("p j d -> p (j d)"), psW[s][:],
                                      r[:, 2 * j:2 * j + 2].rearrange("p j d -> p (j d)"), ALU.add)\
                       .then_inc(free[s], 1)
                for j in range(2):
                    s, n = full_at(at, ("out", j))
                    dve.wait_ge(free[s], n + CREDIT)
                dve.memset(carrier[:], 0.0).then_inc(out_ready, 1)
            turns(dve, turn)

        @block.tensor
        def _(pe):
            pe.wait_ge(weights, 16 * LOADS + CREDIT)
            pe.wait_ge(consts, 4 + CREDIT)
            ident = keep["ident"]
            n = [0]

            def bank():
                if n[0] >= 2:
                    pe.wait_ge(wt_free, n[0] - 1 + CREDIT)
                n[0] += 1
                return psW[(n[0] - 1) % 2]

            for k in range(KD):
                for half in range(2):
                    dst = bank()
                    for e in range(4):
                        ins = pe.transpose(dst[:, e * P:(e + 1) * P], w_in[:, half * 4 + e, k * P:(k + 1) * P], ident[:])
                    ins.then_inc(wt_full, 1)
            for c in range(CT):
                dst = bank()
                for k in range(KD):
                    ins = pe.transpose(dst[:, k * P:(k + 1) * P], w_out[:, k, c * P:(c + 1) * P], ident[:])
                ins.then_inc(wt_full, 1)
            for c in range(CT):
                pe.transpose(bank()[:, 0:XD], w_x[:, c * P:(c + 1) * P], ident[0:XD, 0:XD]).then_inc(wt_full, 1)
            dst = bank()
            for c in range(CT):
                ins = pe.transpose(dst[0:RANK, c * P:(c + 1) * P], w_dt[:, c, :], ident[:])
            ins.then_inc(wt_full, 1)
            pe.wait_ge(wt_free, n[0] + CREDIT)
            pe.wait_ge(w_ready, 1 + CREDIT)

            def work(at, kind):
                s, n = full_at(at, kind)
                if not isinstance(n, int) or n > 1:
                    pe.wait_ge(free[s], n - 1 + CREDIT)
                return s, psW[s]

            def input_products(nb, v, at, kind, e, ks):
                s, dst = work(at, (kind, e)) if 0 in ks else (full_at(at, (kind, e))[0], psW[full_at(at, (kind, e))[0]])
                K = KD if kind == "xz" else CT if kind == "xd" else 1
                if kind == "xz":
                    if e == 0 and 0 in ks:
                        pe.wait_ge(x_in, 16 * nb + 16 + CREDIT)
                    for k in ks:
                        ins = pe.matmul(dst[:], winT[:, k, e * P:(e + 1) * P], xT[:, k], start=(k == 0), stop=(k == KD - 1))
                elif kind == "xd":
                    for c in ks:
                        pe.wait_ge(xs_ready, CT * nb + c + 1 + CREDIT)
                        ins = pe.matmul(dst[0:XD, :], wxT[:, c], xs[:, v, c], start=(c == 0), stop=(c == CT - 1))
                else:
                    if e == 0:
                        sx, nx = full_at(at, ("xd", 0))
                        pe.wait_ge(free[sx], nx + CREDIT)
                    ins = pe.matmul(dst[:], wdtT[:, e * P:(e + 1) * P], xdt[:], start=True, stop=True)
                if K - 1 in ks:
                    ins.then_inc(full[s], 1)

            def spread_b(blk, v, sidx):
                if sidx == 0:
                    pe.wait_ge(bc_ready, blk + 1 + CREDIT)
                if sidx or not isinstance(blk, int):
                    pe.wait_ge(u_ready, UNITS * blk + CT * sidx + CREDIT)
                pe.matmul(psB[:], pick[:, sidx], bc[:, v], start=True, stop=True).then_inc(b_full, 1)

            def spread_c(blk, v, sidx):
                if sidx == 0:
                    pe.wait_ge(bc_ready, blk + 1 + CREDIT)
                if sidx or not isinstance(blk, int):
                    pe.wait_ge(crep_ready, NS * blk + sidx + CREDIT)
                pe.matmul(psC[:], pick[:, NS + sidx], bc[:, v], start=True, stop=True).then_inc(c_full, 1)

            for kind, e in FIRST:
                input_products(0, 0, None, kind, e, range({"xz": KD, "xd": CT, "dt": 1}[kind]))
            spread_b(0, 0, 0)
            spread_c(0, 0, 0)

            def turn(b, q):
                blk, v, at = b * BPB + q, q % 2, (b, q)

                def sign_products(kind, f):
                    s, dst = work(at, (kind, f))
                    if kind == "l1":
                        if f == 0:
                            pe.wait_ge(xl_ready, blk + 1 + CREDIT)
                        ops = [(w0[:, k, f * P:(f + 1) * P], x[:, k]) for k in range(KD) for x in (xh, xl)]
                    elif kind == "l2":
                        if f == 0:
                            for g in (FT - 2, FT - 1):
                                sl, nl = full_at(at, ("l1", g))
                                pe.wait_ge(free[sl], nl + CREDIT)
                        ops = [(w1[:, k, f * P:(f + 1) * P], x[:, k]) for k in range(FT) for x in (f1h, f1l)]
                    else:
                        if f == 0:
                            for g in (FT - 2, FT - 1):
                                sl, nl = full_at(at, ("l2", g))
                                pe.wait_ge(free[sl], nl + CREDIT)
                        for j in range(2):
                            col = (2 * f + j) * P
                            ops = [(x[:, k, col:col + P], w2[:, k]) for k in range(FT) for x in (f2h, f2l)]
                            for n, (lhs, rhs) in enumerate(ops):
                                ins = pe.matmul(dst[:, j * D:(j + 1) * D], lhs, rhs, start=(n == 0),
                                                stop=(n == len(ops) - 1))
                        ins.then_inc(full[s], 1)
                        return
                    for n, (lhs, rhs) in enumerate(ops):
                        ins = pe.matmul(dst[:], lhs, rhs, start=(n == 0), stop=(n == len(ops) - 1))
                    ins.then_inc(full[s], 1)

                def add_state(sidx, c):
                    t = sidx * CT + c
                    s, i = t % 2, t // 2
                    if sidx == 0:
                        pe.wait_ge(yg_ready, CT * blk + CREDIT)
                    pe.wait_ge(hc_ready[s], UNITS // 2 * blk + i + 1 + CREDIT)
                    pe.matmul(psY[c][:], ident[:], hc[:, t % 4], start=(sidx == 0), stop=(sidx == NS - 1),
                              skip_group_check=True).then_inc(y_added[s], 1)

                for sidx in range(NS):
                    signs, inputs = sign_unit(sidx), input_unit(sidx)
                    for c in range(CT):
                        if c == 0:
                            for kind, f in signs:
                                sign_products(kind, f)
                        if c >= 2:
                            for kind, e in inputs:
                                if kind == "dt":
                                    if e % 2 == c - 2:
                                        input_products(blk + 1, 1 - v, at, kind, e, [0])
                                else:
                                    half = (KD if kind == "xz" else CT) // 2
                                    input_products(blk + 1, 1 - v, at, kind, e, range((c - 2) * half, (c - 1) * half))
                        nxt = (blk, v, sidx + 1) if sidx + 1 < NS else (blk + 1, 1 - v, 0)
                        if c == 2:
                            spread_c(*nxt)
                        if c == 3:
                            spread_b(*nxt)
                        add_state(sidx, c)
                banks = [work(at, ("out", j)) for j in range(2)]
                for j, (s, dst) in enumerate(banks):
                    for half in range(2):
                        col = (2 * j + half) * P
                        for c in range(CT):
                            if j == 0:
                                pe.wait_ge(ys_ready, CT * blk + c + 1 + CREDIT)
                            ins = pe.matmul(dst[:, half * D:(half + 1) * D], sz[:, v, c, col:col + P], woutT[:, c],
                                            start=(c == 0), stop=(c == CT - 1))
                    ins.then_inc(full[s], 1)
            turns(pe, turn)


def build(nc, io, out):
    with ExitStack() as ctx:
        scratch = lambda name, shape, dt=F32: nc.dram_tensor(name, shape, dt, kind="Internal").ap()
        dram = {
            "rows": scratch("rows_d", [E * REG + N, D]),
            "y": scratch("y_d", [TT * P, D]),
            "q": scratch("q_d", [BATCH, 2 * HEADS, 3, HD, T], BF16),
            "k": scratch("k_d", [BATCH, 2 * HEADS, HD, 3, T], BF16),
            "x1": scratch("x1_d", [N, D]),
            "xn2T": scratch("xn2T_d", [KD, P, N]),
        }
        sb = lambda c, name, shape, dt=F32: c.enter_context(nc.sbuf_tensor(name, shape, dt))
        keep = {
            "ident": sb(ctx, "ident", [P, P]),
            "moe_w": ctx.enter_context(nc.semaphore("moe_w")),
        }
        with ExitStack() as attn:
            keep["c"] = sb(attn, "c_all", [P, NBLK, 2 * TPB])
            keep["yslot"] = sb(attn, "yslot_all", [P, NBLK, 2 * TPB], I32)
            keep["v"] = sb(attn, "v_all", [P, BATCH, HEADS, ST_T, VD])
            with ExitStack() as moe:
                keep["hot"] = sb(moe, "hot_all", [P, NBLK, 2, TPB, E])
                keep["slot"] = sb(moe, "slot_all", [P, NBLK, 2 * TPB])
                keep["table"] = sb(moe, "table", [P, 2, TT], I32)
                keep["wg"] = sb(moe, "wg", [P, NE, KD, M])
                keep["wu"] = sb(moe, "wu", [P, NE, KD, M])
                keep["wd"] = sb(moe, "wd", [P, NE, M // P, D])
                phase_norm_qkv(nc, io, keep, dram)
                phase_experts(nc, io, keep, dram)
            keep["o"] = sb(attn, "o_all", [P, NH, ST_T, VD])
            phase_attention(nc, io, keep, dram)
            phase_project(nc, io, keep, dram)
        phase_state_space(nc, io, keep, dram, out)


_SHORT = {
    "L0_attn_x": "x", "L0_attn_w_attn": "w_attn", "L0_attn_w_proj": "w_proj", "L0_attn_lambda_q1": "lq1",
    "L0_attn_lambda_q2": "lq2", "L0_attn_lambda_k1": "lk1", "L0_attn_lambda_k2": "lk2", "L0_attn_gamma": "gamma",
    "L0_ffn_gate_w": "gate_w", "L0_ffn_beta": "beta", "L0_ffn_gate_proj_w": "gate_proj", "L0_ffn_up_proj_w": "up_proj",
    "L0_ffn_down_proj_w": "down_proj", "L0_ffn_shared_gate_w": "shared_gate", "L0_ffn_shared_up_w": "shared_up",
    "L0_ffn_shared_down_w": "shared_down", "L1_attn_in_proj_w": "in_proj", "L1_attn_conv_w": "conv_w",
    "L1_attn_conv_b": "conv_b", "L1_attn_x_proj_w": "x_proj", "L1_attn_dt_proj_w": "dt_proj",
    "L1_attn_dt_proj_b": "dt_b", "L1_attn_A_log": "A_log", "L1_attn_D_skip": "D_skip", "L1_attn_out_proj_w": "out_proj",
    "L1_ffn_k0": "k0", "L1_ffn_k1": "k1", "L1_ffn_k2": "k2", "L1_ffn_s0": "s0", "L1_ffn_s1": "s1", "L1_ffn_s2": "s2",
}


def kernel(**inputs):
    import numpy as _np
    import concourse.bacc as _bacc
    from concourse import mybir as _mybir
    from concourse.bass_utils import run_bass_kernel_spmd as _run

    nc = _bacc.Bacc("TRN2", target_bir_lowering=False, num_devices=1)
    arrays, io = {}, {}
    for name, short in _SHORT.items():
        a = _np.ascontiguousarray(inputs[name])
        if a.ndim == 0:
            a = a.reshape(1)
        arrays[f"in_{name}_dram"] = a
        io[short] = nc.dram_tensor(f"in_{name}_dram", a.shape, _mybir.dt.from_np(a.dtype), kind="ExternalInput").ap()
    io["x"] = io["x"].rearrange("b t d -> (b t) d")
    out = nc.dram_tensor("out_0_dram", (BATCH, T, D), _mybir.dt.float32, kind="ExternalOutput").ap()
    build(nc, io, out.rearrange("b t d -> (b t) d"))
    r = _run(nc, [arrays], core_ids=[0])
    return r.results[0]["out_0_dram"]
```
